# Optimizing a Trainium2 kernel written in Bass

```python
import numpy as np
import jax
import jax.numpy as jnp

def _softmax(x, axis=-1):
    return jax.nn.softmax(x, axis=axis)

def _gelu(x):
    return jax.nn.gelu(x, approximate=True)

def _silu(x):
    return jax.nn.silu(x)

def _sigmoid(x):
    return jax.nn.sigmoid(x)

def _layernorm(x, axis=-1, eps=1e-05):
    m = jnp.mean(x, axis=axis, keepdims=True)
    v = jnp.var(x, axis=axis, keepdims=True)
    return (x - m) / jnp.sqrt(v + eps)

def _scatter_add(tgt, idx, src, axis=0):
    return tgt.at[idx].add(src)

def _segment_sum(src, seg, n):
    return jax.ops.segment_sum(src, seg, n)
kernel_name = 'mk_xattn_ffn_d4_seqx_r8_8e9f14'

def setup_inputs(seed: int=0):
    np.random.seed(seed)
    _w = jnp.asarray

    def _rec_inputs():
        import jax
        import jax.numpy as jnp
        _rk = jax.random.key(seed)
        x = -0.000125 + 0.9999 * jax.random.normal(jax.random.fold_in(_rk, 1), (4, 256, 256), jnp.float32)
        _lenS = 256 - jax.random.randint(jax.random.fold_in(_rk, 7), (4,), 0, max(1, 256 // 4) + 1, jnp.int32)
        _lenS2 = 1601 - jax.random.randint(jax.random.fold_in(_rk, 8), (4,), 0, max(1, 1601 // 4) + 1, jnp.int32)
        _ctx_2048P = jax.random.normal(jax.random.fold_in(_rk, 11), (4, 16, 256), jnp.float32)
        _ctx_2048c = jax.random.dirichlet(jax.random.fold_in(_rk, 511), 0.3 * jnp.ones((16,), jnp.float32), (4, 1601))
        _ctx_2048t = jnp.einsum('bsk,bkd->bsd', _ctx_2048c, _ctx_2048P)
        _ctx_2048t = _ctx_2048t * jax.lax.rsqrt(jnp.mean(jnp.square(_ctx_2048t)) + 1e-12) * 0.953939
        ctx_2048 = -0.000540021 + 0.99982 * (_ctx_2048t + 0.3 * jax.random.normal(jax.random.fold_in(_rk, 611), (4, 1601, 256), jnp.float32))
        _validS = jnp.arange(256)[None, :] < _lenS[:, None]
        _validS2 = jnp.arange(1601)[None, :] < _lenS2[:, None]
        _causal = jnp.tril(jnp.ones((256, 256), dtype=bool))
        mask_Bx1xSxS_fk0 = jnp.where(jnp.broadcast_to(_validS[:, None, None, :], (4, 1, 256, 256)), -1000000000.0, 0.0).astype(jnp.float32)
        return (x, ctx_2048, mask_Bx1xSxS_fk0)
    x, ctx_2048, mask_Bx1xSxS_fk0 = _rec_inputs()

    def _L0_xattn_setup():
        import jax, jax.numpy as jnp
        import numpy as np
        DIM = 256
        N_HEADS = 16
        HEAD_DIM = DIM // N_HEADS
        EPS = 1e-06
        IMG_LEN = 257

        def rms_norm(x, g, eps=EPS):
            var = jnp.mean(x * x, axis=-1, keepdims=True)
            return x * jax.lax.rsqrt(var + eps) * g

        def _attend(q, k, v, k_mask=None):
            scale = 1.0 / jnp.sqrt(jnp.asarray(HEAD_DIM, q.dtype))
            scores = jnp.einsum('bqnd,bknd->bnqk', q, k) * scale
            if k_mask is not None:
                neg = jnp.asarray(jnp.finfo(scores.dtype).min, scores.dtype)
                scores = jnp.where(k_mask[:, None, None, :], scores, neg)
            probs = jax.nn.softmax(scores, axis=-1)
            return jnp.einsum('bnqk,bknd->bqnd', probs, v)
        key = jax.random.key(seed)
        ks = jax.random.split(key, 16)
        B, L1, L2 = (1, 2048, 769)
        std = 0.02
        inp = {'x': jax.random.normal(ks[0], (B, L1, DIM), jnp.float32), 'context': jax.random.normal(ks[1], (B, L2, DIM), jnp.float32), 'context_lens': jax.random.randint(ks[2], (B,), 32, 513, jnp.int32), 'Wq': jax.random.normal(ks[3], (DIM, DIM), jnp.float32) * std, 'bq': jnp.zeros((DIM,), jnp.float32), 'gq': jnp.ones((DIM,), jnp.float32), 'Wk': jax.random.normal(ks[4], (DIM, DIM), jnp.float32) * std, 'bk': jnp.zeros((DIM,), jnp.float32), 'gk': jnp.ones((DIM,), jnp.float32), 'Wv': jax.random.normal(ks[5], (DIM, DIM), jnp.float32) * std, 'bv': jnp.zeros((DIM,), jnp.float32), 'Wk_img': jax.random.normal(ks[6], (DIM, DIM), jnp.float32) * std, 'bk_img': jnp.zeros((DIM,), jnp.float32), 'gk_img': jnp.ones((DIM,), jnp.float32), 'Wv_img': jax.random.normal(ks[7], (DIM, DIM), jnp.float32) * std, 'bv_img': jnp.zeros((DIM,), jnp.float32), 'Wo': jax.random.normal(ks[8], (DIM, DIM), jnp.float32) * std, 'bo': jnp.zeros((DIM,), jnp.float32)}
        return inp
    _L0_xattn_all = _L0_xattn_setup()
    _L0_xattn_in = {k: v for k, v in _L0_xattn_all.items() if k in ('context_lens', 'Wq', 'bq', 'gq', 'Wk', 'bk', 'gk', 'Wv', 'bv', 'Wk_img', 'bk_img', 'gk_img', 'Wv_img', 'bv_img', 'Wo', 'bo')}
    del _L0_xattn_all

    def _L0_ffn_setup():
        import jax, jax.numpy as jnp
        import numpy as np
        B_, S, D = (2, 256, 256)
        F_ = 1024
        R = 16
        H = 16
        HD = D // H
        MOD_SCALE = 0.1
        EPS = 1e-06

        def _rmsnorm(x, w):
            v = jnp.mean(x * x, axis=-1, keepdims=True)
            return x * jax.lax.rsqrt(v + EPS) * w

        def _attention(x, Wq, Wk, Wv, Wo):
            b, s, d = x.shape
            q = (x @ Wq.T).reshape(b, s, H, HD)
            k = (x @ Wk.T).reshape(b, s, H, HD)
            v = (x @ Wv.T).reshape(b, s, H, HD)
            scores = jnp.einsum('bqhd,bkhd->bhqk', q, k) / np.sqrt(HD).astype(np.float32)
            causal = jnp.tril(jnp.ones((s, s), bool))
            scores = jnp.where(causal, scores, jnp.finfo(scores.dtype).min)
            probs = jax.nn.softmax(scores, axis=-1)
            out = jnp.einsum('bhqk,bkhd->bqhd', probs, v).reshape(b, s, d)
            return out @ Wo.T
        key = jax.random.key(seed)
        ks = jax.random.split(key, 12)
        sd = 0.02
        return {'hidden_states': jax.random.normal(ks[0], (B_, S, D), jnp.float32), 'ln1_w': jnp.ones((D,), jnp.float32), 'ln2_w': jnp.ones((D,), jnp.float32), 'Wq': jax.random.normal(ks[1], (D, D), jnp.float32) * sd, 'Wk': jax.random.normal(ks[2], (D, D), jnp.float32) * sd, 'Wv': jax.random.normal(ks[3], (D, D), jnp.float32) * sd, 'Wo': jax.random.normal(ks[4], (D, D), jnp.float32) * sd, 'A': jax.random.normal(ks[5], (D, R), jnp.float32) * (0.01 / np.sqrt(D)), 'B': jax.random.normal(ks[6], (R, F_), jnp.float32) * (0.01 / np.sqrt(R)), 'W_in_base': jax.random.normal(ks[7], (F_, D), jnp.float32) * sd, 'W_up_base': jax.random.normal(ks[8], (F_, D), jnp.float32) * sd, 'W_down': jax.random.normal(ks[9], (D, F_), jnp.float32) * sd}
    _L0_ffn_all = _L0_ffn_setup()
    _L0_ffn_in = {k: v for k, v in _L0_ffn_all.items() if k in ('ln1_w', 'ln2_w', 'Wq', 'Wk', 'Wv', 'Wo', 'A', 'B', 'W_in_base', 'W_up_base', 'W_down')}
    del _L0_ffn_all

    def _L1_xattn_setup():
        import jax, jax.numpy as jnp
        import numpy as np
        from jax import lax
        LN_EPS = 1e-05
        key = jax.random.key(seed)
        ks = jax.random.split(key, 8)
        B, S, T, D = (4, 128, 256, 256)
        scale = 0.02
        return {'Z': jax.random.normal(ks[0], (B, S, D), dtype=jnp.float32), 'kv': jax.random.normal(ks[1], (B, T, D), dtype=jnp.float32), 'decay': jnp.float32(0.9), 'W_in': jax.random.normal(ks[2], (D, D), dtype=jnp.float32) * scale, 'b_in': jnp.zeros((D,), dtype=jnp.float32), 'W_out': jax.random.normal(ks[3], (D, D), dtype=jnp.float32) * scale, 'b_out': jnp.zeros((D,), dtype=jnp.float32), 'gamma': jnp.ones((D,), dtype=jnp.float32), 'beta': jnp.zeros((D,), dtype=jnp.float32)}
    _L1_xattn_all = _L1_xattn_setup()
    _L1_xattn_in = {k: v for k, v in _L1_xattn_all.items() if k in ('decay', 'W_in', 'b_in', 'W_out', 'b_out', 'gamma', 'beta')}
    del _L1_xattn_all

    def _L1_ffn_setup():
        import jax, jax.numpy as jnp
        import numpy as np
        H = 256
        E = 64
        I = 64
        SI = 64
        TOP_K = 8
        B, T = (2, 64)
        key = jax.random.key(seed)
        ks = jax.random.split(key, 8)
        s = 0.02
        return {'h': jax.random.normal(ks[0], (B, T, H), jnp.float32), 'gate_w': jax.random.normal(ks[1], (E, H), jnp.float32) * s, 'gu_w': jax.random.normal(ks[2], (E, 2 * I, H), jnp.float32) * s, 'dp_w': jax.random.normal(ks[3], (E, H, I), jnp.float32) * s, 'sh_gate_w': jax.random.normal(ks[4], (SI, H), jnp.float32) * s, 'sh_up_w': jax.random.normal(ks[5], (SI, H), jnp.float32) * s, 'sh_down_w': jax.random.normal(ks[6], (H, SI), jnp.float32) * s, 'sh_gate1_w': jax.random.normal(ks[7], (1, H), jnp.float32) * s}
    _L1_ffn_all = _L1_ffn_setup()
    _L1_ffn_in = {k: v for k, v in _L1_ffn_all.items() if k in ('gate_w', 'gu_w', 'dp_w', 'sh_gate_w', 'sh_up_w', 'sh_down_w', 'sh_gate1_w')}
    del _L1_ffn_all

    def _L2_xattn_setup():
        import jax, jax.numpy as jnp
        import numpy as np
        import math
        B, S, HID, H = (2, 256, 256, 32)
        D = HID // H
        AL = 10

        def _rope_tables(seq_len, dim, dtype):
            inv_freq = 1.0 / 10000.0 ** (np.arange(0, dim, 2, dtype=np.float32) / dim)
            t = np.arange(seq_len, dtype=np.float32)
            freqs = np.outer(t, inv_freq)
            emb = np.concatenate([freqs, freqs], -1)
            return (jnp.asarray(np.cos(emb), dtype), jnp.asarray(np.sin(emb), dtype))

        def _rotate_half(x):
            x1, x2 = jnp.split(x, 2, axis=-1)
            return jnp.concatenate([-x2, x1], axis=-1)
        key = jax.random.key(seed)
        ks = jax.random.split(key, 8)
        hidden_states = jax.random.normal(ks[0], (B, S, HID), dtype=jnp.float32)
        adapter = jax.random.normal(ks[1], (B, AL, HID), dtype=jnp.float32)
        causal = jnp.tril(jnp.ones((S, S), dtype=bool))
        attention_mask = jnp.broadcast_to(jnp.where(causal, 0.0, -1000000000.0).astype(jnp.float32)[None, None], (B, 1, S, S))
        scale = 0.02
        Wq = jax.random.normal(ks[2], (HID, HID), dtype=jnp.float32) * scale
        Wk = jax.random.normal(ks[3], (HID, HID), dtype=jnp.float32) * scale
        Wv = jax.random.normal(ks[4], (HID, HID), dtype=jnp.float32) * scale
        Wo = jax.random.normal(ks[5], (HID, HID), dtype=jnp.float32) * scale
        gate = jax.random.normal(ks[6], (1, H, 1, 1), dtype=jnp.float32) * 0.1
        return {'hidden_states': hidden_states, 'attention_mask': attention_mask, 'adapter': adapter, 'Wq': Wq, 'Wk': Wk, 'Wv': Wv, 'Wo': Wo, 'gate': gate}
    _L2_xattn_all = _L2_xattn_setup()
    _L2_xattn_in = {k: v for k, v in _L2_xattn_all.items() if k in ('Wq', 'Wk', 'Wv', 'Wo', 'gate')}
    del _L2_xattn_all

    def _L2_ffn_setup():
        import jax, jax.numpy as jnp
        import numpy as np
        B, S, H = (4, 512, 256)
        I = 176
        E = 8
        K = 2
        INIT = 0.02
        key = jax.random.key(seed)
        k0, k1, k2, k3, k4, k5 = jax.random.split(key, 6)
        return {'x': jax.random.normal(k0, (B, S, H), dtype=jnp.float32), 'w_shared1': jax.random.normal(k1, (H, I), dtype=jnp.float32) * INIT, 'w_shared2': jax.random.normal(k2, (I, H), dtype=jnp.float32) * INIT, 'w1': jax.random.normal(k3, (E, H, I), dtype=jnp.float32) * INIT, 'w2': jax.random.normal(k4, (E, I, H), dtype=jnp.float32) * INIT, 'w_router': jax.random.normal(k5, (H, E), dtype=jnp.float32) * INIT}
    _L2_ffn_all = _L2_ffn_setup()
    _L2_ffn_in = {k: v for k, v in _L2_ffn_all.items() if k in ('w_shared1', 'w_shared2', 'w1', 'w2', 'w_router')}
    del _L2_ffn_all

    def _L3_xattn_setup():
        import jax, jax.numpy as jnp
        import numpy as np
        EPS = 1e-06
        NUM_HEADS = 16

        def _feature_map(x):
            return jnp.where(x > 0, x + 1.0, jnp.exp(x))
        key = jax.random.key(seed)
        ks = jax.random.split(key, 7)
        B, L, S, D = (4, 512, 512, 256)
        sc = 1.0 / np.sqrt(D)
        return {'query': jax.random.normal(ks[0], (B, L, D), jnp.float32), 'kv': jax.random.normal(ks[1], (B, S, D), jnp.float32), 'Wq': jax.random.normal(ks[2], (D, D), jnp.float32) * sc, 'Wg': jax.random.normal(ks[3], (D, D), jnp.float32) * sc, 'bg': jnp.ones((D,), jnp.float32), 'Wkv': jax.random.normal(ks[4], (2 * D, D), jnp.float32) * sc, 'Wo': jax.random.normal(ks[5], (D, D), jnp.float32) * sc}
    _L3_xattn_all = _L3_xattn_setup()
    _L3_xattn_in = {k: v for k, v in _L3_xattn_all.items() if k in ('Wq', 'Wg', 'bg', 'Wkv', 'Wo')}
    del _L3_xattn_all

    def _L3_ffn_setup():
        import jax, jax.numpy as jnp
        import numpy as np
        H = 256
        I = 176
        E = 16
        G = 4
        TOPK_GROUP = 2
        TOP_K = 6
        N_SHARED = 2
        SCALE_FACTOR = 2.5
        B, S = (2, 256)

        def _gate(hs_flat, gate_weight, bias):
            T = hs_flat.shape[0]
            logits = hs_flat @ gate_weight.T
            scores = jax.nn.sigmoid(logits)
            scores_for_choice = scores + bias[None, :]
            gs = scores_for_choice.reshape(T, G, E // G)
            group_scores = jnp.sum(jax.lax.top_k(gs, 2)[0], axis=-1)
            _, group_idx = jax.lax.top_k(group_scores, TOPK_GROUP)
            group_mask = jnp.zeros((T, G), scores.dtype).at[jnp.arange(T)[:, None], group_idx].set(1.0)
            score_mask = jnp.repeat(group_mask, E // G, axis=1)
            tmp_scores = jnp.where(score_mask > 0, scores_for_choice, 0.0)
            _, topk_idx = jax.lax.top_k(tmp_scores, TOP_K)
            topk_weight = jnp.take_along_axis(scores, topk_idx, axis=1)
            topk_weight = topk_weight / (jnp.sum(topk_weight, axis=-1, keepdims=True) + 1e-20)
            topk_weight = topk_weight * SCALE_FACTOR
            return (topk_idx, topk_weight)
        key = jax.random.key(seed)
        ks = jax.random.split(key, 8)
        scale = 0.01
        SI = I * N_SHARED
        return {'hidden_states': jax.random.normal(ks[0], (B, S, H), jnp.float32), 'gate_weight': jax.random.uniform(ks[1], (E, H), jnp.float32, -0.05, 0.05), 'e_score_correction_bias': jnp.zeros((E,), jnp.float32), 'gate_proj': jax.random.normal(ks[2], (E, I, H), jnp.float32) * scale, 'up_proj': jax.random.normal(ks[3], (E, I, H), jnp.float32) * scale, 'down_proj': jax.random.normal(ks[4], (E, H, I), jnp.float32) * scale, 'shared_gate_w': jax.random.normal(ks[5], (SI, H), jnp.float32) * scale, 'shared_up_w': jax.random.normal(ks[6], (SI, H), jnp.float32) * scale, 'shared_down_w': jax.random.normal(ks[7], (H, SI), jnp.float32) * scale}
    _L3_ffn_all = _L3_ffn_setup()
    _L3_ffn_in = {k: v for k, v in _L3_ffn_all.items() if k in ('gate_weight', 'e_score_correction_bias', 'gate_proj', 'up_proj', 'down_proj', 'shared_gate_w', 'shared_up_w', 'shared_down_w')}
    del _L3_ffn_all
    return {'x': x, 'ctx_2048': ctx_2048, 'mask_Bx1xSxS_fk0': mask_Bx1xSxS_fk0, 'L0_xattn_context_lens': _L0_xattn_in['context_lens'], 'L0_xattn_Wq': _L0_xattn_in['Wq'], 'L0_xattn_bq': _L0_xattn_in['bq'], 'L0_xattn_gq': _L0_xattn_in['gq'], 'L0_xattn_Wk': _L0_xattn_in['Wk'], 'L0_xattn_bk': _L0_xattn_in['bk'], 'L0_xattn_gk': _L0_xattn_in['gk'], 'L0_xattn_Wv': _L0_xattn_in['Wv'], 'L0_xattn_bv': _L0_xattn_in['bv'], 'L0_xattn_Wk_img': _L0_xattn_in['Wk_img'], 'L0_xattn_bk_img': _L0_xattn_in['bk_img'], 'L0_xattn_gk_img': _L0_xattn_in['gk_img'], 'L0_xattn_Wv_img': _L0_xattn_in['Wv_img'], 'L0_xattn_bv_img': _L0_xattn_in['bv_img'], 'L0_xattn_Wo': _L0_xattn_in['Wo'], 'L0_xattn_bo': _L0_xattn_in['bo'], 'L0_ffn_ln1_w': _L0_ffn_in['ln1_w'], 'L0_ffn_ln2_w': _L0_ffn_in['ln2_w'], 'L0_ffn_Wq': _L0_ffn_in['Wq'], 'L0_ffn_Wk': _L0_ffn_in['Wk'], 'L0_ffn_Wv': _L0_ffn_in['Wv'], 'L0_ffn_Wo': _L0_ffn_in['Wo'], 'L0_ffn_A': _L0_ffn_in['A'], 'L0_ffn_B': _L0_ffn_in['B'], 'L0_ffn_W_in_base': _L0_ffn_in['W_in_base'], 'L0_ffn_W_up_base': _L0_ffn_in['W_up_base'], 'L0_ffn_W_down': _L0_ffn_in['W_down'], 'L1_xattn_decay': _L1_xattn_in['decay'], 'L1_xattn_W_in': _L1_xattn_in['W_in'], 'L1_xattn_b_in': _L1_xattn_in['b_in'], 'L1_xattn_W_out': _L1_xattn_in['W_out'], 'L1_xattn_b_out': _L1_xattn_in['b_out'], 'L1_xattn_gamma': _L1_xattn_in['gamma'], 'L1_xattn_beta': _L1_xattn_in['beta'], 'L1_ffn_gate_w': _L1_ffn_in['gate_w'], 'L1_ffn_gu_w': _L1_ffn_in['gu_w'], 'L1_ffn_dp_w': _L1_ffn_in['dp_w'], 'L1_ffn_sh_gate_w': _L1_ffn_in['sh_gate_w'], 'L1_ffn_sh_up_w': _L1_ffn_in['sh_up_w'], 'L1_ffn_sh_down_w': _L1_ffn_in['sh_down_w'], 'L1_ffn_sh_gate1_w': _L1_ffn_in['sh_gate1_w'], 'L2_xattn_Wq': _L2_xattn_in['Wq'], 'L2_xattn_Wk': _L2_xattn_in['Wk'], 'L2_xattn_Wv': _L2_xattn_in['Wv'], 'L2_xattn_Wo': _L2_xattn_in['Wo'], 'L2_xattn_gate': _L2_xattn_in['gate'], 'L2_ffn_w_shared1': _L2_ffn_in['w_shared1'], 'L2_ffn_w_shared2': _L2_ffn_in['w_shared2'], 'L2_ffn_w1': _L2_ffn_in['w1'], 'L2_ffn_w2': _L2_ffn_in['w2'], 'L2_ffn_w_router': _L2_ffn_in['w_router'], 'L3_xattn_Wq': _L3_xattn_in['Wq'], 'L3_xattn_Wg': _L3_xattn_in['Wg'], 'L3_xattn_bg': _L3_xattn_in['bg'], 'L3_xattn_Wkv': _L3_xattn_in['Wkv'], 'L3_xattn_Wo': _L3_xattn_in['Wo'], 'L3_ffn_gate_weight': _L3_ffn_in['gate_weight'], 'L3_ffn_e_score_correction_bias': _L3_ffn_in['e_score_correction_bias'], 'L3_ffn_gate_proj': _L3_ffn_in['gate_proj'], 'L3_ffn_up_proj': _L3_ffn_in['up_proj'], 'L3_ffn_down_proj': _L3_ffn_in['down_proj'], 'L3_ffn_shared_gate_w': _L3_ffn_in['shared_gate_w'], 'L3_ffn_shared_up_w': _L3_ffn_in['shared_up_w'], 'L3_ffn_shared_down_w': _L3_ffn_in['shared_down_w']}

def reference(x, ctx_2048, mask_Bx1xSxS_fk0, L0_xattn_context_lens, L0_xattn_Wq, L0_xattn_bq, L0_xattn_gq, L0_xattn_Wk, L0_xattn_bk, L0_xattn_gk, L0_xattn_Wv, L0_xattn_bv, L0_xattn_Wk_img, L0_xattn_bk_img, L0_xattn_gk_img, L0_xattn_Wv_img, L0_xattn_bv_img, L0_xattn_Wo, L0_xattn_bo, L0_ffn_ln1_w, L0_ffn_ln2_w, L0_ffn_Wq, L0_ffn_Wk, L0_ffn_Wv, L0_ffn_Wo, L0_ffn_A, L0_ffn_B, L0_ffn_W_in_base, L0_ffn_W_up_base, L0_ffn_W_down, L1_xattn_decay, L1_xattn_W_in, L1_xattn_b_in, L1_xattn_W_out, L1_xattn_b_out, L1_xattn_gamma, L1_xattn_beta, L1_ffn_gate_w, L1_ffn_gu_w, L1_ffn_dp_w, L1_ffn_sh_gate_w, L1_ffn_sh_up_w, L1_ffn_sh_down_w, L1_ffn_sh_gate1_w, L2_xattn_Wq, L2_xattn_Wk, L2_xattn_Wv, L2_xattn_Wo, L2_xattn_gate, L2_ffn_w_shared1, L2_ffn_w_shared2, L2_ffn_w1, L2_ffn_w2, L2_ffn_w_router, L3_xattn_Wq, L3_xattn_Wg, L3_xattn_bg, L3_xattn_Wkv, L3_xattn_Wo, L3_ffn_gate_weight, L3_ffn_e_score_correction_bias, L3_ffn_gate_proj, L3_ffn_up_proj, L3_ffn_down_proj, L3_ffn_shared_gate_w, L3_ffn_shared_up_w, L3_ffn_shared_down_w):
    import jax
    import jax.numpy as jnp

    def _L0_xattn_ref(x, context, context_lens, Wq, bq, gq, Wk, bk, gk, Wv, bv, Wk_img, bk_img, gk_img, Wv_img, bv_img, Wo, bo):
        import jax, jax.numpy as jnp
        import numpy as np
        DIM = 256
        N_HEADS = 16
        HEAD_DIM = DIM // N_HEADS
        EPS = 1e-06
        IMG_LEN = 257

        def rms_norm(x, g, eps=EPS):
            var = jnp.mean(x * x, axis=-1, keepdims=True)
            return x * jax.lax.rsqrt(var + eps) * g

        def _attend(q, k, v, k_mask=None):
            scale = 1.0 / jnp.sqrt(jnp.asarray(HEAD_DIM, q.dtype))
            scores = jnp.einsum('bqnd,bknd->bnqk', q, k) * scale
            if k_mask is not None:
                neg = jnp.asarray(jnp.finfo(scores.dtype).min, scores.dtype)
                scores = jnp.where(k_mask[:, None, None, :], scores, neg)
            probs = jax.nn.softmax(scores, axis=-1)
            return jnp.einsum('bnqk,bknd->bqnd', probs, v)
        b = x.shape[0]
        n, d = (N_HEADS, HEAD_DIM)
        ctx_img = context[:, :IMG_LEN]
        ctx_txt = context[:, IMG_LEN:]
        q = rms_norm(x @ Wq + bq, gq).reshape(b, -1, n, d)
        k = rms_norm(ctx_txt @ Wk + bk, gk).reshape(b, -1, n, d)
        v = (ctx_txt @ Wv + bv).reshape(b, -1, n, d)
        k_img = rms_norm(ctx_img @ Wk_img + bk_img, gk_img).reshape(b, -1, n, d)
        v_img = (ctx_img @ Wv_img + bv_img).reshape(b, -1, n, d)
        img_x = _attend(q, k_img, v_img)
        k_mask = jnp.arange(k.shape[1])[None, :] < context_lens[:, None]
        txt_x = _attend(q, k, v, k_mask)
        out = (txt_x + img_x).reshape(b, -1, n * d)
        return out @ Wo + bo

    def _L0_ffn_ref(hidden_states, ln1_w, ln2_w, Wq, Wk, Wv, Wo, A, B, W_in_base, W_up_base, W_down):
        import jax, jax.numpy as jnp
        import numpy as np
        B_, S, D = (2, 256, 256)
        F_ = 1024
        R = 16
        H = 16
        HD = D // H
        MOD_SCALE = 0.1
        EPS = 1e-06

        def _rmsnorm(x, w):
            v = jnp.mean(x * x, axis=-1, keepdims=True)
            return x * jax.lax.rsqrt(v + EPS) * w

        def _attention(x, Wq, Wk, Wv, Wo):
            b, s, d = x.shape
            q = (x @ Wq.T).reshape(b, s, H, HD)
            k = (x @ Wk.T).reshape(b, s, H, HD)
            v = (x @ Wv.T).reshape(b, s, H, HD)
            scores = jnp.einsum('bqhd,bkhd->bhqk', q, k) / np.sqrt(HD).astype(np.float32)
            causal = jnp.tril(jnp.ones((s, s), bool))
            scores = jnp.where(causal, scores, jnp.finfo(scores.dtype).min)
            probs = jax.nn.softmax(scores, axis=-1)
            out = jnp.einsum('bhqk,bkhd->bqhd', probs, v).reshape(b, s, d)
            return out @ Wo.T
        residual = hidden_states
        x = _rmsnorm(hidden_states, ln1_w)
        attn = _attention(x, Wq, Wk, Wv, Wo)
        mod = MOD_SCALE * jnp.tanh(attn @ A)
        h = _rmsnorm(residual, ln2_w)
        gate_pre = h @ W_in_base.T + mod * (h @ A) @ B
        gate = jax.nn.silu(gate_pre)
        up = h @ W_up_base.T
        mlp_out = gate * up @ W_down.T
        return residual + mlp_out

    def _L1_xattn_ref(Z, kv, decay, W_in, b_in, W_out, b_out, gamma, beta):
        import jax, jax.numpy as jnp
        import numpy as np
        from jax import lax
        LN_EPS = 1e-05
        B, T, D = kv.shape
        K = jax.nn.sigmoid(decay)
        x = jnp.einsum('btd,ed->bte', kv, W_in) + b_in

        def scan_fn(s, xt):
            s = K * s + xt
            return (s, s)
        s0 = jnp.zeros((B, D), dtype=kv.dtype)
        _, states = lax.scan(scan_fn, s0, jnp.swapaxes(x, 0, 1))
        states = jnp.swapaxes(states, 0, 1)
        proj = jnp.einsum('btd,ed->bte', states, W_out) + b_out
        summary = jnp.mean(proj, axis=1, keepdims=True)
        y = Z + summary
        mu = jnp.mean(y, axis=-1, keepdims=True)
        var = jnp.mean((y - mu) ** 2, axis=-1, keepdims=True)
        return (y - mu) / jnp.sqrt(var + LN_EPS) * gamma + beta

    def _L1_ffn_ref(h, gate_w, gu_w, dp_w, sh_gate_w, sh_up_w, sh_down_w, sh_gate1_w):
        import jax, jax.numpy as jnp
        import numpy as np
        H = 256
        E = 64
        I = 64
        SI = 64
        TOP_K = 8
        B, T = (2, 64)
        Bb, Tt, Hh = h.shape
        x = h.reshape(Bb * Tt, Hh)
        N = x.shape[0]
        logits = x @ gate_w.T
        topv, topi = jax.lax.top_k(logits, TOP_K)
        rw = jax.nn.softmax(topv.astype(jnp.float32), axis=-1).astype(x.dtype)
        W = jnp.zeros((N, E), x.dtype).at[jnp.arange(N)[:, None], topi].set(rw)
        gu = jnp.einsum('nh,eih->nei', x, gu_w)
        gate, up = (gu[..., :I], gu[..., I:])
        inter = jax.nn.silu(gate) * up
        inter_w = inter * W[:, :, None]
        out = jnp.einsum('nei,ehi->nh', inter_w, dp_w)
        sh_inter = jax.nn.silu(x @ sh_gate_w.T) * (x @ sh_up_w.T)
        sh_out = sh_inter @ sh_down_w.T
        sh_g = jax.nn.sigmoid(x @ sh_gate1_w.T)
        out = out + sh_g * sh_out
        return out.reshape(Bb, Tt, Hh)

    def _L2_xattn_ref(hidden_states, attention_mask, adapter, Wq, Wk, Wv, Wo, gate):
        import jax, jax.numpy as jnp
        import numpy as np
        import math
        B, S, HID, H = (2, 256, 256, 32)
        D = HID // H
        AL = 10

        def _rope_tables(seq_len, dim, dtype):
            inv_freq = 1.0 / 10000.0 ** (np.arange(0, dim, 2, dtype=np.float32) / dim)
            t = np.arange(seq_len, dtype=np.float32)
            freqs = np.outer(t, inv_freq)
            emb = np.concatenate([freqs, freqs], -1)
            return (jnp.asarray(np.cos(emb), dtype), jnp.asarray(np.sin(emb), dtype))

        def _rotate_half(x):
            x1, x2 = jnp.split(x, 2, axis=-1)
            return jnp.concatenate([-x2, x1], axis=-1)
        bsz, q_len, hid = hidden_states.shape
        n_heads = gate.shape[1]
        head_dim = hid // n_heads
        inv_sqrt_d = 1.0 / math.sqrt(head_dim)

        def split_heads(x, length):
            return x.reshape(bsz, length, n_heads, head_dim).transpose(0, 2, 1, 3)
        q = split_heads(hidden_states @ Wq, q_len)
        k = split_heads(hidden_states @ Wk, q_len)
        v = split_heads(hidden_states @ Wv, q_len)
        cos, sin = _rope_tables(q_len, head_dim, q.dtype)
        q = q * cos + _rotate_half(q) * sin
        k = k * cos + _rotate_half(k) * sin
        scores = jnp.einsum('bhqd,bhkd->bhqk', q, k) * inv_sqrt_d
        scores = scores + attention_mask
        scores = jnp.maximum(scores, jnp.finfo(scores.dtype).min)
        w = jax.nn.softmax(scores.astype(jnp.float32), axis=-1).astype(q.dtype)
        attn_output = jnp.einsum('bhqk,bhkd->bhqd', w, v)
        adapter_len = adapter.shape[1]
        a_k = split_heads(adapter @ Wk, adapter_len)
        a_v = split_heads(adapter @ Wv, adapter_len)
        a_scores = jnp.einsum('bhqd,bhkd->bhqk', q, a_k) * inv_sqrt_d
        a_scores = jnp.tanh(gate) * jax.nn.softmax(a_scores.astype(jnp.float32), axis=-1).astype(q.dtype)
        attn_output = attn_output + jnp.einsum('bhqk,bhkd->bhqd', a_scores, a_v)
        attn_output = attn_output.transpose(0, 2, 1, 3).reshape(bsz, q_len, hid)
        return attn_output @ Wo

    def _L2_ffn_ref(x, w_shared1, w_shared2, w1, w2, w_router):
        import jax, jax.numpy as jnp
        import numpy as np
        B, S, H = (4, 512, 256)
        I = 176
        E = 8
        K = 2
        INIT = 0.02
        bs, seq_len, hidden = x.shape
        xf = x.reshape(-1, hidden)
        T = xf.shape[0]
        shared = jax.nn.silu(xf @ w_shared1) @ w_shared2
        router_logits = xf @ w_router
        routing_probs = jax.nn.softmax(router_logits, axis=-1)
        top_k_probs, top_k_idx = jax.lax.top_k(routing_probs, K)
        top_k_probs = top_k_probs / jnp.sum(top_k_probs, axis=-1, keepdims=True)
        comb = jnp.zeros((T, E), dtype=xf.dtype).at[jnp.arange(T)[:, None], top_k_idx].add(top_k_probs)
        routed = jnp.zeros_like(xf)
        for e in range(E):
            expert_out = jax.nn.silu(xf @ w1[e]) @ w2[e]
            routed = routed + comb[:, e:e + 1] * expert_out
        final = (shared + routed).reshape(bs, seq_len, hidden)
        return final

    def _L3_xattn_ref(query, kv, Wq, Wg, bg, Wkv, Wo):
        import jax, jax.numpy as jnp
        import numpy as np
        EPS = 1e-06
        NUM_HEADS = 16

        def _feature_map(x):
            return jnp.where(x > 0, x + 1.0, jnp.exp(x))
        B, L, D = query.shape
        S = kv.shape[1]
        H = NUM_HEADS
        hd = D // H
        q = query @ Wq.T
        gate = jax.nn.sigmoid(query @ Wg.T + bg)
        kvp = kv @ Wkv.T
        k, v = jnp.split(kvp, 2, axis=-1)
        q = _feature_map(q.reshape(B, L, H, hd).transpose(0, 2, 1, 3))
        k = _feature_map(k.reshape(B, S, H, hd).transpose(0, 2, 1, 3))
        v = v.reshape(B, S, H, hd).transpose(0, 2, 1, 3)
        kv_summary = jnp.einsum('bhsd,bhse->bhde', k, v)
        k_sum = k.sum(axis=-2)
        z = 1.0 / (jnp.einsum('bhld,bhd->bhl', q, k_sum)[..., None] + EPS)
        attn = jnp.einsum('bhld,bhde->bhle', q, kv_summary) * z
        attn = attn.transpose(0, 2, 1, 3).reshape(B, L, D)
        out = attn * gate @ Wo.T
        return out

    def _L3_ffn_ref(hidden_states, gate_weight, e_score_correction_bias, gate_proj, up_proj, down_proj, shared_gate_w, shared_up_w, shared_down_w):
        import jax, jax.numpy as jnp
        import numpy as np
        H = 256
        I = 176
        E = 16
        G = 4
        TOPK_GROUP = 2
        TOP_K = 6
        N_SHARED = 2
        SCALE_FACTOR = 2.5
        B, S = (2, 256)

        def _gate(hs_flat, gate_weight, bias):
            T = hs_flat.shape[0]
            logits = hs_flat @ gate_weight.T
            scores = jax.nn.sigmoid(logits)
            scores_for_choice = scores + bias[None, :]
            gs = scores_for_choice.reshape(T, G, E // G)
            group_scores = jnp.sum(jax.lax.top_k(gs, 2)[0], axis=-1)
            _, group_idx = jax.lax.top_k(group_scores, TOPK_GROUP)
            group_mask = jnp.zeros((T, G), scores.dtype).at[jnp.arange(T)[:, None], group_idx].set(1.0)
            score_mask = jnp.repeat(group_mask, E // G, axis=1)
            tmp_scores = jnp.where(score_mask > 0, scores_for_choice, 0.0)
            _, topk_idx = jax.lax.top_k(tmp_scores, TOP_K)
            topk_weight = jnp.take_along_axis(scores, topk_idx, axis=1)
            topk_weight = topk_weight / (jnp.sum(topk_weight, axis=-1, keepdims=True) + 1e-20)
            topk_weight = topk_weight * SCALE_FACTOR
            return (topk_idx, topk_weight)
        b, s, h = hidden_states.shape
        hs = hidden_states.reshape(-1, h)
        T = hs.shape[0]
        topk_idx, topk_weight = _gate(hs, gate_weight, e_score_correction_bias)
        comb = jnp.zeros((T, E), hs.dtype).at[jnp.arange(T)[:, None], topk_idx].add(topk_weight)
        out = jnp.zeros_like(hs)
        for e in range(E):
            g = hs @ gate_proj[e].T
            u = hs @ up_proj[e].T
            inter = jax.nn.silu(g) * u
            out = out + comb[:, e:e + 1] * (inter @ down_proj[e].T)
        y = out.reshape(b, s, h)
        sg = hidden_states @ shared_gate_w.T
        su = hidden_states @ shared_up_w.T
        shared_out = jax.nn.silu(sg) * su @ shared_down_w.T
        return y + shared_out
    x = x + _L0_xattn_ref(_layernorm(x, axis=-1), ctx_2048, L0_xattn_context_lens, L0_xattn_Wq, L0_xattn_bq, L0_xattn_gq, L0_xattn_Wk, L0_xattn_bk, L0_xattn_gk, L0_xattn_Wv, L0_xattn_bv, L0_xattn_Wk_img, L0_xattn_bk_img, L0_xattn_gk_img, L0_xattn_Wv_img, L0_xattn_bv_img, L0_xattn_Wo, L0_xattn_bo)
    x = x + _L0_ffn_ref(_layernorm(x, axis=-1), L0_ffn_ln1_w, L0_ffn_ln2_w, L0_ffn_Wq, L0_ffn_Wk, L0_ffn_Wv, L0_ffn_Wo, L0_ffn_A, L0_ffn_B, L0_ffn_W_in_base, L0_ffn_W_up_base, L0_ffn_W_down)
    x = x + _L1_xattn_ref(_layernorm(x, axis=-1), ctx_2048, L1_xattn_decay, L1_xattn_W_in, L1_xattn_b_in, L1_xattn_W_out, L1_xattn_b_out, L1_xattn_gamma, L1_xattn_beta)
    x = x + _L1_ffn_ref(_layernorm(x, axis=-1), L1_ffn_gate_w, L1_ffn_gu_w, L1_ffn_dp_w, L1_ffn_sh_gate_w, L1_ffn_sh_up_w, L1_ffn_sh_down_w, L1_ffn_sh_gate1_w)
    x = x + _L2_xattn_ref(_layernorm(x, axis=-1), mask_Bx1xSxS_fk0, ctx_2048, L2_xattn_Wq, L2_xattn_Wk, L2_xattn_Wv, L2_xattn_Wo, L2_xattn_gate)
    x = x + _L2_ffn_ref(_layernorm(x, axis=-1), L2_ffn_w_shared1, L2_ffn_w_shared2, L2_ffn_w1, L2_ffn_w2, L2_ffn_w_router)
    x = x + _L3_xattn_ref(_layernorm(x, axis=-1), ctx_2048, L3_xattn_Wq, L3_xattn_Wg, L3_xattn_bg, L3_xattn_Wkv, L3_xattn_Wo)
    x = x + _L3_ffn_ref(_layernorm(x, axis=-1), L3_ffn_gate_weight, L3_ffn_e_score_correction_bias, L3_ffn_gate_proj, L3_ffn_up_proj, L3_ffn_down_proj, L3_ffn_shared_gate_w, L3_ffn_shared_up_w, L3_ffn_shared_down_w)
    return x

_drawn_inputs = setup_inputs


def setup_inputs(seed=0):
    import zlib

    import numpy as np

    out = dict(_drawn_inputs(seed))
    spreads = {'L0_xattn_bq': (0.0, 0.8),
     'L0_xattn_gq': (1.0, 0.6),
     'L0_xattn_bk': (0.0, 0.8),
     'L0_xattn_gk': (1.0, 0.6),
     'L0_xattn_bv': (0.0, 0.1),
     'L0_xattn_bk_img': (0.0, 0.8),
     'L0_xattn_gk_img': (1.0, 0.6),
     'L0_xattn_bv_img': (0.0, 0.1),
     'L0_xattn_bo': (0.0, 0.1),
     'L0_ffn_ln1_w': (1.0, 0.6),
     'L0_ffn_ln2_w': (1.0, 0.6),
     'L1_xattn_b_in': (0.0, 0.1),
     'L1_xattn_b_out': (0.0, 0.1),
     'L1_xattn_gamma': (1.0, 0.2),
     'L1_xattn_beta': (0.0, 0.1),
     'L3_xattn_bg': (1.0, 0.6),
     'L3_ffn_e_score_correction_bias': (0.0, 0.8)}
    factors = {'L0_xattn_Wk': 3.0,
     'L0_xattn_Wk_img': 3.063,
     'L0_ffn_Wq': 55.205,
     'L0_ffn_Wk': 61.583,
     'L0_ffn_Wv': 59.786,
     'L0_ffn_Wo': 64.0,
     'L0_ffn_A': 58.955,
     'L0_ffn_B': 61.476,
     'L0_ffn_W_in_base': 3.051,
     'L0_ffn_W_up_base': 3.011,
     'L0_ffn_W_down': 3.023,
     'L1_ffn_gate_w': 8.0,
     'L1_ffn_gu_w': 8.0,
     'L1_ffn_dp_w': 8.0,
     'L1_ffn_sh_gate_w': 8.0,
     'L1_ffn_sh_up_w': 8.0,
     'L1_ffn_sh_down_w': 8.0,
     'L1_ffn_sh_gate1_w': 8.0,
     'L2_xattn_Wq': 8.0,
     'L2_xattn_Wk': 8.0,
     'L2_xattn_Wv': 7.087,
     'L2_xattn_Wo': 7.253,
     'L2_xattn_gate': 8.0,
     'L2_ffn_w_shared1': 3.948,
     'L2_ffn_w_shared2': 3.933,
     'L2_ffn_w1': 5.587,
     'L2_ffn_w2': 5.506,
     'L2_ffn_w_router': 6.237,
     'L3_xattn_Wq': 64.0,
     'L3_ffn_gate_weight': 8.0,
     'L3_ffn_gate_proj': 8.0,
     'L3_ffn_up_proj': 8.0,
     'L3_ffn_down_proj': 8.0,
     'L3_ffn_shared_gate_w': 8.0,
     'L3_ffn_shared_up_w': 8.0,
     'L3_ffn_shared_down_w': 8.0,
     'L3_xattn_Wg': 3.942}
    for name, (base, spread) in spreads.items():
        noise = np.random.default_rng([zlib.crc32(name.encode()), seed]).standard_normal(out[name].shape)
        drawn = base * np.exp(spread * noise) if base else spread * noise
        out[name] = jnp.asarray(drawn.astype(out[name].dtype))
    for name, factor in factors.items():
        out[name] = (out[name] * factor).astype(out[name].dtype)
    return out
```

```python
from contextlib import ExitStack

import numpy as np
import concourse.bass as bass
from concourse import mybir

F32 = mybir.dt.float32
BF16 = mybir.dt.bfloat16
I32 = mybir.dt.int32
ALU = mybir.AluOpType
ACT = mybir.ActivationFunctionType
AX = mybir.AxisListType

P = 128
NB = 4
S = 256
D = 256
CTX = 1601
IMG = 257
TXT = CTX - IMG
BIG = 2.0 ** 100
LOWEST = -3.4028234663852886e38

L0_TILES = [(0, 128), (128, 128), (256, 1)] + [(IMG + P * t, min(P, TXT - P * t)) for t in range(11)]
CTX_TILES = [(P * t, min(P, CTX - P * t)) for t in range(13)]
L0_SPANS = [(0, IMG)] + [(IMG + 448 * c, 448) for c in range(3)]
L2_SPANS = [(400 * c, 401) for c in range(4)]

C_EPS5, C_EPS6, C_ONE = 0, 1, 2
C_KEY = 3
C_TAIL = C_KEY + 11
C_COS = C_TAIL + 14 * 7
C_SIN = C_COS + 16
C_BLK = C_SIN + 16
C_BMASK = C_BLK + 8
C_IDENT = C_BMASK + 128
C_CAUSAL = C_IDENT + 128
NCST = C_CAUSAL + 512

FFNS = {"f1": (True, 33, 65), "f2": (False, 13, 9), "f3": (True, 25, 17)}


class Counts:

    def __init__(self, eng, tag, steps):
        self.eng, self.tag, self.steps = eng, tag, steps
        self.total, self.frame = {}, None

    def same(self, sem, more=0):
        name = sem.name
        if self.frame is None:
            return self.total.get(name, 0) + more
        i, key, seen = self.frame
        per = self.steps.get((self.tag, key), {}).get(name, 0)
        return i * per + (self.total.get(name, 0) + seen.get(name, 0) + more)

    def skip(self, sem, n=1):
        store = self.total if self.frame is None else self.frame[2]
        store[sem.name] = store.get(sem.name, 0) + n

    def up(self, sem, n=1):
        self.skip(sem, n)
        return self.same(sem)

    def settle(self, sem):
        if self.frame is not None:
            self.eng.sem_inc(sem, 1)

    def loop(self, count, key):
        seen = {}
        with self.eng.Fori(0, count) as i:
            self.frame = (i, key, seen)
            yield i
        self.frame = None
        self.steps[(self.tag, key)] = seen
        for name, n in seen.items():
            self.total[name] = self.total.get(name, 0) + count * n


def build(nc, d, out, steps):
    with ExitStack() as top:
        sems = {}

        def sem(name):
            if name not in sems:
                sems[name] = top.enter_context(nc.semaphore(name))
            return sems[name]

        def sbuf(ctx, name, shape, dt=F32):
            return ctx.enter_context(nc.sbuf_tensor(name, shape, dt))[tuple(slice(None) for _ in shape)]

        act_step, dve_step, pool_step = sem("act_step"), sem("dve_step"), sem("pool_step")
        consts_in = sem("consts_in")
        consts_ready = sem("consts_ready")
        phase_end = sem("phase_end")
        w_in = sem("w_in")
        ctx_in, ctx_used = sem("ctx_in"), sem("ctx_used")
        mask_in, mask_used = sem("mask_in"), sem("mask_used")
        tr_full, tr_free = sem("tr_full"), sem("tr_free")
        ln_var, ln_std = sem("ln_var"), sem("ln_std")
        t2_in, t2_out = sem("t2_in"), sem("t2_out")
        q_ps, q_sb = sem("q_ps"), sem("q_sb")
        kv_ps, kv_free = sem("kv_ps"), sem("kv_free")
        kraw_ready, ss_ready, k_std = sem("kraw_ready"), sem("ss_ready"), sem("k_std")
        kn_ready, kn_cast = sem("kn_ready"), sem("kn_cast")
        kst_ready, kst_free = sem("kst_ready"), sem("kst_free")
        kt_full, kt_free = [sem("kt_full_a"), sem("kt_full_b")], [sem("kt_free_a"), sem("kt_free_b")]
        qn_ready, qt_ready = sem("qn_ready"), sem("qt_ready")
        mx_full, mx_free = sem("mx_full"), sem("mx_free")
        st_full, p_ready, pv_done, pvs_ready = sem("st_full"), sem("p_ready"), sem("pv_done"), sem("pvs_ready")
        s_full, s_masked, sp_ready = sem("s_full"), sem("s_masked"), sem("sp_ready")
        pt_full, pt_ready, spv_done = sem("pt_full"), sem("pt_ready"), sem("spv_done")
        proj_ps, proj_used = sem("proj_ps"), sem("proj_used")
        mod_ps, mod_sb = sem("mod_ps"), sem("mod_sb")
        gu_ps, silu_ready, inter_ready, down_ps = sem("gu_ps"), sem("silu_ready"), sem("inter_ready"), sem("down_ps")
        sum_ps, sum_sb = sem("sum_ps"), sem("sum_sb")
        gate_ready = sem("gate_ready")
        route_ps, route_exp, wt_ready = sem("route_ps"), sem("route_exp"), sem("wt_ready")
        wc_in = [sem("wc_in_a"), sem("wc_in_b")]
        mlp_ps, attn_ps, v_ps, gate_w, route_in = sem("mlp_ps"), sem("attn_ps"), sem("v_ps"), sem("gate_w"), sem("route_in")
        fm_exp, fm_in, km_ready, ks_ps = sem("fm_exp"), sem("fm_in"), sem("km_ready"), sem("ks_ps")
        gate_in, dec_in = sem("gate_in"), sem("dec_in")
        out_done = sem("out_done")
        settled = sem("settled")

        X = sbuf(top, "X", [P, NB, 2, D])
        identb = sbuf(top, "identb", [P, P], BF16)
        cst = sbuf(top, "cst", [P, NCST])
        z = sbuf(top, "z", [P, 2, D])
        zT = sbuf(top, "zT", [P, 2, S])
        onat = sbuf(top, "onat", [P, 2, D])
        oT = sbuf(top, "oT", [P, 2, S])
        st6 = sbuf(top, "st6", [P, 2, 6])
        mv = sbuf(top, "mv", [P, 2, 2])
        std = sbuf(top, "std", [P, 2])
        rstd = sbuf(top, "rstd", [P, 2])
        cw = sbuf(top, "cw", [P, NB, 2])
        cwb = sbuf(top, "cwb", [P, 2])
        csum = sbuf(top, "csum", [P, 1])
        PS = top.enter_context(nc.psum_tensor("PS", [P, 8, 512], F32))
        ARENA_COLS = 47900
        arena = sbuf(top, "arena", [P, ARENA_COLS])
        ident = cst[:, C_IDENT:C_IDENT + P]
        eps5, eps6 = cst[:, C_EPS5:C_EPS5 + 1], cst[:, C_EPS6:C_EPS6 + 1]

        class Arena:

            def __init__(self):
                self.at = 0

            def cut(self, shape, dt=F32):
                n = int(np.prod(shape)) // (1 if dt == F32 else 2)
                a = arena[:, self.at:self.at + n]
                self.at += n
                assert self.at <= ARENA_COLS, (self.at, ARENA_COLS)
                if dt != F32:
                    a = a.bitcast(dt)
                if len(shape) > 1:
                    names = "abcd"[:len(shape)]
                    a = a.rearrange(f"p ({' '.join(names)}) -> p {' '.join(names)}", **dict(zip(names, shape)))
                return a

        def bank(i):
            return PS[:, i, :]

        def bank16(i):
            return PS[:, i, :].bitcast(BF16)

        def link(w, ins):
            s = {"act": act_step, "dve": dve_step, "pool": pool_step}[w.tag]
            ins.then_inc(s, 1)
            w.eng.wait_ge(s, w.up(s))

        def spread(ap, axis, n):
            a = ap.unsqueeze(axis)
            shape = list(a.shape)
            shape[axis] = n
            return a.broadcast_to(shape)

        def ln_dve(w, b, dst=None, src=None):
            dst = z if dst is None else dst
            src = X[:, b, :, :] if src is None else src
            for i in range(2):
                link(w, nc.vector.bn_stats(st6[:, i, :], src[:, i, :]))
            w.settle(settled)
            link(w, nc.vector.bn_aggr(mv[:, 0, :], st6[:, 0, :]))
            w.settle(settled)
            nc.vector.bn_aggr(mv[:, 1, :], st6[:, 1, :]).then_inc(ln_var, 1)
            nc.vector.wait_ge(ln_std, w.up(ln_std))
            link(w, nc.vector.reciprocal(rstd[:, :], std[:, :]))
            for i in range(2):
                link(w, nc.vector.tensor_scalar(dst[:, i, :], src[:, i, :], mv[:, i, 0:1], rstd[:, i:i + 1],
                                                ALU.subtract, ALU.mult))

        def ln_act(w):
            nc.scalar.wait_ge(ln_var, w.up(ln_var))
            nc.scalar.activation(std[:, :], mv[:, :, 1], ACT.Sqrt, bias=eps5).then_inc(ln_std, 1)

        def t2_pe(w, src):
            nc.tensor.wait_ge(t2_in, w.up(t2_in))
            nc.tensor.wait_ge(tr_free, w.up(tr_free))
            for c in range(2):
                for i in range(2):
                    ins = nc.tensor.transpose(bank(7)[:, c * 256 + i * P:c * 256 + (i + 1) * P],
                                              src[:, i, c * P:(c + 1) * P], ident)
            ins.then_inc(tr_full, 1)

        def t2_act(w, dst):
            nc.scalar.wait_ge(tr_full, w.up(tr_full))
            nc.scalar.activation(dst, bank(7).rearrange("p (c t) -> p c t", c=2), ACT.Copy).then_inc(t2_out, 1)
            nc.scalar.wait_ge(t2_out, w.up(t2_out))
            nc.scalar.sem_inc(tr_free, 1)

        def skip_tr(w, n=1):
            w.skip(tr_full, n)

        def proj_nat(lhsT, rhs, ps, last=None):
            for i in range(2):
                for c in range(2):
                    ins = nc.tensor.matmul(ps[:, i * 256:(i + 1) * 256], lhsT[:, c, i * P:(i + 1) * P],
                                           rhs[:, c, 0:256], start=(c == 0), stop=(c == 1))
            return ins

        def split_q(w, q, r, QNv, H, e):
            for i in range(2):
                blocks = QNv[:, i, :, 0:6 * e].rearrange("p h (j e) -> p h j e", j=6)
                qh = q[:, i, :].rearrange("p (h e) -> p h e", h=H)
                rh = r[:, i, :].rearrange("p (h e) -> p h e", h=H)
                link(w, nc.vector.tensor_copy(blocks[:, :, 0, :], qh))
                nc.vector.tensor_copy(blocks[:, :, 3, :], qh)
                nc.vector.tensor_copy(blocks[:, :, 5, :], qh)
                link(w, nc.vector.tensor_tensor(rh, qh, blocks[:, :, 0, :], ALU.subtract))
                link(w, nc.vector.tensor_copy(blocks[:, :, 1, :], rh))
                nc.vector.tensor_copy(blocks[:, :, 4, :], rh)
                link(w, nc.vector.tensor_tensor(blocks[:, :, 2, :], rh, blocks[:, :, 1, :], ALU.subtract))

        def split_k_act(w, kn, KNv, n, H, e):
            for j in range(3):
                ins = nc.scalar.activation(KNv[:n, :, j * e:(j + 1) * e], kn[:n, :].rearrange("p (h e) -> p h e", h=H), ACT.Copy)
            ins.then_inc(kn_cast, 1)

        def split_k_dve(w, kn, r, KNv, n, H, e):
            kh = kn[:n, :].rearrange("p (h e) -> p h e", h=H)
            rh = r[:n, :].rearrange("p (h e) -> p h e", h=H)
            link(w, nc.vector.tensor_tensor(rh, kh, KNv[:n, :, 0:e], ALU.subtract))
            link(w, nc.vector.tensor_copy(KNv[:n, :, 3 * e:4 * e], rh))
            nc.vector.tensor_copy(KNv[:n, :, 4 * e:5 * e], rh)
            return nc.vector.tensor_tensor(KNv[:n, :, 5 * e:6 * e], rh, KNv[:n, :, 3 * e:4 * e], ALU.subtract)

        def q_stack_pe(w, QN, slots, quads):
            for g in quads:
                nc.tensor.wait_ge(tr_free, w.up(tr_free))
                for s in range(slots):
                    for i in range(2):
                        ins = nc.tensor.transpose(bank16(7)[:, s * 256 + i * P:s * 256 + (i + 1) * P],
                                                  QN[:, i, g * slots + s, :], identb[:, :])
                ins.then_inc(tr_full, 1)

        def q_stack_act(w, dst, slots, done):
            nc.scalar.wait_ge(tr_full, w.up(tr_full))
            src = bank16(7)[:, 0:slots * 256].rearrange("p (s t) -> p s t", s=slots)
            if slots == 4:
                nc.scalar.activation(dst, src, ACT.Copy).then_inc(done, 1)
            else:
                nc.scalar.activation(dst[0:64, 0:4:2, :], src[0:64], ACT.Copy)
                nc.scalar.activation(dst[64:P, 1:4:2, :], src[64:P], ACT.Copy).then_inc(done, 1)
            nc.scalar.wait_ge(done, w.up(done))
            nc.scalar.sem_inc(tr_free, 1)

        class Ctx:

            def __init__(self, a, e, tiles, spans):
                self.e, self.H, self.tiles, self.spans = e, D // e, tiles, spans
                self.slots = 4 if e == 16 else 2
                self.quads = self.H // 4
                self.kinds = 2 if e == 16 else 1
                self.turn = 10
                self.plan = [3, 2, 3, 2, 2, 3, 2, 3, 2, 3] + ([1, 3, 3] if len(tiles) == 13 else [1, 1, 2, 3])
                self.lead = sum(self.plan[self.turn:])
                self.kT = a.cut([16, CTX], BF16)
                self.V = a.cut([len(tiles), self.H, e + 1])
                self.KN = [a.cut([16, P], BF16) for _ in range(2)]
                self.QN = a.cut([2, 16, P], BF16)
                self.QT = a.cut([self.H, S], BF16)
                self.QTm = [a.cut([4, S], BF16) for _ in range(2)]
                self.p = [a.cut([4 * S]) for _ in range(2)]
                self.pvs = a.cut([512])
                self.kn = [a.cut([D]) for _ in range(2)]
                self.r = a.cut([D])
                self.q = a.cut([2, D])
                self.qr = a.cut([2, D])
                self.mpart = a.cut([2, 4, 4])
                self.nm = a.cut([2, 4, self.kinds])
                self.nr = a.cut([2, 4, self.kinds])
                self.rec = a.cut([2 * self.kinds, 4])
                self.tmp = a.cut([2 * self.kinds, 4, e])
                wdt = 2048 // self.H
                self.KNv = [k.rearrange("p s (g c) -> p (s g) c", c=wdt) for k in self.KN]
                self.QNv = self.QN.rearrange("p i s (g c) -> p i (s g) c", c=wdt)

        def keys_pe(w, cx, ctxT, wkv, stacks=False):
            nc.tensor.wait_ge(ctx_in, w.up(ctx_in, 16))
            for t, (k0, n) in enumerate(cx.tiles):
                nc.tensor.wait_ge(kv_free, w.up(kv_free))
                for c in range(2):
                    ins = nc.tensor.matmul(bank(t % 3)[:n, :], ctxT[:, c, k0:k0 + n], wkv(t)[:, c, :],
                                           start=(c == 0), stop=(c == 1))
                ins.then_inc(kv_ps, 1)
                if stacks and t:
                    key_stacks_pe(w, cx, [t - 1])
            if stacks:
                key_stacks_pe(w, cx, [len(cx.tiles) - 1])

        def key_stacks_pe(w, cx, which=None):
            for t in range(len(cx.tiles)) if which is None else which:
                k0, n = cx.tiles[t]
                nc.tensor.wait_ge(kst_ready, w.up(kst_ready))
                for half in range(2):
                    nc.tensor.wait_ge(kt_free[half], w.up(kt_free[half]))
                    if n < P:
                        w.settle(settled)
                    for s in range(8):
                        ins = nc.tensor.transpose(bank16(4 + half)[:, s * P:s * P + n],
                                                  cx.KN[t % 2][:n, half * 8 + s, :], identb[:n, :n])
                    ins.then_inc(kt_full[half], 1)

        def key_stack_out(w, copy, cx, t, half):
            k0, n = cx.tiles[t]
            w.eng.wait_ge(kt_full[half], w.up(kt_full[half]))
            src = bank16(4 + half).rearrange("p (s t) -> p s t", s=8)[:, :, 0:n]
            copy(cx.kT[:, half * 8:half * 8 + 8, k0:k0 + n], src).then_inc(kt_free[half], 1)

        def act_copy(dst, src):
            return nc.scalar.activation(dst, src, ACT.Copy)

        def keys_act(w, cx, kn_of):
            for t, (k0, n) in enumerate(cx.tiles):
                nc.scalar.wait_ge(kn_ready, w.up(kn_ready))
                if t >= 2:
                    nc.scalar.wait_ge(kt_full[1], w.up(kt_full[1]))
                split_k_act(w, kn_of(t), cx.KNv[t % 2], n, cx.H, cx.e)
                if t:
                    key_stack_out(w, act_copy, cx, t - 1, 0)
            key_stack_out(w, act_copy, cx, len(cx.tiles) - 1, 0)
            w.skip(kt_full[1], 2)

        def keys_dve(w, cx, make, kn_of, tail=None):
            for t, (k0, n) in enumerate(cx.tiles):
                make(t)
                nc.vector.wait_ge(kn_cast, w.up(kn_cast))
                if tail:
                    tail(t)
                split_k_dve(w, kn_of(t), cx.r, cx.KNv[t % 2], n, cx.H, cx.e).then_inc(kst_ready, 1)
                if t:
                    key_stack_out(w, nc.vector.tensor_copy, cx, t - 1, 1)
                nc.vector.wait_ge(kst_ready, w.up(kst_ready))
            key_stack_out(w, nc.vector.tensor_copy, cx, len(cx.tiles) - 1, 1)

        def att_pe(w, cx, first=True):
            nt = len(cx.tiles)

            def max_chunks(g):
                for i in range(2):
                    for h in range(4):
                        for k0, n in cx.spans:
                            yield g, i, h, k0, n

            chunks = [c for g in range(cx.quads) for c in max_chunks(g)]

            def max_passes(n):
                for chunk in chunks[:n]:
                    max_pass(chunk)
                del chunks[:n]

            count = [0]

            def max_pass(chunk):
                g, i, h, k0, n = chunk
                nc.tensor.wait_ge(mx_free, w.up(mx_free))
                head = 4 * g + h
                slot = head * 16 // cx.H
                nc.tensor.matmul(bank(4 + count[0] % 2)[:, 0:n], cx.QT[:, head, i * P:(i + 1) * P],
                                 cx.kT[:, slot, k0:k0 + n], start=True, stop=True).then_inc(mx_full, 1)
                count[0] += 1

            def scores(g, kt):
                k0, n = cx.tiles[kt]
                e = g * nt + kt
                for s in range(cx.slots):
                    wd = 1024 // cx.slots
                    col = s * wd
                    nh = 4 // cx.slots
                    ins = nc.tensor.matmul(PS[:n, 2 * (e % 2) + col // 512, col % 512:col % 512 + wd],
                                           cx.kT[:, g * cx.slots + s, k0:k0 + n],
                                           cx.QTm[g % 2][:, s * nh:(s + 1) * nh, :],
                                           start=True, stop=True)
                ins.then_inc(st_full, 1)

            def values(g, kt):
                k0, n = cx.tiles[kt]
                e = g * nt + kt
                nc.tensor.wait_ge(p_ready, w.up(p_ready))
                if n < P:
                    w.settle(settled)
                first, last = (0, 3) if cx.kinds == 2 and kt < 3 else (3 if cx.kinds == 2 else 0, nt)
                ty = 1 if cx.kinds == 2 and kt >= 3 else 0
                off = ty * 256 if cx.kinds == 2 else (g % 2) * 256
                for h in range(4):
                    ins = nc.tensor.matmul(bank(6)[32 * h:32 * h + cx.e + 1, off:off + 256],
                                           cx.V[:n, kt, 4 * g + h, :], cx.p[e % 2][:n, h * S:(h + 1) * S],
                                           start=(kt == first), stop=(kt == last - 1),
                                           tile_position=(0, 32 * h))
                ins.then_inc(pv_done, 1)

            def out_transposes(g):
                nc.tensor.wait_ge(tr_free, w.up(tr_free))
                off = 0 if cx.kinds == 2 else (g % 2) * 256
                for u in range(2 * cx.kinds):
                    ins = nc.tensor.transpose(bank(7)[:, u * P:(u + 1) * P],
                                              cx.pvs[:, off + u * P:off + (u + 1) * P], ident)
                ins.then_inc(tr_full, 1)

            def maxima(g):
                nc.tensor.wait_ge(qn_ready, w.up(qn_ready))
                q_stack_pe(w, cx.QN, cx.slots, [g])

            if first:
                nc.tensor.wait_ge(qt_ready, w.up(qt_ready, cx.quads))
            for half in range(2):
                nc.tensor.wait_ge(kt_free[half], w.same(kt_free[half], 1))
            max_passes(32 + cx.lead)
            maxima(0)
            for g in range(cx.quads):
                nc.tensor.wait_ge(qt_ready, w.up(qt_ready))
                for kt in range(nt):
                    scores(g, kt)
                    max_passes(cx.plan[kt] // 2)
                    if kt == 3 and g:
                        out_transposes(g - 1)
                    if kt == cx.turn + 1 and g + 1 < cx.quads:
                        maxima(g + 1)
                    if kt == 1 and g:
                        nc.tensor.wait_ge(pvs_ready, w.up(pvs_ready))
                    if kt:
                        values(g, kt - 1)
                    elif g:
                        values(g - 1, nt - 1)
                    max_passes(cx.plan[kt] - cx.plan[kt] // 2)
            values(cx.quads - 1, nt - 1)
            nc.tensor.wait_ge(pvs_ready, w.up(pvs_ready))
            out_transposes(cx.quads - 1)

        def att_act(w, cx):
            nt = len(cx.tiles)
            q_stack_act(w, cx.QTm[0], cx.slots, qt_ready)
            for g in range(cx.quads):
                for kt in range(nt):
                    k0, n = cx.tiles[kt]
                    e = g * nt + kt
                    nc.scalar.wait_ge(st_full, w.up(st_full))
                    nc.scalar.wait_ge(pv_done, w.up(pv_done))
                    nc.scalar.activation(cx.p[e % 2][:n, :], PS[:n, 2 * (e % 2):2 * (e % 2) + 2, :].rearrange("p a b -> p (a b)"),
                                         ACT.Exp).then_inc(p_ready, 1)
                    if kt == 3 and g:
                        skip_tr(w)
                    if kt == cx.turn + 1 and g + 1 < cx.quads:
                        q_stack_act(w, cx.QTm[(g + 1) % 2], cx.slots, qt_ready)
            skip_tr(w)

        def att_dve(w, cx, finish):
            nt, ns, ty = len(cx.tiles), len(cx.spans), cx.kinds
            count = [0]

            def reduce(i, h, c):
                nc.vector.wait_ge(mx_full, w.up(mx_full))
                n = cx.spans[c][1]
                nc.vector.tensor_reduce(cx.mpart[:, i, h, c:c + 1], bank(4 + count[0] % 2)[:, 0:n],
                                        AX.X, ALU.max).then_inc(mx_free, 1)
                w.skip(mx_free)
                count[0] += 1

            def maxima(g):
                nc.vector.wait_ge(mx_free, w.same(mx_free))
                QNm = cx.QNv[:, :, 4 * g:4 * g + 4, 6 * cx.e:6 * cx.e + 3 * ty].rearrange("p i h (t j) -> p i h t j", t=ty)
                if ty == 2:
                    nc.vector.tensor_scalar(cx.nm[:, :, :, 0], cx.mpart[:, :, :, 0], -1.0, None, ALU.mult)
                    link(w, nc.vector.tensor_reduce(cx.nm[:, :, :, 1], cx.mpart[:, :, :, 1:4], AX.X, ALU.max, negate=True))
                else:
                    link(w, nc.vector.tensor_reduce(cx.nm[:, :, :, 0], cx.mpart[:, :, :, :], AX.X, ALU.max, negate=True))
                for t in range(ty):
                    link(w, nc.vector.tensor_copy(QNm[:, :, :, t, 0], cx.nm[:, :, :, t]))
                    link(w, nc.vector.tensor_tensor(cx.nr[:, :, :, t], cx.nm[:, :, :, t], QNm[:, :, :, t, 0], ALU.subtract))
                    link(w, nc.vector.tensor_copy(QNm[:, :, :, t, 1], cx.nr[:, :, :, t]))
                    last = nc.vector.tensor_tensor(QNm[:, :, :, t, 2], cx.nr[:, :, :, t], QNm[:, :, :, t, 1], ALU.subtract)
                    if t < ty - 1:
                        link(w, last)
                last.then_inc(qn_ready, 1)
                skip_tr(w)

            def evacuate(g):
                off = 0 if ty == 2 else (g % 2) * 256
                nc.vector.wait_ge(pv_done, w.up(pv_done, nt))
                nc.vector.tensor_copy(cx.pvs[:, off:off + 256 * ty], bank(6)[:, off:off + 256 * ty]).then_inc(pvs_ready, 1)

            def outputs(g):
                nc.vector.wait_ge(tr_full, w.up(tr_full))
                u = bank(7)[:, 0:256 * ty].rearrange("p (u h e) -> p u h e", u=2 * ty, h=4)
                link(w, nc.vector.reciprocal(cx.rec[:, :, :], u[:, :, :, cx.e]))
                finish(w, cx, g, u)
                nc.vector.sem_inc(tr_free, 1)

            parts = [(g, i, h, c) for g in range(cx.quads) for i in range(2) for h in range(4) for c in range(ns)]
            whole = 8 * ns

            def reduces(n):
                for g, i, h, c in parts[:n]:
                    reduce(i, h, c)
                    if (i, h, c) == (1, 3, ns - 1):
                        maxima(g)
                del parts[:n]

            reduces(whole + cx.lead)
            for g in range(cx.quads):
                for kt in range(nt):
                    if kt == 1 and g:
                        evacuate(g - 1)
                    reduces(cx.plan[kt])
                    if kt == 3 and g:
                        outputs(g - 1)
            evacuate(cx.quads - 1)
            outputs(cx.quads - 1)

        class Self:

            def __init__(self, a, e, cx=None):
                self.e, self.H, self.tiles = e, D // e, [(0, P), (P, P)]
                self.slots, self.quads, self.kinds = (4 if e == 16 else 2), D // e // 4, 1
                self.kT = a.cut([16, S], BF16)
                self.V = a.cut([2, self.H, e + 1])
                self.s = [a.cut([2, S]) for _ in range(3)]
                self.pT = [a.cut([2, S]) for _ in range(2)]
                self.nm = a.cut([3, 2])
                self.sm = a.cut([3, 2])
                if cx is None:
                    self.KN = [a.cut([16, P], BF16) for _ in range(2)]
                    self.QN = a.cut([2, 16, P], BF16)
                    self.QT = a.cut([self.H, S], BF16)
                    self.p = [a.cut([2 * S]) for _ in range(2)]
                    self.pvs, self.r = a.cut([512]), a.cut([D])
                    self.q, self.qr = a.cut([2, D]), a.cut([2, D])
                    self.rec, self.tmp = a.cut([2, 4]), a.cut([2, 4, e])
                else:
                    self.KN, self.QN, self.QT, self.pvs, self.r, self.q, self.qr = cx.KN, cx.QN, cx.QT, cx.pvs, cx.r, cx.q, cx.qr
                    self.rec, self.tmp = cx.rec, cx.tmp
                    self.p = [x[:, 0:512] for x in cx.p]
                wdt = 2048 // self.H
                self.KNv = [k.rearrange("p s (g c) -> p (s g) c", c=wdt) for k in self.KN]
                self.QNv = self.QN.rearrange("p i s (g c) -> p i (s g) c", c=wdt)

        def self_pe(w, sx):
            def scores(u):
                for i in range(2):
                    ins = nc.tensor.matmul(bank((0, 1, 4)[u % 3])[:, i * 256:(i + 1) * 256], sx.QT[:, u, i * P:(i + 1) * P],
                                           sx.kT[:, u * 16 // sx.H, :], start=True, stop=True)
                ins.then_inc(s_full, 1)

            def probs(u):
                nc.tensor.wait_ge(sp_ready, w.up(sp_ready))
                for k in range(2):
                    for i in range(2):
                        ins = nc.tensor.transpose(bank(2 + u % 2)[:, k * 256 + i * P:k * 256 + (i + 1) * P],
                                                  sx.p[u % 2][:, i * 256 + k * P:i * 256 + (k + 1) * P], ident)
                ins.then_inc(pt_full, 1)

            def values(u):
                nc.tensor.wait_ge(pt_ready, w.up(pt_ready))
                h, g = u % 4, u // 4
                for k in range(2):
                    ins = nc.tensor.matmul(bank(6)[32 * h:32 * h + sx.e + 1, (g % 2) * 256:(g % 2) * 256 + 256],
                                           sx.V[:, k, u, :], sx.pT[u % 2][:, k, :], start=(k == 0), stop=(k == 1),
                                           tile_position=(0, 32 * h))
                ins.then_inc(spv_done, 1)

            def out_transposes(g):
                nc.tensor.wait_ge(tr_free, w.up(tr_free))
                for i in range(2):
                    ins = nc.tensor.transpose(bank(7)[:, i * P:(i + 1) * P],
                                              sx.pvs[:, (g % 2) * 256 + i * P:(g % 2) * 256 + (i + 1) * P], ident)
                ins.then_inc(tr_full, 1)

            nc.tensor.wait_ge(qt_ready, w.up(qt_ready, sx.quads))
            for half in range(2):
                nc.tensor.wait_ge(kt_free[half], w.same(kt_free[half], 1))
            for u in range(sx.H + 4):
                if u < sx.H:
                    scores(u)
                if 2 <= u <= sx.H + 1:
                    probs(u - 2)
                if u % 4 == 3 and u >= 7:
                    nc.tensor.wait_ge(pvs_ready, w.up(pvs_ready))
                if 3 <= u <= sx.H + 2:
                    values(u - 3)
                if u % 4 == 3 and u >= 7:
                    out_transposes((u - 7) // 4)

        def self_act(w, sx):
            def copy(u):
                nc.scalar.wait_ge(pt_full, w.up(pt_full))
                nc.scalar.wait_ge(spv_done, w.up(spv_done))
                nc.scalar.activation(sx.pT[u % 2], bank(2 + u % 2).rearrange("p (k t) -> p k t", k=2),
                                     ACT.Copy).then_inc(pt_ready, 1)

            for u in range(sx.H + 1):
                if u < sx.H:
                    nc.scalar.wait_ge(s_masked, w.up(s_masked))
                    for i in range(2):
                        ins = nc.scalar.activation(sx.p[u % 2][:, i * 256:(i + 1) * 256], sx.s[u % 3][:, i, :], ACT.Exp,
                                                   bias=sx.nm[:, u % 3, i:i + 1])
                    ins.then_inc(sp_ready, 1)
                if u:
                    copy(u - 1)
            w.skip(tr_full, sx.quads)

        def self_dve(w, sx, mask, finish):
            def masked(u):
                nc.vector.wait_ge(s_full, w.up(s_full))
                if u >= 3:
                    nc.vector.wait_ge(sp_ready, w.up(sp_ready))
                for i in range(2):
                    w.settle(settled)
                    link(w, nc.vector.tensor_tensor_reduce(
                        out=sx.s[u % 3][:, i, :], in0=bank((0, 1, 4)[u % 3])[:, i * 256:(i + 1) * 256], in1=mask[:, i, :],
                        scale=1.0, scalar=LOWEST, op0=ALU.add, op1=ALU.max, accum_out=sx.sm[:, u % 3, i:i + 1]))
                nc.vector.tensor_scalar(sx.nm[:, u % 3, :], sx.sm[:, u % 3, :], -1.0, None, ALU.mult).then_inc(s_masked, 1)

            for u in range(sx.H + 4):
                if u < sx.H:
                    masked(u)
                if u >= 6 and u % 4 == 2:
                    g = (u - 6) // 4
                    nc.vector.wait_ge(spv_done, w.up(spv_done, 4))
                    nc.vector.tensor_copy(sx.pvs[:, (g % 2) * 256:(g % 2) * 256 + 256],
                                          bank(6)[:, (g % 2) * 256:(g % 2) * 256 + 256]).then_inc(pvs_ready, 1)
                if u >= 7 and u % 4 == 3:
                    g = (u - 7) // 4
                    nc.vector.wait_ge(tr_full, w.up(tr_full))
                    v = bank(7)[:, 0:256].rearrange("p (u h e) -> p u h e", u=2, h=4)
                    link(w, nc.vector.reciprocal(sx.rec[:, 0:2, :], v[:, :, :, sx.e]))
                    finish(w, sx, g, v)
                    nc.vector.sem_inc(tr_free, 1)
            w.skip(sp_ready, 3)

        def vec(a, n):
            return a.cut([n, D])

        a = Arena()
        x0 = Ctx(a, 16, L0_TILES, L0_SPANS)
        x0_ctxT = a.cut([2, CTX])
        x0_w = a.cut([2, 6 * 256])
        x0_v = vec(a, 9)
        x0_kraw = a.cut([14, D])
        x0_ss, x0_std, x0_rk = a.cut([16]), a.cut([16]), a.cut([16])
        x0_tail = a.cut([14, 7])
        x0_len = a.cut([1])
        x0_flag = a.cut([2])
        x0_junk = x0_kraw[:, 0, :]
        x0_sq = a.cut([D])
        x0_wts = a.cut([CTX])
        x0_junk2 = x0.kT.rearrange("p s t -> p (s t)")[:, 0:2 * CTX].bitcast(F32)
        x0_dec = a.cut([2])

        def x0_wkv(t):
            return x0_w[:, :, 256:768] if t >= 3 else x0_w[:, :, 768:1280]

        def x0_sp(sp, w):
            sp.dma_start(x0_dec[:, 0:1], d["decay"].partition_broadcast(P)).then_inc(dec_in, 16)
            sp.dma_start(x0_len.bitcast(I32), d["lens"].partition_broadcast(P)).then_inc(w_in, 16)
            sp.dma_start(x0_w[:, :, :], d["w_x0"]).then_inc(w_in, 16)
            sp.dma_start(x0_v.rearrange("p n d -> p (n d)"), d["v_x0"].partition_broadcast(P)).then_inc(w_in, 16)
            for b in w.loop(NB, "x0"):
                sp.wait_ge(ctx_used, w.up(ctx_used))
                sp.dma_start(x0_ctxT[:, :, :], d["ctxT"][b]).then_inc(ctx_in, 16)

        def x0_pe(w):
            nc.tensor.wait_ge(w_in, w.up(w_in, 48))
            for b in w.loop(NB, "x0"):
                t2_pe(w, z)
                nc.tensor.wait_ge(t2_out, w.up(t2_out))
                proj_nat(zT, x0_w[:, :, 0:256], bank(3)).then_inc(q_ps, 1)
                keys_pe(w, x0, x0_ctxT, x0_wkv)
                nc.tensor.wait_ge(qn_ready, w.up(qn_ready))
                q_stack_pe(w, x0.QN, x0.slots, range(x0.quads))
                key_stacks_pe(w, x0)
                att_pe(w, x0)
                t2_pe(w, onat)
                nc.tensor.wait_ge(t2_out, w.up(t2_out))
                proj_nat(oT, x0_w[:, :, 1280:1536], bank(0)).then_inc(proj_ps, 1)

        def x0_act(w):
            nc.scalar.wait_ge(dec_in, w.up(dec_in, 16))
            nc.scalar.activation(x0_dec[:, 1:2], x0_dec[:, 0:1], ACT.Exp, scale=-1.0).then_inc(fm_exp, 1)
            for b in w.loop(NB, "x0"):
                ln_act(w)
                t2_act(w, zT)
                nc.scalar.wait_ge(q_sb, w.up(q_sb))
                for i in range(2):
                    link(w, nc.scalar.activation(x0_sq[:, :], x0.q[:, i, :], ACT.Square, accum_out=x0_ss[:, 14 + i:15 + i]))
                for t, (k0, n) in enumerate(x0.tiles):
                    nc.scalar.wait_ge(kraw_ready, w.up(kraw_ready))
                    link(w, nc.scalar.activation(x0_sq[:n, :], x0_kraw[:n, t, :], ACT.Square, accum_out=x0_ss[:n, t:t + 1]))
                nc.scalar.activation(x0_std[:, :], x0_ss[:, :], ACT.Sqrt, bias=eps6, scale=1.0 / D).then_inc(k_std, 1)
                for g in range(x0.quads):
                    q_stack_act(w, x0.QT[:, 4 * g:4 * g + 4, :], x0.slots, qt_ready)
                keys_act(w, x0, lambda t: x0.kn[t % 2])
                att_act(w, x0)
                t2_act(w, oT)

        def x0_start(w):
            nc.vector.wait_ge(w_in, w.up(w_in, 48))
            for buf in x0.KN:
                nc.vector.memset(buf[:, :, :], 0.0)
            nc.vector.memset(x0.QN[:, :, :, :], 0.0)
            nc.vector.memset(x0_ss[:, :], 1.0)
            nc.vector.memset(x0.V[:, :, :, 16:17], 1.0)
            link(w, nc.vector.memset(bank(6), 0.0))
            nc.vector.memset(x0.QN[:, :, :, 102:103], 1.0)
            link(w, nc.vector.tensor_copy(x0_flag[:, 0:1], x0_len.bitcast(I32)))
            link(w, nc.vector.tensor_scalar(x0_flag[:, 1:2], x0_flag[:, 0:1], 0.0, None, ALU.is_gt))
            link(w, nc.vector.tensor_copy(x0_tail[:, :, :], cst[:, C_TAIL:C_TAIL + 98].rearrange("p (t j) -> p t j", t=14)))
            link(w, nc.vector.tensor_scalar(x0_tail[:, 3:14, 6], cst[:, C_KEY:C_KEY + 11], x0_flag[:, 0:1], -BIG,
                                            ALU.is_ge, ALU.mult))
            link(w, nc.vector.tensor_scalar(x0_tail[:, 3:14, 6], x0_tail[:, 3:14, 6], x0_flag[:, 1:2], None, ALU.mult))
            nc.vector.tensor_scalar(x0_v[:, 3, :], x0_v[:, 3, :], x0_flag[:, 1:2], None, ALU.mult)
            nc.vector.tensor_scalar(x0_v[:, 1, :], x0_v[:, 1, :], 0.25, None, ALU.mult)
            nc.vector.wait_ge(fm_exp, w.up(fm_exp))
            link(w, nc.vector.tensor_scalar(x0_dec[:, 0:1], x0_dec[:, 1:2], 1.0, None, ALU.add))
            link(w, nc.vector.reciprocal(x0_dec[:, 1:2], x0_dec[:, 0:1]))
            decay_row = x0_junk2[:, 0:CTX]
            ones_row = x0_kraw.rearrange("p t d -> p (t d)")[:, 0:CTX]
            nc.vector.memset(ones_row, 1.0)
            link(w, nc.vector.memset(decay_row, 0.0))
            link(w, nc.vector.tensor_scalar(decay_row, decay_row, x0_dec[:, 1:2], None, ALU.add))
            link(w, nc.vector.tensor_tensor_scan(x0_wts[:, ::-1], decay_row, ones_row, 0.0, ALU.mult, ALU.add))
            link(w, nc.vector.tensor_reduce(csum[:, :], x0_wts[:, :], AX.X, ALU.add))

        def x0_finish(w, cx, g, u):
            link(w, nc.vector.tensor_tensor(cx.tmp[:, :, :, :], u[:, :, :, 0:16], spread(cx.rec[:, :, :], 3, 16), ALU.mult))
            t = cx.tmp.rearrange("p u h e -> p u (h e)")
            link(w, nc.vector.tensor_tensor(onat[:, :, g * 64:(g + 1) * 64], t[:, 0:2, :], t[:, 2:4, :], ALU.add))

        def x0_dve(w):
            x0_start(w)
            for b in w.loop(NB, "x0"):
                ln_dve(w, b)
                nc.vector.sem_inc(t2_in, 1)
                w.skip(tr_full)
                nc.vector.wait_ge(q_ps, w.up(q_ps))
                nc.vector.tensor_tensor(x0.q[:, :, :], bank(3).rearrange("p (i d) -> p i d", i=2),
                                        spread(x0_v[:, 0, :], 1, 2), ALU.add).then_inc(q_sb, 1)
                for t, (k0, n) in enumerate(x0.tiles):
                    bk, bv = (2, 4) if t >= 3 else (5, 7)
                    nc.vector.wait_ge(kv_ps, w.up(kv_ps))
                    nc.vector.tensor_tensor(x0_kraw[:n, t, :], bank(t % 3)[:n, 0:256], x0_v[:n, bk, :], ALU.add).then_inc(kraw_ready, 1)
                    nc.vector.tensor_tensor(x0.V[:n, t, :, 0:16], bank(t % 3)[:n, 256:512].rearrange("p (h e) -> p h e", h=16),
                                            x0_v[:n, bv, :].rearrange("p (h e) -> p h e", h=16), ALU.add).then_inc(kv_free, 1)
                nc.vector.wait_ge(k_std, w.up(k_std))
                link(w, nc.vector.reciprocal(x0_rk[:, :], x0_std[:, :]))
                for i in range(2):
                    ins = nc.vector.scalar_tensor_tensor(out=x0.q[:, i, :], in0=x0.q[:, i, :], scalar=x0_rk[:, 14 + i:15 + i],
                                                         in1=x0_v[:, 1, :], op0=ALU.mult, op1=ALU.mult)
                link(w, ins)
                link(w, nc.vector.memset(x0.QN[:, :, :, 96:102], 0.0))
                split_q(w, x0.q, x0.qr, x0.QNv, 16, 16)
                nc.vector.sem_inc(qn_ready, 1)
                w.skip(tr_full, x0.quads)

                def make(t):
                    k0, n = x0.tiles[t]
                    nc.vector.scalar_tensor_tensor(out=x0.kn[t % 2][:n, :], in0=x0_kraw[:n, t, :], scalar=x0_rk[:n, t:t + 1],
                                                   in1=x0_v[:n, 3 if t >= 3 else 6, :], op0=ALU.mult, op1=ALU.mult).then_inc(kn_ready, 1)

                def tail(t):
                    n = x0.tiles[t][1]
                    nc.vector.tensor_copy(x0.KN[t % 2][:n, :, 96:103], spread(x0_tail[:n, t, :], 1, 16))

                keys_dve(w, x0, make, lambda t: x0.kn[t % 2], tail)
                for c in range(2):
                    link(w, nc.vector.tensor_tensor_reduce(out=x0_kraw.rearrange("p t d -> p (t d)")[:, 0:CTX], in0=x0_ctxT[:, c, :], in1=x0_wts[:, :],
                                                           scale=1.0, scalar=0.0, op0=ALU.mult, op1=ALU.add,
                                                           accum_out=cwb[:, c:c + 1]))
                nc.vector.tensor_copy(cw[:, b, :], cwb[:, :])
                nc.vector.sem_inc(ctx_used, 1)
                att_dve(w, x0, x0_finish)
                nc.vector.sem_inc(t2_in, 1)
                w.skip(tr_full)
                nc.vector.wait_ge(proj_ps, w.up(proj_ps))
                link(w, nc.vector.tensor_tensor(X[:, b, :, :], X[:, b, :, :], bank(0).rearrange("p (i d) -> p i d", i=2), ALU.add))
                link(w, nc.vector.tensor_tensor(X[:, b, :, :], X[:, b, :, :], spread(x0_v[:, 8, :], 1, 2), ALU.add))
                nc.vector.sem_inc(phase_end, 1)

        a = Arena()
        f0 = Self(a, 16)
        f0_w = a.cut([2, 4 * 256])
        f0_mlp = a.cut([2, 2, 1024])
        f0_down = a.cut([8, D])
        f0_A = a.cut([2, 16])
        f0_B = a.cut([1024])
        f0_v = a.cut([2, D])
        f0_x1, f0_h = a.cut([2, D]), a.cut([2, D])
        f0_xT, f0_hT, f0_aT = a.cut([2, S]), a.cut([2, S]), a.cut([2, S])
        f0_kraw = a.cut([2, D])
        f0_sq = a.cut([D])
        f0_ss, f0_std, f0_rr = a.cut([2]), a.cut([2]), a.cut([2])
        f0_th, f0_mT = a.cut([S]), a.cut([S])
        f0_sg = [a.cut([S]) for _ in range(2)]
        f0_inter = a.cut([8, S])

        def f0_sp(sp, w):
            sp.wait_ge(phase_end, w.up(phase_end, 4))
            for dst, name in ((f0_w, "w_f0"), (f0_mlp, "mlp_f0"), (f0_down, "down_f0"), (f0_A, "A_f0")):
                sp.dma_start(dst, d[name]).then_inc(w_in, 16)
            sp.dma_start(f0_B[0:16, :], d["B_f0"]).then_inc(w_in, 16)
            sp.dma_start(f0_v.rearrange("p n d -> p (n d)"), d["v_f0"].partition_broadcast(P)).then_inc(w_in, 16)

        def f0_pe(w):
            nc.tensor.wait_ge(phase_end, w.up(phase_end, 4))
            nc.tensor.wait_ge(w_in, w.up(w_in, 96))
            for b in w.loop(NB, "f0"):
                t2_pe(w, f0_x1)
                t2_pe(w, f0_h)
                nc.tensor.wait_ge(t2_out, w.up(t2_out, 2))
                proj_nat(f0_xT, f0_w[:, :, 0:256], bank(3)).then_inc(q_ps, 1)
                for j in (1, 2):
                    proj_nat(f0_xT, f0_w[:, :, j * 256:(j + 1) * 256], bank(3 + j)).then_inc(q_ps, 1)
                nc.tensor.wait_ge(qn_ready, w.up(qn_ready))
                q_stack_pe(w, f0.QN, f0.slots, range(f0.quads))
                key_stacks_pe(w, f0)
                self_pe(w, f0)
                t2_pe(w, onat)
                nc.tensor.wait_ge(t2_out, w.up(t2_out))
                for o in range(2):
                    for c in range(2):
                        ins = nc.tensor.matmul(bank(0)[:, o * 256:(o + 1) * 256], f0_w[:, c, 768 + o * P:768 + (o + 1) * P],
                                               oT[:, c, :], start=(c == 0), stop=(c == 1))
                ins.then_inc(attn_ps, 1)
                nc.tensor.wait_ge(mod_sb, w.up(mod_sb))
                for j, src in enumerate((f0_aT, f0_hT)):
                    for c in range(2):
                        ins = nc.tensor.matmul(bank(1)[0:16, j * 256:(j + 1) * 256], f0_A[:, c, :], src[:, c, :],
                                               start=(c == 0), stop=(c == 1))
                ins.then_inc(mod_ps, 1)
                nc.tensor.wait_ge(mod_sb, w.up(mod_sb))
                for f in range(8):
                    if f >= 2:
                        nc.tensor.wait_ge(inter_ready, w.up(inter_ready))
                    gate, up = bank(2 + f % 2)[:, 0:256], bank(2 + f % 2)[:, 256:512]
                    for c in range(2):
                        nc.tensor.matmul(gate, f0_mlp[:, c, 0, f * P:(f + 1) * P], f0_hT[:, c, :], start=(c == 0), stop=False)
                    nc.tensor.matmul(gate, f0_B[0:16, f * P:(f + 1) * P], f0_mT[0:16, :], start=False, stop=True)
                    for c in range(2):
                        ins = nc.tensor.matmul(up, f0_mlp[:, c, 1, f * P:(f + 1) * P], f0_hT[:, c, :], start=(c == 0), stop=(c == 1))
                    ins.then_inc(gu_ps, 1)
                nc.tensor.wait_ge(inter_ready, w.up(inter_ready, 2))
                for i in range(2):
                    for f in range(8):
                        ins = nc.tensor.matmul(bank(0)[:, i * 256:(i + 1) * 256], f0_inter[:, f, i * P:(i + 1) * P], f0_down[:, f, :],
                                               start=(f == 0), stop=(f == 7))
                ins.then_inc(mlp_ps, 1)

        def f0_act(w):
            nc.scalar.wait_ge(phase_end, w.up(phase_end, 4))
            for b in w.loop(NB, "f0"):
                ln_act(w)
                nc.scalar.wait_ge(ln_var, w.up(ln_var))
                nc.scalar.activation(f0_std, f0_ss, ACT.Sqrt, bias=eps6, scale=1.0 / D).then_inc(ln_std, 1)
                t2_act(w, f0_xT)
                t2_act(w, f0_hT)
                for g in range(f0.quads):
                    q_stack_act(w, f0.QT[:, 4 * g:4 * g + 4, :], f0.slots, qt_ready)
                keys_act(w, f0, lambda t: f0_kraw[:, t, :])
                self_act(w, f0)
                t2_act(w, oT)
                nc.scalar.wait_ge(attn_ps, w.up(attn_ps))
                nc.scalar.activation(f0_aT, bank(0).rearrange("p (c t) -> p c t", c=2), ACT.Copy).then_inc(mod_sb, 1)
                nc.scalar.wait_ge(mod_ps, w.up(mod_ps))
                nc.scalar.activation(f0_th[0:16, :], bank(1)[0:16, 0:256], ACT.Tanh).then_inc(silu_ready, 1)
                for f in range(8):
                    nc.scalar.wait_ge(gu_ps, w.up(gu_ps))
                    if f >= 2:
                        nc.scalar.wait_ge(inter_ready, w.up(inter_ready))
                    nc.scalar.activation(f0_sg[f % 2], bank(2 + f % 2)[:, 0:256], ACT.Silu).then_inc(silu_ready, 1)
                w.skip(inter_ready, 2)

        def f0_dve(w):
            for buf in f0.KN:
                nc.vector.memset(buf, 0.0)
            nc.vector.memset(f0.QN, 0.0)
            nc.vector.memset(f0.V[:, :, :, 16:17], 1.0)
            link(w, nc.vector.memset(bank(6), 0.0))
            nc.vector.wait_ge(w_in, w.up(w_in, 96))
            causal = cst[:, C_CAUSAL:C_CAUSAL + 512].rearrange("p (i k) -> p i k", i=2)
            for b in w.loop(NB, "f0"):
                ln_dve(w, b)
                for i in range(2):
                    link(w, nc.vector.tensor_tensor_reduce(out=f0_sq, in0=z[:, i, :], in1=z[:, i, :], scale=1.0, scalar=0.0,
                                                           op0=ALU.mult, op1=ALU.add, accum_out=f0_ss[:, i:i + 1]))
                nc.vector.sem_inc(ln_var, 1)
                nc.vector.wait_ge(ln_std, w.up(ln_std))
                link(w, nc.vector.reciprocal(f0_rr, f0_std))
                for k, dst in enumerate((f0_x1, f0_h)):
                    for i in range(2):
                        link(w, nc.vector.scalar_tensor_tensor(out=dst[:, i, :], in0=z[:, i, :], scalar=f0_rr[:, i:i + 1],
                                                               in1=f0_v[:, k, :], op0=ALU.mult, op1=ALU.mult))
                nc.vector.sem_inc(t2_in, 2)
                w.skip(tr_full, 2)
                nc.vector.wait_ge(q_ps, w.up(q_ps))
                link(w, nc.vector.tensor_scalar(f0.q, bank(3).rearrange("p (i d) -> p i d", i=2), 0.25, None, ALU.mult))
                split_q(w, f0.q, f0.qr, f0.QNv, 16, 16)
                nc.vector.sem_inc(qn_ready, 1)
                w.skip(tr_full, f0.quads)
                nc.vector.wait_ge(q_ps, w.up(q_ps, 2))
                link(w, nc.vector.tensor_copy(f0_kraw, bank(4).rearrange("p (i d) -> p i d", i=2)))
                link(w, nc.vector.tensor_copy(f0.V[:, :, :, 0:16], bank(5).rearrange("p (i h e) -> p i h e", i=2, h=16)))
                keys_dve(w, f0, lambda t: nc.vector.sem_inc(kn_ready, 1), lambda t: f0_kraw[:, t, :])
                self_dve(w, f0, causal, lambda w, sx, g, v: link(w, nc.vector.tensor_tensor(
                    onat[:, :, g * 64:(g + 1) * 64].rearrange("p i (h e) -> p i h e", h=4), v[:, :, :, 0:16],
                    spread(sx.rec, 3, 16), ALU.mult)))
                nc.vector.sem_inc(t2_in, 1)
                w.skip(tr_full)
                nc.vector.wait_ge(mod_ps, w.up(mod_ps))
                nc.vector.wait_ge(silu_ready, w.up(silu_ready))
                nc.vector.scalar_tensor_tensor(out=f0_mT[0:16, :], in0=bank(1)[0:16, 256:512], scalar=0.1, in1=f0_th[0:16, :],
                                               op0=ALU.mult, op1=ALU.mult).then_inc(mod_sb, 1)
                link(w, nc.vector.tensor_tensor(X[:, b, :, :], X[:, b, :, :], z, ALU.add))
                for f in range(8):
                    nc.vector.wait_ge(silu_ready, w.up(silu_ready))
                    nc.vector.tensor_tensor(f0_inter[:, f, :], f0_sg[f % 2], bank(2 + f % 2)[:, 256:512], ALU.mult).then_inc(inter_ready, 1)
                nc.vector.wait_ge(mlp_ps, w.up(mlp_ps))
                link(w, nc.vector.tensor_tensor(X[:, b, :, :], X[:, b, :, :], bank(0).rearrange("p (i d) -> p i d", i=2), ALU.add))
                nc.vector.sem_inc(phase_end, 1)

        a = Arena()
        x1_w = a.cut([2, 2 * D])
        x1_v = a.cut([3, D])
        x1_bin = a.cut([2])
        x1_scs = a.cut([2])
        x1_s = a.cut([2, NB])
        x1_sB = a.cut([2, NB, P])
        x1_y = a.cut([2, D])

        def x1_sp(sp, w):
            sp.wait_ge(phase_end, w.up(phase_end, 4))
            sp.dma_start(x1_w, d["w_x1"]).then_inc(w_in, 16)
            sp.dma_start(x1_v.rearrange("p n d -> p (n d)"), d["v_x1"].partition_broadcast(P)).then_inc(w_in, 16)
            sp.dma_start(x1_bin, d["bin_x1"]).then_inc(w_in, 16)

        def x1_pe(w):
            nc.tensor.wait_ge(phase_end, w.up(phase_end, 4))
            nc.tensor.wait_ge(w_in, w.up(w_in, 48))
            for o in range(2):
                for c in range(2):
                    ins = nc.tensor.matmul(bank(0)[:, o * NB:(o + 1) * NB], x1_w[:, c, o * P:(o + 1) * P], cw[:, :, c],
                                           start=(c == 0), stop=(c == 1))
            ins.then_inc(sum_ps, 1)
            nc.tensor.wait_ge(sum_sb, w.up(sum_sb))
            for b in range(NB):
                for c in range(2):
                    ins = nc.tensor.matmul(bank(1 + b // 2)[:, b % 2 * 256:b % 2 * 256 + 256], x1_sB[:, c, b, :], x1_w[:, c, D:2 * D],
                                           start=(c == 0), stop=(c == 1))
            ins.then_inc(sum_ps, 1)

        def x1_act(w):
            nc.scalar.wait_ge(phase_end, w.up(phase_end, 4))
            for b in w.loop(NB, "x1"):
                ln_act(w)
                ln_act(w)

        def x1_dve(w):
            nc.vector.wait_ge(w_in, w.up(w_in, 48))
            nc.vector.wait_ge(sum_ps, w.up(sum_ps))
            link(w, nc.vector.tensor_scalar(x1_scs, x1_bin, csum[:, 0:1], None, ALU.mult))
            for o in range(2):
                link(w, nc.vector.tensor_scalar(x1_s[:, o, :], bank(0)[:, o * NB:(o + 1) * NB], x1_scs[:, o:o + 1], 1.0 / CTX,
                                                ALU.add, ALU.mult))
            nc.vector.tensor_copy(x1_sB, spread(x1_s, 3, P)).then_inc(sum_sb, 1)
            nc.vector.wait_ge(sum_ps, w.up(sum_ps))
            for b in w.loop(NB, "x1"):
                ln_dve(w, b)
                link(w, nc.vector.tensor_tensor(x1_y, z, spread(PS[:, 1:3, :].rearrange("p a (b d) -> p (a b) d", b=2)[:, b, :], 1, 2), ALU.add))
                link(w, nc.vector.tensor_tensor(x1_y, x1_y, spread(x1_v[:, 0, :], 1, 2), ALU.add))
                ln_dve(w, b, dst=z, src=x1_y)
                link(w, nc.vector.tensor_tensor(z, z, spread(x1_v[:, 1, :], 1, 2), ALU.mult))
                link(w, nc.vector.tensor_tensor(z, z, spread(x1_v[:, 2, :], 1, 2), ALU.add))
                link(w, nc.vector.tensor_tensor(X[:, b, :, :], X[:, b, :, :], z, ALU.add))
                nc.vector.sem_inc(phase_end, 1)

        class Experts:

            def __init__(self, name):
                self.name = name
                self.up, self.chunks, self.E = FFNS[name]
                a = Arena()
                self.hT = a.cut([2, NB, S])
                self.slot = [a.cut([7, P]) for _ in range(2)]
                self.router = a.cut([2, self.E])
                self.WT = a.cut([NB, S])
                self.W = a.cut([2, self.E])
                self.bias = a.cut([16])
                n = 64 if name == "f1" else 18
                self.lg, self.ex, self.mr, self.sel = (a.cut([2, n]) for _ in range(4))
                self.m8 = a.cut([2, 8])
                self.nm, self.ws, self.rs = a.cut([2]), a.cut([2]), a.cut([2])
                self.gp, self.gr, self.g8 = a.cut([2, 10]), a.cut([2, 10]), a.cut([2, 8])
                self.pr = a.cut([2, 8, 2])
                self.sg = [a.cut([512]) for _ in range(2)]
                self.su = a.cut([512])
                self.inter = [a.cut([512]) for _ in range(2)]
                self.zeros = a.cut([512], BF16)

        def ffn_sp(sp, w, f):
            sp.wait_ge(phase_end, w.up(phase_end, 4))
            sp.dma_start(f.router, d["router_" + f.name]).then_inc(w_in, 16)
            if f.name == "f3":
                sp.dma_start(f.bias, d["bias_f3"].partition_broadcast(P)).then_inc(w_in, 16)
            src = d["chunks_" + f.name]
            for c in range(2):
                sp.dma_start(f.slot[c], src[c]).then_inc(wc_in[c], 16)
            sp.wait_ge(down_ps, w.up(down_ps, 2))
            sp.dma_start(f.slot[0], src[2]).then_inc(wc_in[0], 16)
            for j in w.loop((f.chunks - 3) // 2, f.name + "w"):
                for k in range(2):
                    sp.wait_ge(down_ps, w.up(down_ps, 2))
                    sp.dma_start(f.slot[1 - k], src[2 * j + 3 + k]).then_inc(wc_in[1 - k], 16)
            w.skip(down_ps, 4)

        def ffn_pe(w, f):
            nc.tensor.wait_ge(phase_end, w.up(phase_end, 4))
            nc.tensor.wait_ge(w_in, w.up(w_in, 32 if f.name == "f3" else 16))
            for b in w.loop(NB, f.name):
                t2_pe(w, z)
                nc.tensor.wait_ge(t2_out, w.up(t2_out))
                for i in range(2):
                    for c in range(2):
                        ins = nc.tensor.matmul(bank(0)[:, i * 256:i * 256 + f.E], zT[:, c, i * P:(i + 1) * P], f.router[:, c, :],
                                               start=(c == 0), stop=(c == 1))
                ins.then_inc(route_ps, 1)
                nc.tensor.wait_ge(wt_ready, w.up(wt_ready))
                nc.tensor.wait_ge(tr_free, w.up(tr_free))
                for i in range(2):
                    ins = nc.tensor.transpose(bank(7)[0:f.E, i * P:(i + 1) * P], f.W[:, i, :], ident)
                ins.then_inc(tr_full, 1)
                w.skip(t2_out)
            nc.tensor.wait_ge(t2_out, w.same(t2_out))

            def unit(s, hf, lag):
                rhs = [f.hT[:, c, 2 * hf:2 * hf + 2, :] for c in range(2)]
                for c in range(2):
                    ins = nc.tensor.matmul(bank(hf), f.slot[s][:, c, :], rhs[c], start=(c == 0), stop=(c == 1))
                ins.then_inc(gu_ps, 1)
                if lag:
                    nc.tensor.wait_ge(inter_ready, w.up(inter_ready))
                if f.up:
                    for c in range(2):
                        nc.tensor.matmul(bank(2), f.slot[s][:, 2 + c, :], rhs[c], start=(c == 0), stop=(c == 1))
                nc.tensor.matmul(bank(3), f.slot[s][0:f.E, 6, :], f.WT[0:f.E, 2 * hf:2 * hf + 2, :], start=True, stop=True).then_inc(route_ps, 1)
                if lag:
                    lag()

            def down(s, hf):
                for j in range(4):
                    t = 4 * hf + j
                    ins = nc.tensor.matmul(bank(4 + t // 2)[:, t % 2 * 256:t % 2 * 256 + 256], f.inter[hf][:, j * P:(j + 1) * P],
                                           f.slot[s][:, 4:6, :], start=False, stop=False, skip_group_check=True)
                ins.then_inc(down_ps, 1)

            for k in range(4):
                nc.tensor.matmul(bank(4 + k), f.zeros[:, 0:P], f.zeros, start=True, stop=False, skip_group_check=True)
            nc.tensor.wait_ge(wc_in[0], w.up(wc_in[0], 16))
            unit(0, 0, None)
            unit(0, 1, lambda: down(0, 0))
            for j in w.loop((f.chunks - 1) // 2, f.name + "c"):
                nc.tensor.wait_ge(wc_in[1], w.up(wc_in[1], 16))
                unit(1, 0, lambda: down(0, 1))
                unit(1, 1, lambda: down(1, 0))
                nc.tensor.wait_ge(wc_in[0], w.up(wc_in[0], 16))
                unit(0, 0, lambda: down(1, 1))
                unit(0, 1, lambda: down(0, 0))
            nc.tensor.wait_ge(inter_ready, w.up(inter_ready))
            down(0, 1)

        def ffn_act(w, f):
            nc.scalar.wait_ge(phase_end, w.up(phase_end, 4))
            for b in w.loop(NB, f.name):
                ln_act(w)
                t2_act(w, zT)
                nc.scalar.wait_ge(route_in, w.up(route_in))
                if f.name == "f3":
                    for i in range(2):
                        ins = nc.scalar.activation(f.ex[:, i, 0:16], bank(0)[:, i * 256:i * 256 + 16], ACT.Exp, scale=-1.0)
                else:
                    n = f.E - 1
                    for i in range(2):
                        ins = nc.scalar.activation(f.ex[:, i, 0:n], f.lg[:, i, 0:n], ACT.Exp, bias=f.nm[:, i:i + 1])
                    if f.name == "f1":
                        for i in range(2):
                            ins = nc.scalar.activation(f.ws[:, i:i + 1], bank(0)[:, i * 256 + n:i * 256 + n + 1], ACT.Exp, scale=-1.0)
                ins.then_inc(route_exp, 1)
                nc.scalar.wait_ge(tr_full, w.up(tr_full))
                link(w, nc.scalar.activation(f.WT[0:f.E, b, :], bank(7)[0:f.E, 0:256], ACT.Copy))
                nc.scalar.sem_inc(tr_free, 1)
                nc.scalar.sem_inc(t2_out, 1)
                w.skip(t2_out)

            def silu(hf, wait=True):
                nc.scalar.wait_ge(gu_ps, w.up(gu_ps))
                if wait:
                    nc.scalar.wait_ge(inter_ready, w.up(inter_ready))
                nc.scalar.activation(f.sg[hf], bank(hf), ACT.Silu).then_inc(silu_ready, 1)

            silu(0, False)
            silu(1, False)
            for j in w.loop((f.chunks - 1) // 2, f.name + "c"):
                for hf in (0, 1, 0, 1):
                    silu(hf)
            w.skip(inter_ready, 2)

        def ffn_route(w, f):
            logits = bank(0).rearrange("p (i e) -> p i e", i=2)
            n, top = {"f1": (64, 8), "f2": (8, 2), "f3": (16, 6)}[f.name]
            pad = f.lg.shape[2] - n
            if f.name == "f3":
                nc.vector.sem_inc(route_in, 1)
                nc.vector.wait_ge(route_exp, w.up(route_exp))
                link(w, nc.vector.tensor_scalar(f.sel[:, :, 0:16], f.ex[:, :, 0:16], 1.0, None, ALU.add))
                link(w, nc.vector.reciprocal(f.ex[:, :, 0:16], f.sel[:, :, 0:16]))
                link(w, nc.vector.tensor_tensor(f.lg[:, :, 0:16], f.ex[:, :, 0:16], spread(f.bias, 1, 2), ALU.add))
                q = f.lg[:, :, 0:16].rearrange("p i (a b) -> p i a b", b=2)
                link(w, nc.vector.tensor_tensor(f.pr[:, :, :, 0], q[:, :, :, 0], q[:, :, :, 1], ALU.max))
                link(w, nc.vector.tensor_tensor(f.pr[:, :, :, 1], q[:, :, :, 0], q[:, :, :, 1], ALU.min))
                hi = f.pr[:, :, :, 0].rearrange("p i (g b) -> p i g b", b=2)
                lo = f.pr[:, :, :, 1].rearrange("p i (g b) -> p i g b", b=2)
                link(w, nc.vector.tensor_tensor(f.mr[:, :, 0:4], hi[:, :, :, 0], hi[:, :, :, 1], ALU.max))
                link(w, nc.vector.tensor_tensor(f.mr[:, :, 4:8], hi[:, :, :, 0], hi[:, :, :, 1], ALU.min))
                link(w, nc.vector.tensor_tensor(f.mr[:, :, 8:12], lo[:, :, :, 0], lo[:, :, :, 1], ALU.max))
                link(w, nc.vector.tensor_tensor(f.mr[:, :, 4:8], f.mr[:, :, 4:8], f.mr[:, :, 8:12], ALU.max))
                link(w, nc.vector.tensor_tensor(f.gp[:, :, 0:4], f.mr[:, :, 0:4], f.mr[:, :, 4:8], ALU.add))
                for i in range(2):
                    w.settle(settled)
                    link(w, nc.vector.max(f.g8[:, i, :], f.gp[:, i, :]))
                link(w, nc.vector.memset(f.g8[:, :, 2:8], -1e30))
                for i in range(2):
                    w.settle(settled)
                    link(w, nc.vector.match_replace(f.gr[:, i, :], f.g8[:, i, :], f.gp[:, i, :], -3e38))
                link(w, nc.vector.tensor_tensor(f.gr[:, :, 0:4], f.gr[:, :, 0:4], f.gp[:, :, 0:4], ALU.is_lt))
                lg4 = f.lg[:, :, 0:16].rearrange("p i (g b) -> p i g b", b=4)
                link(w, nc.vector.tensor_tensor(lg4, lg4, spread(f.gr[:, :, 0:4], 3, 4), ALU.mult))
                link(w, nc.vector.tensor_scalar(f.lg[:, :, 0:16], f.lg[:, :, 0:16], 0.0, None, ALU.add))
            else:
                link(w, nc.vector.tensor_copy(f.lg[:, :, 0:n], logits[:, :, 0:n]))
            for i in range(2):
                w.settle(settled)
                link(w, nc.vector.max(f.m8[:, i, :], f.lg[:, i, 0:n]))
            if f.name != "f3":
                link(w, nc.vector.tensor_scalar(f.nm, f.m8[:, :, 0], -1.0, None, ALU.mult))
                nc.vector.sem_inc(route_in, 1)
            if top < 8:
                link(w, nc.vector.memset(f.m8[:, :, top:8], -1e30))
            for i in range(2):
                w.settle(settled)
                link(w, nc.vector.match_replace(f.mr[:, i, :], f.m8[:, i, :], f.lg[:, i, :], -3e38))
            link(w, nc.vector.tensor_tensor(f.sel[:, :, 0:n], f.mr[:, :, 0:n], f.lg[:, :, 0:n], ALU.is_lt))
            if f.name != "f3":
                nc.vector.wait_ge(route_exp, w.up(route_exp))
            if f.name == "f1":
                link(w, nc.vector.tensor_scalar(f.rs, f.ws, 1.0, None, ALU.add))
                link(w, nc.vector.reciprocal(f.W[:, :, n], f.rs))
            link(w, nc.vector.tensor_tensor(f.mr[:, :, 0:n], f.ex[:, :, 0:n], f.sel[:, :, 0:n], ALU.mult))
            link(w, nc.vector.tensor_reduce(f.ws, f.mr[:, :, 0:n], AX.X, ALU.add))
            if f.name == "f3":
                link(w, nc.vector.tensor_scalar(f.ws, f.ws, 1e-20, None, ALU.add))
            link(w, nc.vector.reciprocal(f.rs, f.ws))
            if f.name == "f3":
                link(w, nc.vector.tensor_scalar(f.rs, f.rs, 2.5, None, ALU.mult))
            link(w, nc.vector.tensor_tensor(f.W[:, :, 0:n], f.mr[:, :, 0:n], spread(f.rs, 2, n), ALU.mult))
            nc.vector.sem_inc(wt_ready, 1)

        def ffn_dve(w, f):
            nc.vector.memset(f.lg, -1e30)
            nc.vector.memset(f.gp, -1e30)
            nc.vector.memset(f.W, 1.0)
            link(w, nc.vector.memset(f.zeros, 0.0))
            nc.vector.wait_ge(w_in, w.up(w_in, 32 if f.name == "f3" else 16))
            for b in w.loop(NB, f.name):
                ln_dve(w, b)
                nc.vector.sem_inc(t2_in, 1)
                w.skip(tr_full, 2)
                nc.vector.wait_ge(route_ps, w.up(route_ps))
                link(w, nc.vector.tensor_copy(f.hT[:, :, b, :], zT))
                ffn_route(w, f)

            def gated(hf):
                nc.vector.wait_ge(silu_ready, w.up(silu_ready))
                nc.vector.wait_ge(route_ps, w.up(route_ps))
                src = f.sg[hf]
                if f.up:
                    link(w, nc.vector.tensor_tensor(f.su, f.sg[hf], bank(2), ALU.mult))
                    src = f.su
                nc.vector.tensor_tensor(f.inter[hf], src, bank(3), ALU.mult).then_inc(inter_ready, 1)

            gated(0)
            gated(1)
            for j in w.loop((f.chunks - 1) // 2, f.name + "c"):
                for hf in (0, 1, 0, 1):
                    nc.vector.wait_ge(down_ps, w.up(down_ps))
                    gated(hf)
            nc.vector.wait_ge(down_ps, w.up(down_ps, 2))
            for b in range(NB):
                link(w, nc.vector.tensor_tensor(X[:, b, :, :], X[:, b, :, :], bank(4 + b).rearrange("p (i d) -> p i d", i=2), ALU.add))
                nc.vector.sem_inc(phase_end, 1)

        ffns = {name: Experts(name) for name in FFNS}

        a = Arena()
        x2 = Ctx(a, 8, CTX_TILES, L2_SPANS)
        x2s = Self(a, 8, x2)
        x2_ctxT = a.cut([2, CTX])
        x2_w = a.cut([2, 4 * 256])
        x2_mask = a.cut([2, S])
        x2_kraw = a.cut([2, D])
        x2_gate, x2_tg = a.cut([32]), a.cut([32])
        cos = cst[:, C_COS:C_COS + 16].rearrange("p (i e) -> p i e", i=2)
        sin = cst[:, C_SIN:C_SIN + 16].rearrange("p (i e) -> p i e", i=2)

        def x2_sp(sp, w):
            sp.wait_ge(phase_end, w.up(phase_end, 4))
            sp.dma_start(x2_w, d["w_x2"]).then_inc(w_in, 16)
            sp.dma_start(x2_gate, d["gate_x2"].partition_broadcast(P)).then_inc(gate_w, 16)
            for b in w.loop(NB, "x2"):
                sp.wait_ge(mask_used, w.up(mask_used))
                sp.dma_start(x2_mask, d["mask"][b]).then_inc(mask_in, 16)
                sp.wait_ge(ctx_used, w.up(ctx_used))
                sp.dma_start(x2_ctxT, d["ctxT"][b]).then_inc(ctx_in, 16)

        def x2_pe(w):
            nc.tensor.wait_ge(phase_end, w.up(phase_end, 4))
            nc.tensor.wait_ge(w_in, w.up(w_in, 16))
            for b in w.loop(NB, "x2"):
                t2_pe(w, z)
                nc.tensor.wait_ge(t2_out, w.up(t2_out))
                for j in range(3):
                    proj_nat(zT, x2_w[:, :, j * 256:(j + 1) * 256], bank(3 + j)).then_inc(q_ps, 1)
                nc.tensor.wait_ge(qn_ready, w.up(qn_ready))
                q_stack_pe(w, x2.QN, x2.slots, range(x2.quads))
                key_stacks_pe(w, x2s)
                self_pe(w, x2s)
                keys_pe(w, x2, x2_ctxT, lambda t: x2_w[:, :, 256:768], stacks=True)
                att_pe(w, x2, first=False)
                t2_pe(w, onat)
                nc.tensor.wait_ge(t2_out, w.up(t2_out))
                proj_nat(oT, x2_w[:, :, 768:1024], bank(0)).then_inc(proj_ps, 1)

        def x2_act(w):
            nc.scalar.wait_ge(phase_end, w.up(phase_end, 4))
            nc.scalar.wait_ge(gate_w, w.up(gate_w, 16))
            nc.scalar.activation(x2_tg, x2_gate, ACT.Tanh).then_inc(gate_ready, 1)
            for b in w.loop(NB, "x2"):
                ln_act(w)
                t2_act(w, zT)
                for g in range(x2.quads):
                    q_stack_act(w, x2.QT[:, 4 * g:4 * g + 4, :], x2.slots, qt_ready)
                keys_act(w, x2s, lambda t: x2_kraw[:, t, :])
                self_act(w, x2s)
                keys_act(w, x2, lambda t: x2.kn[t % 2])
                att_act(w, x2)
                t2_act(w, oT)

        def x2_finish_self(w, sx, g, v):
            link(w, nc.vector.tensor_tensor(onat[:, :, g * 32:(g + 1) * 32].rearrange("p i (h e) -> p i h e", h=4),
                                            v[:, :, :, 0:8], spread(sx.rec, 3, 8), ALU.mult))

        def x2_finish(w, cx, g, u):
            link(w, nc.vector.tensor_tensor(cx.rec, cx.rec, spread(x2_tg[:, 4 * g:4 * g + 4], 1, 2), ALU.mult))
            link(w, nc.vector.tensor_tensor(cx.tmp, u[:, :, :, 0:8], spread(cx.rec, 3, 8), ALU.mult))
            o = onat[:, :, g * 32:(g + 1) * 32]
            link(w, nc.vector.tensor_tensor(o, o, cx.tmp.rearrange("p i h e -> p i (h e)"), ALU.add))

        def rope(w, dst, ps):
            v = ps.rearrange("p (i h e) -> p i h e", i=2, h=32)
            o = dst.rearrange("p i (h e) -> p i h e", h=32)
            r = x2.qr.rearrange("p i (h e) -> p i h e", h=32)
            link(w, nc.vector.tensor_tensor(o, v, spread(cos, 2, 32), ALU.mult))
            link(w, nc.vector.tensor_tensor(r[:, :, :, 0:4], v[:, :, :, 4:8], spread(sin[:, :, 0:4], 2, 32), ALU.mult))
            link(w, nc.vector.tensor_tensor(r[:, :, :, 4:8], v[:, :, :, 0:4], spread(sin[:, :, 4:8], 2, 32), ALU.mult))
            link(w, nc.vector.tensor_tensor(dst, dst, x2.qr, ALU.add))

        def x2_dve(w):
            for buf in x2.KN + [x2.QN, x2.QT] + x2.QTm:
                link(w, nc.vector.memset(buf, 0.0))
            for kv in x2.KNv:
                link(w, nc.vector.memset(kv[:, :, 48:51], 1.0))
            nc.vector.memset(x2.V[:, :, :, 8:9], 1.0)
            nc.vector.memset(x2s.V[:, :, :, 8:9], 1.0)
            link(w, nc.vector.memset(bank(6), 0.0))
            nc.vector.wait_ge(gate_ready, w.up(gate_ready))
            nc.vector.wait_ge(w_in, w.up(w_in, 16))
            for b in w.loop(NB, "x2"):
                ln_dve(w, b)
                nc.vector.sem_inc(t2_in, 1)
                w.skip(tr_full)
                nc.vector.wait_ge(mask_in, w.up(mask_in, 16))
                link(w, nc.vector.tensor_scalar(x2_mask, x2_mask, LOWEST, None, ALU.max))
                nc.vector.wait_ge(q_ps, w.up(q_ps))
                rope(w, x2.q, bank(3))
                link(w, nc.vector.tensor_scalar(x2.q, x2.q, 8.0 ** -0.5, None, ALU.mult))
                link(w, nc.vector.memset(x2.QNv[:, :, :, 48:51], 0.0))
                split_q(w, x2.q, x2.qr, x2.QNv, 32, 8)
                nc.vector.sem_inc(qn_ready, 1)
                w.skip(tr_full, x2.quads)
                nc.vector.wait_ge(q_ps, w.up(q_ps, 2))
                rope(w, x2_kraw, bank(4))
                link(w, nc.vector.tensor_copy(x2s.V[:, :, :, 0:8], bank(5).rearrange("p (i h e) -> p i h e", i=2, h=32)))
                keys_dve(w, x2s, lambda t: nc.vector.sem_inc(kn_ready, 1), lambda t: x2_kraw[:, t, :])
                self_dve(w, x2s, x2_mask, x2_finish_self)
                nc.vector.sem_inc(mask_used, 1)

                def make(t):
                    k0, n = x2.tiles[t]
                    nc.vector.wait_ge(kv_ps, w.up(kv_ps))
                    nc.vector.tensor_copy(x2.kn[t % 2][:n, :], bank(t % 3)[:n, 0:256]).then_inc(kn_ready, 1)
                    nc.vector.tensor_copy(x2.V[:n, t, :, 0:8], bank(t % 3)[:n, 256:512].rearrange("p (h e) -> p h e", h=32)).then_inc(kv_free, 1)

                keys_dve(w, x2, make, lambda t: x2.kn[t % 2])
                nc.vector.sem_inc(ctx_used, 1)
                att_dve(w, x2, x2_finish)
                nc.vector.sem_inc(t2_in, 1)
                w.skip(tr_full)
                nc.vector.wait_ge(proj_ps, w.up(proj_ps))
                link(w, nc.vector.tensor_tensor(X[:, b, :, :], X[:, b, :, :], bank(0).rearrange("p (i d) -> p i d", i=2), ALU.add))
                nc.vector.sem_inc(phase_end, 1)

        a = Arena()
        x3_ctxT = a.cut([2, CTX])
        x3_w = a.cut([2, 5 * 256])
        x3_bg = a.cut([D])
        x3_qT, x3_qe, x3_qm = a.cut([2, S]), a.cut([2, S]), a.cut([2, S])
        x3_g, x3_ge = a.cut([2, D]), a.cut([2, D])
        x3_ke = [a.cut([D]) for _ in range(2)]
        x3_kmin = [a.cut([D]) for _ in range(2)]
        x3_km = [a.cut([D]) for _ in range(2)]
        x3_vm = [a.cut([2, P + 1]) for _ in range(2)]
        x3_S = a.cut([2, P + 8])
        x3_rec = a.cut([2, 16])

        def x3_sp(sp, w):
            sp.wait_ge(phase_end, w.up(phase_end, 4))
            sp.dma_start(x3_w, d["w_x3"]).then_inc(w_in, 16)
            sp.dma_start(x3_bg, d["bg_x3"].partition_broadcast(P)).then_inc(w_in, 16)
            for b in w.loop(NB, "x3"):
                sp.wait_ge(ctx_used, w.up(ctx_used))
                sp.dma_start(x3_ctxT, d["ctxT"][b]).then_inc(ctx_in, 16)

        def x3_pe(w):
            nc.tensor.wait_ge(phase_end, w.up(phase_end, 4))
            nc.tensor.wait_ge(w_in, w.up(w_in, 32))
            for b in w.loop(NB, "x3"):
                t2_pe(w, z)
                nc.tensor.wait_ge(t2_out, w.up(t2_out))
                for o in range(2):
                    for c in range(2):
                        ins = nc.tensor.matmul(bank(0)[:, o * 256:(o + 1) * 256], x3_w[:, c, o * P:(o + 1) * P], zT[:, c, :],
                                               start=(c == 0), stop=(c == 1))
                ins.then_inc(q_ps, 1)
                proj_nat(zT, x3_w[:, :, 256:512], bank(1)).then_inc(q_ps, 1)
                nc.tensor.wait_ge(ctx_in, w.up(ctx_in, 16))

                def summary(t):
                    n = CTX_TILES[t][1]
                    nc.tensor.wait_ge(km_ready, w.up(km_ready))
                    if n < P:
                        w.settle(settled)
                    for c in range(2):
                        ins = nc.tensor.matmul(bank(4 + c)[:, 0:P + 1], x3_km[t % 2][:n, c * P:(c + 1) * P], x3_vm[t % 2][:n, c, :],
                                               start=(t == 0), stop=(t == len(CTX_TILES) - 1))
                    ins.then_inc(ks_ps, 1)

                nc.tensor.wait_ge(gate_in, w.up(gate_in))
                for t, (k0, n) in enumerate(CTX_TILES):
                    for j, to in enumerate((2 + t % 2, (0, 6)[t % 2])):
                        for c in range(2):
                            ins = nc.tensor.matmul(bank(to)[:n, 0:256], x3_ctxT[:, c, k0:k0 + n], x3_w[:, c, 512 + 256 * j:768 + 256 * j],
                                                   start=(c == 0), stop=(c == 1))
                        ins.then_inc((kv_ps, v_ps)[j], 1)
                    if t:
                        summary(t - 1)
                summary(len(CTX_TILES) - 1)
                nc.tensor.wait_ge(sum_sb, w.up(sum_sb))
                for i in range(2):
                    for c in range(2):
                        ins = nc.tensor.matmul(bank((6, 0)[i])[:, c * 136:(c + 1) * 136], x3_qT[:, c, i * P:(i + 1) * P], x3_S[:, c, :],
                                               start=True, stop=True)
                ins.then_inc(sum_ps, 1)
                t2_pe(w, onat)
                nc.tensor.wait_ge(t2_out, w.up(t2_out))
                proj_nat(oT, x3_w[:, :, 1024:1280], bank(1)).then_inc(proj_ps, 1)

        def x3_act(w):
            nc.scalar.wait_ge(phase_end, w.up(phase_end, 4))
            for b in w.loop(NB, "x3"):
                ln_act(w)
                t2_act(w, zT)
                nc.scalar.wait_ge(fm_in, w.up(fm_in))
                nc.scalar.activation(x3_qe, x3_qm, ACT.Exp).then_inc(fm_exp, 1)
                nc.scalar.wait_ge(gate_in, w.up(gate_in))
                nc.scalar.activation(x3_ge, x3_g, ACT.Exp, scale=-1.0).then_inc(gate_ready, 1)
                for t, (k0, n) in enumerate(CTX_TILES):
                    nc.scalar.wait_ge(v_ps, w.up(v_ps))
                    nc.scalar.wait_ge(ks_ps, w.up(ks_ps))
                    link(w, nc.scalar.activation(x3_vm[t % 2][:n, :, 0:P], bank((0, 6)[t % 2])[:n, 0:256].rearrange("p (c e) -> p c e", c=2), ACT.Copy))
                    nc.scalar.wait_ge(fm_in, w.up(fm_in))
                    nc.scalar.activation(x3_ke[t % 2][:n, :], x3_kmin[t % 2][:n, :], ACT.Exp).then_inc(fm_exp, 1)
                t2_act(w, oT)

        def x3_dve(w):
            for v in x3_vm:
                link(w, nc.vector.memset(v, 1.0))
            nc.vector.wait_ge(w_in, w.up(w_in, 32))
            blk = cst[:, C_BLK:C_BLK + 8]
            for b in w.loop(NB, "x3"):
                ln_dve(w, b)
                nc.vector.sem_inc(t2_in, 1)
                w.skip(tr_full)
                nc.vector.wait_ge(q_ps, w.up(q_ps))
                qps = bank(0).rearrange("p (c t) -> p c t", c=2)
                nc.vector.tensor_scalar(x3_qm, qps, 0.0, None, ALU.min).then_inc(fm_in, 1)
                nc.vector.wait_ge(fm_exp, w.up(fm_exp))
                link(w, nc.vector.scalar_tensor_tensor(out=x3_qT, in0=qps, scalar=1.0, in1=x3_qe, op0=ALU.add, op1=ALU.max))
                nc.vector.wait_ge(q_ps, w.up(q_ps))
                nc.vector.tensor_tensor(x3_g, bank(1).rearrange("p (i d) -> p i d", i=2), spread(x3_bg, 1, 2), ALU.add).then_inc(gate_in, 1)
                nc.vector.wait_ge(gate_ready, w.up(gate_ready))
                link(w, nc.vector.tensor_scalar(x3_g, x3_ge, 1.0, None, ALU.add))
                link(w, nc.vector.reciprocal(x3_g, x3_g))

                def feature(t):
                    n = CTX_TILES[t][1]
                    nc.vector.wait_ge(fm_exp, w.up(fm_exp))
                    nc.vector.wait_ge(ks_ps, w.up(ks_ps))
                    nc.vector.scalar_tensor_tensor(out=x3_km[t % 2][:n, :], in0=bank(2 + t % 2)[:n, 0:256], scalar=1.0,
                                                   in1=x3_ke[t % 2][:n, :], op0=ALU.add, op1=ALU.max).then_inc(km_ready, 1)

                for t, (k0, n) in enumerate(CTX_TILES):
                    nc.vector.wait_ge(kv_ps, w.up(kv_ps))
                    nc.vector.tensor_scalar(x3_kmin[t % 2][:n, :], bank(2 + t % 2)[:n, 0:256], 0.0, None, ALU.min).then_inc(fm_in, 1)
                    feature(t)
                nc.vector.sem_inc(ctx_used, 1)
                nc.vector.wait_ge(ks_ps, w.same(ks_ps, 2))
                for c in range(2):
                    link(w, nc.vector.tensor_tensor(x3_S[:, c, 0:P], bank(4 + c)[:, 0:P], cst[:, C_BMASK:C_BMASK + P], ALU.mult))
                    link(w, nc.vector.tensor_scalar(x3_S[:, c, P:P + 8], blk, bank(4 + c)[:, P:P + 1], None, ALU.mult))
                nc.vector.sem_inc(sum_sb, 1)
                nc.vector.wait_ge(sum_ps, w.up(sum_ps))
                for i in range(2):
                    v = bank((6, 0)[i])[:, 0:272].rearrange("p (c e) -> p c e", c=2)
                    rec = x3_rec[:, i, :]
                    rc = rec.rearrange("p (c h) -> p c h", c=2)
                    link(w, nc.vector.tensor_scalar(rc, v[:, :, P:P + 8], 1e-6, None, ALU.add))
                    link(w, nc.vector.reciprocal(rec, rec))
                    link(w, nc.vector.tensor_tensor(onat[:, i, :].rearrange("p (c h e) -> p c h e", c=2, h=8),
                                                    v[:, :, 0:P].rearrange("p c (h e) -> p c h e", h=8),
                                                    spread(rc, 3, 16), ALU.mult))
                link(w, nc.vector.tensor_tensor(onat, onat, x3_g, ALU.mult))
                nc.vector.sem_inc(t2_in, 1)
                w.skip(tr_full)
                nc.vector.wait_ge(proj_ps, w.up(proj_ps))
                link(w, nc.vector.tensor_tensor(X[:, b, :, :], X[:, b, :, :], bank(1).rearrange("p (i d) -> p i d", i=2), ALU.add))
                nc.vector.sem_inc(phase_end, 1)

        with nc.Block() as block:
            @block.sync
            def _(sp):
                w = Counts(sp, "sp", steps)
                sp.dma_start(cst, d["consts"]).then_inc(consts_in, 16)
                for b in range(NB):
                    sp.dma_start(X[:, b, :, :], d["x"][b].rearrange("(i p) d -> p i d", p=P)).then_inc(consts_in, 16)
                x0_sp(sp, w)
                f0_sp(sp, w)
                x1_sp(sp, w)
                ffn_sp(sp, w, ffns['f1'])
                x2_sp(sp, w)
                ffn_sp(sp, w, ffns['f2'])
                x3_sp(sp, w)
                ffn_sp(sp, w, ffns['f3'])
                sp.wait_ge(phase_end, w.up(phase_end, 4))
                for b in range(NB):
                    sp.dma_start(out[b].rearrange("(i p) d -> p i d", p=P), X[:, b, :, :]).then_inc(out_done, 16)
                sp.wait_ge(out_done, 16 * NB)

            @block.gpsimd
            def _(pool):
                pool.sem_inc(ctx_used, 1)
                pool.sem_inc(tr_free, 1)
                pool.sem_inc(kv_free, 3)
                pool.sem_inc(kt_free[0], 1)
                pool.sem_inc(kt_free[1], 1)
                pool.sem_inc(mx_free, 2)
                pool.sem_inc(pv_done, 2)
                pool.sem_inc(spv_done, 2)
                pool.sem_inc(mask_used, 1)
                pool.sem_inc(ks_ps, 2)

            @block.scalar
            def _(act):
                w = Counts(act, "act", steps)
                act.wait_ge(consts_in, w.up(consts_in, 80))
                x0_act(w)
                f0_act(w)
                x1_act(w)
                ffn_act(w, ffns['f1'])
                x2_act(w)
                ffn_act(w, ffns['f2'])
                x3_act(w)
                ffn_act(w, ffns['f3'])

            @block.vector
            def _(dve):
                w = Counts(dve, "dve", steps)
                w.skip(mx_free, 2)
                w.skip(pv_done, 2)
                w.skip(spv_done, 2)
                dve.wait_ge(consts_in, w.up(consts_in, 80))
                nc.vector.tensor_copy(identb, ident).then_inc(consts_ready, 1)
                x0_dve(w)
                f0_dve(w)
                x1_dve(w)
                ffn_dve(w, ffns['f1'])
                x2_dve(w)
                ffn_dve(w, ffns['f2'])
                x3_dve(w)
                ffn_dve(w, ffns['f3'])

            @block.tensor
            def _(pe):
                w = Counts(pe, "pe", steps)
                pe.wait_ge(consts_ready, w.up(consts_ready))
                x0_pe(w)
                f0_pe(w)
                x1_pe(w)
                ffn_pe(w, ffns['f1'])
                x2_pe(w)
                ffn_pe(w, ffns['f2'])
                x3_pe(w)
                ffn_pe(w, ffns['f3'])


def host_consts():
    c = np.zeros((P, NCST), np.float32)
    p = np.arange(P)
    c[:, C_EPS5], c[:, C_EPS6], c[:, C_ONE] = 1e-5, 1e-6, 1.0
    for t in range(11):
        c[:, C_KEY + t] = P * t + p
    tail = np.zeros((14, 7), np.float32)
    tail[:3, 0:3] = 1.0
    tail[3:, 3:6] = 1.0
    c[:, C_TAIL:C_TAIL + 98] = tail.reshape(1, -1)
    inv = 1.0 / 10000.0 ** (np.arange(0, 8, 2, dtype=np.float32) / 8)
    emb = np.outer(np.arange(S, dtype=np.float32), inv)
    emb = np.concatenate([emb, emb], -1)
    cos, sin = np.cos(emb), np.sin(emb)
    sin = np.concatenate([-sin[:, :4], sin[:, 4:]], -1)
    c[:, C_COS:C_COS + 16] = cos.reshape(2, P, 8).transpose(1, 0, 2).reshape(P, 16)
    c[:, C_SIN:C_SIN + 16] = sin.reshape(2, P, 8).transpose(1, 0, 2).reshape(P, 16)
    c[:, C_BLK:C_BLK + 8] = (p[:, None] // 16 == np.arange(8)[None, :])
    c[:, C_BMASK:C_BMASK + P] = (p[:, None] // 16 == p[None, :] // 16)
    c[:, C_IDENT:C_IDENT + P] = np.eye(P)
    q = p[:, None, None] + P * np.arange(2)[None, :, None]
    k = np.arange(S)[None, None, :]
    c[:, C_CAUSAL:C_CAUSAL + 512] = np.where(k > q, -BIG, 0.0).reshape(P, 512)
    return c


def rows(w, n=None):
    return np.ascontiguousarray(w.reshape(2, P, -1).transpose(1, 0, 2))


def kernel(**inputs):
    import concourse.bacc as bacc
    from concourse.bass_utils import run_bass_kernel_spmd

    v = {k: np.asarray(a) for k, a in inputs.items()}
    cat = np.concatenate
    arrays = {
        "consts": host_consts(),
        "x": v["x"],
        "ctxT": v["ctx_2048"].transpose(0, 2, 1).reshape(NB, 2, P, CTX).transpose(0, 2, 1, 3),
        "decay": v["L1_xattn_decay"].reshape(1),
        "lens": v["L0_xattn_context_lens"].reshape(1),
        "w_x0": rows(cat([v["L0_xattn_" + n] for n in ("Wq", "Wk", "Wv", "Wk_img", "Wv_img", "Wo")], 1)),
        "v_x0": cat([v["L0_xattn_" + n] for n in ("bq", "gq", "bk", "gk", "bv", "bk_img", "gk_img", "bv_img", "bo")]),
    }
    T = np.transpose

    def chunks(gate, up, down, name):
        n, E, R = FFNS[name][1], FFNS[name][2], FFNS[name][1] * P

        def padded(w):
            return cat([w, np.zeros((R - w.shape[0],) + w.shape[1:], w.dtype)])

        def turned(w):
            return T(padded(w).reshape(n, P, 2, P), (0, 3, 2, 1))

        sizes = {"f1": [64] * 65, "f2": [176] * 9, "f3": [176] * 16 + [352]}[name]
        owner = np.full(R, -1)
        owner[:sum(sizes)] = np.repeat(np.arange(E), sizes)
        pick = np.zeros((n, P, 1, P), np.float32)
        pick[:, :E, 0, :] = T(owner.reshape(n, P)[:, None, :] == np.arange(E)[None, :, None], (0, 1, 2))
        g = turned(gate)
        u = turned(up) if up is not None else np.zeros_like(g)
        return cat([g, u, padded(down).reshape(n, P, 2, P), pick], 2)

    gu = v["L1_ffn_gu_w"]
    arrays.update({
        "w_f0": rows(cat([v["L0_ffn_" + n].T for n in ("Wq", "Wk", "Wv", "Wo")], 1)),
        "mlp_f0": T(np.stack([rows(v["L0_ffn_W_in_base"].T), rows(v["L0_ffn_W_up_base"].T)]), (1, 2, 0, 3)),
        "down_f0": T(v["L0_ffn_W_down"].T.reshape(8, P, D), (1, 0, 2)),
        "A_f0": rows(v["L0_ffn_A"]),
        "B_f0": v["L0_ffn_B"],
        "v_f0": cat([v["L0_ffn_ln1_w"], v["L0_ffn_ln2_w"]]),
        "w_x1": rows(cat([v["L1_xattn_W_in"].T, v["L1_xattn_W_out"].T], 1)),
        "v_x1": cat([v["L1_xattn_" + n] for n in ("b_out", "gamma", "beta")]),
        "bin_x1": v["L1_xattn_b_in"].reshape(2, P).T,
        "router_f1": rows(cat([v["L1_ffn_gate_w"], v["L1_ffn_sh_gate1_w"]]).T),
        "chunks_f1": chunks(cat([gu[:, :64].reshape(-1, D), v["L1_ffn_sh_gate_w"]]), cat([gu[:, 64:].reshape(-1, D), v["L1_ffn_sh_up_w"]]),
                            cat([T(v["L1_ffn_dp_w"], (0, 2, 1)).reshape(-1, D), v["L1_ffn_sh_down_w"].T]), "f1"),
        "w_x2": rows(cat([v["L2_xattn_" + n] for n in ("Wq", "Wk", "Wv", "Wo")], 1)),
        "gate_x2": v["L2_xattn_gate"].reshape(-1),
        "mask": v["mask_Bx1xSxS_fk0"].reshape(NB, 2, P, S).transpose(0, 2, 1, 3),
        "router_f2": rows(cat([v["L2_ffn_w_router"], np.zeros((D, 1), np.float32)], 1)),
        "chunks_f2": chunks(cat([T(v["L2_ffn_w1"], (0, 2, 1)).reshape(-1, D), v["L2_ffn_w_shared1"].T]), None,
                            cat([v["L2_ffn_w2"].reshape(-1, D), v["L2_ffn_w_shared2"]]), "f2"),
        "w_x3": rows(cat([v["L3_xattn_" + n].T for n in ("Wq", "Wg", "Wkv", "Wo")], 1)),
        "bg_x3": v["L3_xattn_bg"],
        "router_f3": rows(cat([v["L3_ffn_gate_weight"], np.zeros((1, D), np.float32)]).T),
        "bias_f3": v["L3_ffn_e_score_correction_bias"],
        "chunks_f3": chunks(cat([v["L3_ffn_gate_proj"].reshape(-1, D), v["L3_ffn_shared_gate_w"]]),
                            cat([v["L3_ffn_up_proj"].reshape(-1, D), v["L3_ffn_shared_up_w"]]),
                            cat([T(v["L3_ffn_down_proj"], (0, 2, 1)).reshape(-1, D), v["L3_ffn_shared_down_w"].T]), "f3"),
    })
    arrays = {k: np.ascontiguousarray(a) for k, a in arrays.items()}

    def program(steps):
        nc = bacc.Bacc("TRN2", target_bir_lowering=False, num_devices=1)
        d = {k: nc.dram_tensor(f"in_{k}", a.shape, mybir.dt.from_np(a.dtype), kind="ExternalInput").ap() for k, a in arrays.items()}
        out = nc.dram_tensor("out_x", (NB, S, D), F32, kind="ExternalOutput").ap()
        build(nc, d, out, steps)
        return nc

    steps = {}
    program(steps)
    r = run_bass_kernel_spmd(program(steps), [{f"in_{k}": a for k, a in arrays.items()}], core_ids=[0])
    return r.results[0]["out_x"]
```

```python
from contextlib import ExitStack

import numpy as np
import concourse.bass as bass
from concourse import mybir

F32 = mybir.dt.float32
BF16 = mybir.dt.bfloat16
I32 = mybir.dt.int32
ALU = mybir.AluOpType
ACT = mybir.ActivationFunctionType
AX = mybir.AxisListType

P = 128
NB = 4
S = 256
D = 256
CTX = 1601
IMG = 257
TXT = CTX - IMG
T8 = NB * S // P
BIG = 2.0 ** 100
LOWEST = -3.4028234663852886e38

L0_TILES = [(0, 128), (128, 128), (256, 1)] + [(IMG + P * t, min(P, TXT - P * t)) for t in range(11)]
CTX_TILES = [(P * t, min(P, CTX - P * t)) for t in range(13)]
L0_SPANS = [(0, IMG)] + [(IMG + 448 * c, 448) for c in range(3)]
L2_SPANS = [(400 * c, 401) for c in range(4)]

C_EPS5, C_EPS6, C_ONE = 0, 1, 2
C_KEY = 3
C_TAIL = C_KEY + 11
C_COS = C_TAIL + 14 * 7
C_SIN = C_COS + 16
C_BLK = C_SIN + 16
C_BMASK = C_BLK + 8
C_IDENT = C_BMASK + 128
C_CAUSAL = C_IDENT + 128
NCST = C_CAUSAL + 512

FFNS = {"f1": (True, 33, 65), "f2": (False, 13, 9), "f3": (True, 25, 17)}


class Counts:

    def __init__(self, eng, tag, steps):
        self.eng, self.tag, self.steps = eng, tag, steps
        self.total, self.frame = {}, None

    def same(self, sem, more=0):
        name = sem.name
        if self.frame is None:
            return self.total.get(name, 0) + more
        i, key, seen = self.frame
        per = self.steps.get((self.tag, key), {}).get(name, 0)
        return i * per + (self.total.get(name, 0) + seen.get(name, 0) + more)

    def skip(self, sem, n=1):
        store = self.total if self.frame is None else self.frame[2]
        store[sem.name] = store.get(sem.name, 0) + n

    def up(self, sem, n=1):
        self.skip(sem, n)
        return self.same(sem)

    def settle(self, sem):
        if self.frame is not None:
            self.eng.sem_inc(sem, 1)

    def loop(self, count, key):
        seen = {}
        with self.eng.Fori(0, count) as i:
            self.frame = (i, key, seen)
            yield i
        self.frame = None
        self.steps[(self.tag, key)] = seen
        for name, n in seen.items():
            self.total[name] = self.total.get(name, 0) + count * n


def build(nc, d, out, steps):
    with ExitStack() as top:
        sems = {}

        def sem(name):
            if name not in sems:
                sems[name] = top.enter_context(nc.semaphore(name))
            return sems[name]

        def sbuf(ctx, name, shape, dt=F32):
            return ctx.enter_context(nc.sbuf_tensor(name, shape, dt))[tuple(slice(None) for _ in shape)]

        act_step, dve_step, pool_step = sem("act_step"), sem("dve_step"), sem("pool_step")
        consts_in = sem("consts_in")
        consts_ready = sem("consts_ready")
        phase_end = sem("phase_end")
        w_in = sem("w_in")
        ctx_in, ctx_used = sem("ctx_in"), sem("ctx_used")
        mask_in, mask_used = sem("mask_in"), sem("mask_used")
        tr_full, tr_free = sem("tr_full"), sem("tr_free")
        ln_var, ln_std = sem("ln_var"), sem("ln_std")
        t2_in, t2_out = sem("t2_in"), sem("t2_out")
        q_ps, q_sb = sem("q_ps"), sem("q_sb")
        kv_ps, kv_free = sem("kv_ps"), sem("kv_free")
        kraw_ready, ss_ready, k_std = sem("kraw_ready"), sem("ss_ready"), sem("k_std")
        kn_ready, kn_cast = sem("kn_ready"), sem("kn_cast")
        kst_ready, kst_free = sem("kst_ready"), sem("kst_free")
        kt_full, kt_free = [sem("kt_full_a"), sem("kt_full_b")], [sem("kt_free_a"), sem("kt_free_b")]
        qn_ready, qt_ready = sem("qn_ready"), sem("qt_ready")
        mx_full, mx_free = sem("mx_full"), sem("mx_free")
        st_full, p_ready, pv_done, pvs_ready = sem("st_full"), sem("p_ready"), sem("pv_done"), sem("pvs_ready")
        s_full, s_masked, sp_ready = sem("s_full"), sem("s_masked"), sem("sp_ready")
        pt_full, pt_ready, spv_done = sem("pt_full"), sem("pt_ready"), sem("spv_done")
        proj_ps, proj_used = sem("proj_ps"), sem("proj_used")
        mod_ps, mod_sb = sem("mod_ps"), sem("mod_sb")
        gu_ps, silu_ready, inter_ready, down_ps = sem("gu_ps"), sem("silu_ready"), sem("inter_ready"), sem("down_ps")
        sum_ps, sum_sb = sem("sum_ps"), sem("sum_sb")
        gate_ready = sem("gate_ready")
        logits_ps = sem("logits_ps")
        route_ps, route_exp, wt_ready = sem("route_ps"), sem("route_exp"), sem("wt_ready")
        wc_in = [sem("wc_in_a"), sem("wc_in_b")]
        norm_out = sem("norm_out")
        qkv_out = sem("qkv_out")
        mlp_ps, attn_ps, v_ps, gate_w, route_in = sem("mlp_ps"), sem("attn_ps"), sem("v_ps"), sem("gate_w"), sem("route_in")
        fm_exp, fm_in, km_ready, ks_ps = sem("fm_exp"), sem("fm_in"), sem("km_ready"), sem("ks_ps")
        gate_in, dec_in = sem("gate_in"), sem("dec_in")
        out_done = sem("out_done")
        settled = sem("settled")

        X = sbuf(top, "X", [P, NB, 2, D])
        identb = sbuf(top, "identb", [P, P], BF16)
        cst = sbuf(top, "cst", [P, NCST])
        z = sbuf(top, "z", [P, 2, D])
        zT = sbuf(top, "zT", [P, 2, S])
        onat = sbuf(top, "onat", [P, 2, D])
        oT = sbuf(top, "oT", [P, 2, S])
        st6 = sbuf(top, "st6", [P, 2, 6])
        mv = sbuf(top, "mv", [P, 2, 2])
        std = sbuf(top, "std", [P, 2])
        rstd = sbuf(top, "rstd", [P, 2])
        all6 = sbuf(top, "all6", [P, T8, 6])
        all_mv = sbuf(top, "all_mv", [P, T8, 2])
        all_std = sbuf(top, "all_std", [P, T8])
        all_rstd = sbuf(top, "all_rstd", [P, T8])
        cw = sbuf(top, "cw", [P, NB, 2])
        cwb = sbuf(top, "cwb", [P, 2])
        csum = sbuf(top, "csum", [P, 1])
        PS = top.enter_context(nc.psum_tensor("PS", [P, 8, 512], F32))
        ARENA_COLS = 47900
        arena = sbuf(top, "arena", [P, ARENA_COLS])
        ident = cst[:, C_IDENT:C_IDENT + P]
        eps5, eps6 = cst[:, C_EPS5:C_EPS5 + 1], cst[:, C_EPS6:C_EPS6 + 1]

        class Arena:

            def __init__(self):
                self.at = 0

            def cut(self, shape, dt=F32):
                n = int(np.prod(shape)) // (1 if dt == F32 else 2)
                a = arena[:, self.at:self.at + n]
                self.at += n
                assert self.at <= ARENA_COLS, (self.at, ARENA_COLS)
                if dt != F32:
                    a = a.bitcast(dt)
                if len(shape) > 1:
                    names = "abcd"[:len(shape)]
                    a = a.rearrange(f"p ({' '.join(names)}) -> p {' '.join(names)}", **dict(zip(names, shape)))
                return a

        def bank(i):
            return PS[:, i, :]

        def bank16(i):
            return PS[:, i, :].bitcast(BF16)

        def link(w, ins):
            s = {"act": act_step, "dve": dve_step, "pool": pool_step}[w.tag]
            ins.then_inc(s, 1)
            w.eng.wait_ge(s, w.up(s))

        def spread(ap, axis, n):
            a = ap.unsqueeze(axis)
            shape = list(a.shape)
            shape[axis] = n
            return a.broadcast_to(shape)

        STACK_BANKS = (0, 1, 2, 7)

        def ln_dve(w, b, dst=None, src=None):
            dst = z if dst is None else dst
            src = X[:, b, :, :] if src is None else src
            for i in range(2):
                link(w, nc.vector.bn_stats(st6[:, i, :], src[:, i, :]))
            w.settle(settled)
            link(w, nc.vector.bn_aggr(mv[:, 0, :], st6[:, 0, :]))
            w.settle(settled)
            nc.vector.bn_aggr(mv[:, 1, :], st6[:, 1, :]).then_inc(ln_var, 1)
            nc.vector.wait_ge(ln_std, w.up(ln_std))
            link(w, nc.vector.reciprocal(rstd[:, :], std[:, :]))
            for i in range(2):
                link(w, nc.vector.tensor_scalar(dst[:, i, :], src[:, i, :], mv[:, i, 0:1], rstd[:, i:i + 1],
                                                ALU.subtract, ALU.mult))

        def ln_act(w):
            nc.scalar.wait_ge(ln_var, w.up(ln_var))
            nc.scalar.activation(std[:, :], mv[:, :, 1], ACT.Sqrt, bias=eps5).then_inc(ln_std, 1)

        def norm_dve(w, Z):
            for t in range(T8):
                ins = nc.vector.bn_stats(all6[:, t, :], X[:, t // 2, t % 2, :])
            link(w, ins)
            for t in range(T8):
                ins = nc.vector.bn_aggr(all_mv[:, t, :], all6[:, t, :])
            ins.then_inc(ln_var, 1)
            nc.vector.wait_ge(ln_std, w.up(ln_std))
            link(w, nc.vector.reciprocal(all_rstd, all_std))
            for t in range(T8):
                ins = nc.vector.tensor_scalar(Z[:, t, :], X[:, t // 2, t % 2, :], all_mv[:, t, 0:1], all_rstd[:, t:t + 1],
                                              ALU.subtract, ALU.mult)
                if t % 2:
                    ins.then_inc(t2_in, 1)
            w.skip(tr_full, NB)

        def norm_out_act(w, ZT):
            for b in range(NB):
                nc.scalar.wait_ge(tr_full, w.up(tr_full))
                nc.scalar.activation(ZT[:, :, b, :], bank(2 + b).rearrange("p (c t) -> p c t", c=2), ACT.Copy).then_inc(t2_out, 1)
            w.skip(t2_out, NB)

        def norm_pe(w, Z):
            for b in range(NB):
                nc.tensor.wait_ge(t2_in, w.up(t2_in))
                for c in range(2):
                    for i in range(2):
                        ins = nc.tensor.transpose(bank(2 + b)[:, c * 256 + i * P:c * 256 + (i + 1) * P],
                                                  Z[:, 2 * b + i, c * P:(c + 1) * P], ident)
                ins.then_inc(tr_full, 1)

        def norm_act(w, ZT):
            nc.scalar.wait_ge(ln_var, w.up(ln_var))
            nc.scalar.activation(all_std, all_mv[:, :, 1], ACT.Sqrt, bias=eps5).then_inc(ln_std, 1)
            norm_out_act(w, ZT)

        def t2_pe(w, src):
            nc.tensor.wait_ge(t2_in, w.up(t2_in))
            nc.tensor.wait_ge(tr_free, w.up(tr_free))
            for c in range(2):
                for i in range(2):
                    ins = nc.tensor.transpose(bank(7)[:, c * 256 + i * P:c * 256 + (i + 1) * P],
                                              src[:, i, c * P:(c + 1) * P], ident)
            ins.then_inc(tr_full, 1)

        def t2_act(w, dst):
            nc.scalar.wait_ge(tr_full, w.up(tr_full))
            nc.scalar.activation(dst, bank(7).rearrange("p (c t) -> p c t", c=2), ACT.Copy).then_inc(t2_out, 1)
            nc.scalar.wait_ge(t2_out, w.up(t2_out))
            nc.scalar.sem_inc(tr_free, 1)

        def skip_tr(w, n=1):
            w.skip(tr_full, n)

        def proj_nat(lhsT, rhs, ps, last=None):
            for i in range(2):
                for c in range(2):
                    ins = nc.tensor.matmul(ps[:, i * 256:(i + 1) * 256], lhsT[:, c, i * P:(i + 1) * P],
                                           rhs[:, c, 0:256], start=(c == 0), stop=(c == 1))
            return ins

        def split_q(w, q, r, QNv, H, e):
            for i in range(2):
                blocks = QNv[:, i, :, 0:6 * e].rearrange("p h (j e) -> p h j e", j=6)
                qh = q[:, i, :].rearrange("p (h e) -> p h e", h=H)
                rh = r[:, i, :].rearrange("p (h e) -> p h e", h=H)
                link(w, nc.vector.tensor_copy(blocks[:, :, 0, :], qh))
                nc.vector.tensor_copy(blocks[:, :, 3, :], qh)
                nc.vector.tensor_copy(blocks[:, :, 5, :], qh)
                link(w, nc.vector.tensor_tensor(rh, qh, blocks[:, :, 0, :], ALU.subtract))
                link(w, nc.vector.tensor_copy(blocks[:, :, 1, :], rh))
                nc.vector.tensor_copy(blocks[:, :, 4, :], rh)
                link(w, nc.vector.tensor_tensor(blocks[:, :, 2, :], rh, blocks[:, :, 1, :], ALU.subtract))

        def split_k_act(w, kn, KNv, n, H, e):
            nc.scalar.activation(KNv[:n, :, 0:3 * e].rearrange("p h (j e) -> p h j e", j=3),
                                 spread(kn[:n, :].rearrange("p (h e) -> p h e", h=H), 2, 3), ACT.Copy).then_inc(kn_cast, 1)

        def split_k_dve(w, kn, r, KNv, n, H, e):
            kh = kn[:n, :].rearrange("p (h e) -> p h e", h=H)
            rh = r[:n, :].rearrange("p (h e) -> p h e", h=H)
            link(w, nc.vector.tensor_tensor(rh, kh, KNv[:n, :, 0:e], ALU.subtract))
            link(w, nc.vector.tensor_copy(KNv[:n, :, 3 * e:4 * e], rh))
            nc.vector.tensor_copy(KNv[:n, :, 4 * e:5 * e], rh)
            return nc.vector.tensor_tensor(KNv[:n, :, 5 * e:6 * e], rh, KNv[:n, :, 3 * e:4 * e], ALU.subtract)

        def q_stack_pe(w, QN, slots, quads):
            for g in quads:
                nc.tensor.wait_ge(tr_free, w.up(tr_free))
                for s in range(slots):
                    for i in range(2):
                        ins = nc.tensor.transpose(bank16(7)[:, s * 256 + i * P:s * 256 + (i + 1) * P],
                                                  QN[:, i, g * slots + s, :], identb[:, :])
                ins.then_inc(tr_full, 1)

        def q_stacks_pe(w, QN):
            nc.tensor.wait_ge(tr_free, w.up(tr_free))
            for k, to in enumerate(STACK_BANKS):
                for s in range(4):
                    for i in range(2):
                        ins = nc.tensor.transpose(bank16(to)[:, s * 256 + i * P:s * 256 + (i + 1) * P],
                                                  QN[:, i, 4 * k + s, :], identb[:, :])
                ins.then_inc(tr_full, 1)

        def q_stacks_act(w, QT, slots):
            for k, to in enumerate(STACK_BANKS):
                nc.scalar.wait_ge(tr_full, w.up(tr_full))
                src = bank16(to).rearrange("p (s t) -> p s t", s=4)
                if slots == 4:
                    nc.scalar.activation(QT[:, 4 * k:4 * k + 4, :], src, ACT.Copy).then_inc(qt_ready, 1)
                else:
                    nc.scalar.activation(QT[0:64, 8 * k:8 * k + 8:2, :], src[0:64], ACT.Copy)
                    nc.scalar.activation(QT[64:P, 8 * k + 1:8 * k + 8:2, :], src[64:P], ACT.Copy).then_inc(qt_ready, 1)
            nc.scalar.wait_ge(qt_ready, w.up(qt_ready, 4))
            nc.scalar.sem_inc(tr_free, 1)

        def q_stack_act(w, dst, slots, done):
            nc.scalar.wait_ge(tr_full, w.up(tr_full))
            src = bank16(7)[:, 0:slots * 256].rearrange("p (s t) -> p s t", s=slots)
            if slots == 4:
                nc.scalar.activation(dst, src, ACT.Copy).then_inc(done, 1)
            else:
                nc.scalar.activation(dst[0:64, 0:4:2, :], src[0:64], ACT.Copy)
                nc.scalar.activation(dst[64:P, 1:4:2, :], src[64:P], ACT.Copy).then_inc(done, 1)
            nc.scalar.wait_ge(done, w.up(done))
            nc.scalar.sem_inc(tr_free, 1)

        def self_keys_act(w, sx, kn_of):
            nc.scalar.wait_ge(kn_ready, w.up(kn_ready, 2))
            for t in range(2):
                split_k_act(w, kn_of(t), sx.KNv[t], P, sx.H, sx.e)
            for t in range(2):
                key_stack_out(w, act_copy, sx, t, 0)
            w.skip(kt_full[1], 2)

        def self_keys_dve(w, sx, kn_of, q_part):
            for t in range(2):
                nc.vector.wait_ge(kn_cast, w.up(kn_cast))
                split_k_dve(w, kn_of(t), sx.r, sx.KNv[t], P, sx.H, sx.e).then_inc(kst_ready, 1)
                nc.vector.wait_ge(kst_ready, w.up(kst_ready))
            key_stack_out(w, nc.vector.tensor_copy, sx, 0, 1)
            q_part()
            nc.vector.sem_inc(qn_ready, 1)
            w.skip(tr_full, 4)
            key_stack_out(w, nc.vector.tensor_copy, sx, 1, 1)

        class Ctx:

            def __init__(self, a, e, tiles, spans):
                self.e, self.H, self.tiles, self.spans = e, D // e, tiles, spans
                self.slots = 4 if e == 16 else 2
                self.quads = self.H // 4
                self.kinds = 2 if e == 16 else 1
                self.turn = 10
                self.plan = [3, 2, 3, 2, 2, 3, 2, 3, 2, 3] + ([1, 3, 3] if len(tiles) == 13 else [1, 1, 2, 3])
                self.lead = sum(self.plan[self.turn:])
                self.kT = a.cut([16, CTX], BF16)
                self.V = a.cut([len(tiles), self.H, e + 1])
                self.KN = [a.cut([16, P], BF16) for _ in range(2)]
                self.QN = a.cut([2, 16, P], BF16)
                self.QT = a.cut([self.H, S], BF16)
                self.QTm = [a.cut([4, S], BF16) for _ in range(2)]
                self.p = [a.cut([4 * S]) for _ in range(2)]
                self.pvs = a.cut([512])
                self.kn = [a.cut([D]) for _ in range(2)]
                self.r = a.cut([D])
                self.q = a.cut([2, D])
                self.qr = a.cut([2, D])
                self.mpart = a.cut([2, 4, 4])
                self.nm = a.cut([2, 4, self.kinds])
                self.nr = a.cut([2, 4, self.kinds])
                self.rec = a.cut([2 * self.kinds, 4])
                self.tmp = a.cut([2 * self.kinds, 4, e])
                wdt = 2048 // self.H
                self.KNv = [k.rearrange("p s (g c) -> p (s g) c", c=wdt) for k in self.KN]
                self.QNv = self.QN.rearrange("p i s (g c) -> p i (s g) c", c=wdt)

        def keys_pe(w, cx, ctxT, wkv, stacks=False):
            nc.tensor.wait_ge(ctx_in, w.up(ctx_in, 16))
            for t, (k0, n) in enumerate(cx.tiles):
                nc.tensor.wait_ge(kv_free, w.up(kv_free))
                for c in range(2):
                    ins = nc.tensor.matmul(bank(t % 3)[:n, :], ctxT[:, c, k0:k0 + n], wkv(t)[:, c, :],
                                           start=(c == 0), stop=(c == 1))
                ins.then_inc(kv_ps, 1)
                if stacks and t >= 2:
                    key_stacks_pe(w, cx, [t - 2])
            if stacks:
                key_stacks_pe(w, cx, [len(cx.tiles) - 2, len(cx.tiles) - 1])

        def key_stacks_pe(w, cx, which=None):
            for t in range(len(cx.tiles)) if which is None else which:
                k0, n = cx.tiles[t]
                nc.tensor.wait_ge(kst_ready, w.up(kst_ready))
                for half in range(2):
                    nc.tensor.wait_ge(kt_free[half], w.up(kt_free[half]))
                    if n < P:
                        w.settle(settled)
                    for s in range(8):
                        ins = nc.tensor.transpose(bank16(4 + half)[:, s * P:s * P + n],
                                                  cx.KN[t % 2][:n, half * 8 + s, :], identb[:n, :n])
                    ins.then_inc(kt_full[half], 1)

        def key_stack_out(w, copy, cx, t, half):
            k0, n = cx.tiles[t]
            w.eng.wait_ge(kt_full[half], w.up(kt_full[half]))
            src = bank16(4 + half).rearrange("p (s t) -> p s t", s=8)[:, :, 0:n]
            copy(cx.kT[:, half * 8:half * 8 + 8, k0:k0 + n], src).then_inc(kt_free[half], 1)

        def act_copy(dst, src):
            return nc.scalar.activation(dst, src, ACT.Copy)

        def keys_act(w, cx, kn_of):
            for t, (k0, n) in enumerate(cx.tiles):
                nc.scalar.wait_ge(kn_ready, w.up(kn_ready))
                if t >= 2:
                    nc.scalar.wait_ge(kt_full[1], w.up(kt_full[1]))
                split_k_act(w, kn_of(t), cx.KNv[t % 2], n, cx.H, cx.e)
                if t:
                    key_stack_out(w, act_copy, cx, t - 1, 0)
            key_stack_out(w, act_copy, cx, len(cx.tiles) - 1, 0)
            w.skip(kt_full[1], 2)

        def keys_dve(w, cx, make, kn_of, tail=None):
            make(0)
            for t, (k0, n) in enumerate(cx.tiles):
                if t + 1 < len(cx.tiles):
                    make(t + 1)
                nc.vector.wait_ge(kn_cast, w.up(kn_cast))
                if tail:
                    tail(t)
                split_k_dve(w, kn_of(t), cx.r, cx.KNv[t % 2], n, cx.H, cx.e).then_inc(kst_ready, 1)
                if t:
                    key_stack_out(w, nc.vector.tensor_copy, cx, t - 1, 1)
                nc.vector.wait_ge(kst_ready, w.up(kst_ready))
            key_stack_out(w, nc.vector.tensor_copy, cx, len(cx.tiles) - 1, 1)

        def att_pe(w, cx, first=True):
            nt = len(cx.tiles)

            def max_chunks(g):
                for i in range(2):
                    for h in range(4):
                        for k0, n in cx.spans:
                            yield g, i, h, k0, n

            chunks = [c for g in range(cx.quads) for c in max_chunks(g)]

            def max_passes(n):
                for chunk in chunks[:n]:
                    max_pass(chunk)
                del chunks[:n]

            count = [0]

            def max_pass(chunk):
                g, i, h, k0, n = chunk
                nc.tensor.wait_ge(mx_free, w.up(mx_free))
                head = 4 * g + h
                slot = head * 16 // cx.H
                nc.tensor.matmul(bank(4 + count[0] % 2)[:, 0:n], cx.QT[:, head, i * P:(i + 1) * P],
                                 cx.kT[:, slot, k0:k0 + n], start=True, stop=True).then_inc(mx_full, 1)
                count[0] += 1

            def scores(g, kt):
                k0, n = cx.tiles[kt]
                e = g * nt + kt
                for s in range(cx.slots):
                    wd = 1024 // cx.slots
                    col = s * wd
                    nh = 4 // cx.slots
                    ins = nc.tensor.matmul(PS[:n, 2 * (e % 2) + col // 512, col % 512:col % 512 + wd],
                                           cx.kT[:, g * cx.slots + s, k0:k0 + n],
                                           cx.QTm[g % 2][:, s * nh:(s + 1) * nh, :],
                                           start=True, stop=True)
                ins.then_inc(st_full, 1)

            def values(g, kt):
                k0, n = cx.tiles[kt]
                e = g * nt + kt
                nc.tensor.wait_ge(p_ready, w.up(p_ready))
                if n < P:
                    w.settle(settled)
                first, last = (0, 3) if cx.kinds == 2 and kt < 3 else (3 if cx.kinds == 2 else 0, nt)
                ty = 1 if cx.kinds == 2 and kt >= 3 else 0
                off = ty * 256 if cx.kinds == 2 else (g % 2) * 256
                for h in range(4):
                    ins = nc.tensor.matmul(bank(6)[32 * h:32 * h + cx.e + 1, off:off + 256],
                                           cx.V[:n, kt, 4 * g + h, :], cx.p[e % 2][:n, h * S:(h + 1) * S],
                                           start=(kt == first), stop=(kt == last - 1),
                                           tile_position=(0, 32 * h))
                ins.then_inc(pv_done, 1)

            def out_transposes(g):
                nc.tensor.wait_ge(tr_free, w.up(tr_free))
                off = 0 if cx.kinds == 2 else (g % 2) * 256
                for u in range(2 * cx.kinds):
                    ins = nc.tensor.transpose(bank(7)[:, u * P:(u + 1) * P],
                                              cx.pvs[:, off + u * P:off + (u + 1) * P], ident)
                ins.then_inc(tr_full, 1)

            def maxima(g):
                nc.tensor.wait_ge(qn_ready, w.up(qn_ready))
                q_stack_pe(w, cx.QN, cx.slots, [g])

            if first:
                nc.tensor.wait_ge(qt_ready, w.up(qt_ready, 4))
            for half in range(2):
                nc.tensor.wait_ge(kt_free[half], w.same(kt_free[half], 1))
            max_passes(32 + cx.lead)
            maxima(0)
            for g in range(cx.quads):
                nc.tensor.wait_ge(qt_ready, w.up(qt_ready))
                for kt in range(nt):
                    scores(g, kt)
                    max_passes(cx.plan[kt] // 2)
                    if kt == 3 and g:
                        out_transposes(g - 1)
                    if kt == cx.turn + 1 and g + 1 < cx.quads:
                        maxima(g + 1)
                    if kt == 1 and g:
                        nc.tensor.wait_ge(pvs_ready, w.up(pvs_ready))
                    if kt:
                        values(g, kt - 1)
                    elif g:
                        values(g - 1, nt - 1)
                    max_passes(cx.plan[kt] - cx.plan[kt] // 2)
            values(cx.quads - 1, nt - 1)
            nc.tensor.wait_ge(pvs_ready, w.up(pvs_ready))
            out_transposes(cx.quads - 1)

        def att_act(w, cx):
            nt = len(cx.tiles)
            q_stack_act(w, cx.QTm[0], cx.slots, qt_ready)
            for g in range(cx.quads):
                for kt in range(nt):
                    k0, n = cx.tiles[kt]
                    e = g * nt + kt
                    nc.scalar.wait_ge(st_full, w.up(st_full))
                    nc.scalar.wait_ge(pv_done, w.up(pv_done))
                    nc.scalar.activation(cx.p[e % 2][:n, :], PS[:n, 2 * (e % 2):2 * (e % 2) + 2, :].rearrange("p a b -> p (a b)"),
                                         ACT.Exp).then_inc(p_ready, 1)
                    if kt == 3 and g:
                        skip_tr(w)
                    if kt == cx.turn + 1 and g + 1 < cx.quads:
                        q_stack_act(w, cx.QTm[(g + 1) % 2], cx.slots, qt_ready)
            skip_tr(w)

        def att_dve(w, cx, finish):
            nt, ns, ty = len(cx.tiles), len(cx.spans), cx.kinds
            count = [0]

            def reduce(i, h, c):
                nc.vector.wait_ge(mx_full, w.up(mx_full))
                n = cx.spans[c][1]
                nc.vector.tensor_reduce(cx.mpart[:, i, h, c:c + 1], bank(4 + count[0] % 2)[:, 0:n],
                                        AX.X, ALU.max).then_inc(mx_free, 1)
                w.skip(mx_free)
                count[0] += 1

            def maxima(g):
                nc.vector.wait_ge(mx_free, w.same(mx_free))
                QNm = cx.QNv[:, :, 4 * g:4 * g + 4, 6 * cx.e:6 * cx.e + 3 * ty].rearrange("p i h (t j) -> p i h t j", t=ty)
                if ty == 2:
                    nc.vector.tensor_scalar(cx.nm[:, :, :, 0], cx.mpart[:, :, :, 0], -1.0, None, ALU.mult)
                    link(w, nc.vector.tensor_reduce(cx.nm[:, :, :, 1], cx.mpart[:, :, :, 1:4], AX.X, ALU.max, negate=True))
                else:
                    link(w, nc.vector.tensor_reduce(cx.nm[:, :, :, 0], cx.mpart[:, :, :, :], AX.X, ALU.max, negate=True))
                for t in range(ty):
                    link(w, nc.vector.tensor_copy(QNm[:, :, :, t, 0], cx.nm[:, :, :, t]))
                    link(w, nc.vector.tensor_tensor(cx.nr[:, :, :, t], cx.nm[:, :, :, t], QNm[:, :, :, t, 0], ALU.subtract))
                    link(w, nc.vector.tensor_copy(QNm[:, :, :, t, 1], cx.nr[:, :, :, t]))
                    last = nc.vector.tensor_tensor(QNm[:, :, :, t, 2], cx.nr[:, :, :, t], QNm[:, :, :, t, 1], ALU.subtract)
                    if t < ty - 1:
                        link(w, last)
                last.then_inc(qn_ready, 1)
                skip_tr(w)

            def evacuate(g):
                off = 0 if ty == 2 else (g % 2) * 256
                nc.vector.wait_ge(pv_done, w.up(pv_done, nt))
                nc.vector.tensor_copy(cx.pvs[:, off:off + 256 * ty], bank(6)[:, off:off + 256 * ty]).then_inc(pvs_ready, 1)

            def outputs(g):
                nc.vector.wait_ge(tr_full, w.up(tr_full))
                u = bank(7)[:, 0:256 * ty].rearrange("p (u h e) -> p u h e", u=2 * ty, h=4)
                link(w, nc.vector.reciprocal(cx.rec[:, :, :], u[:, :, :, cx.e]))
                finish(w, cx, g, u)
                nc.vector.sem_inc(tr_free, 1)

            parts = [(g, i, h, c) for g in range(cx.quads) for i in range(2) for h in range(4) for c in range(ns)]
            whole = 8 * ns

            def reduces(n):
                for g, i, h, c in parts[:n]:
                    reduce(i, h, c)
                    if (i, h, c) == (1, 3, ns - 1):
                        maxima(g)
                del parts[:n]

            reduces(whole + cx.lead)
            for g in range(cx.quads):
                for kt in range(nt):
                    if kt == 1 and g:
                        evacuate(g - 1)
                    reduces(cx.plan[kt])
                    if kt == 3 and g:
                        outputs(g - 1)
            evacuate(cx.quads - 1)
            outputs(cx.quads - 1)

        class Self:

            def __init__(self, a, e, cx=None):
                self.e, self.H, self.tiles = e, D // e, [(0, P), (P, P)]
                self.slots, self.quads, self.kinds = (4 if e == 16 else 2), D // e // 4, 1
                self.kT = a.cut([16, S], BF16)
                self.V = a.cut([2, self.H, e + 1])
                self.s = [a.cut([2, S]) for _ in range(3)]
                self.pT = [a.cut([2, S]) for _ in range(2)]
                self.nm = a.cut([3, 2])
                self.sm = a.cut([3, 2])
                if cx is None:
                    self.KN = [a.cut([16, P], BF16) for _ in range(2)]
                    self.QN = a.cut([2, 16, P], BF16)
                    self.QT = a.cut([self.H, S], BF16)
                    self.p = [a.cut([2 * S]) for _ in range(2)]
                    self.pvs, self.r = a.cut([512]), a.cut([D])
                    self.q, self.qr = a.cut([2, D]), a.cut([2, D])
                    self.rec, self.tmp = a.cut([2, 4]), a.cut([2, 4, e])
                else:
                    self.KN, self.QN, self.QT, self.pvs, self.r, self.q, self.qr = cx.KN, cx.QN, cx.QT, cx.pvs, cx.r, cx.q, cx.qr
                    self.rec, self.tmp = cx.rec, cx.tmp
                    self.p = [x[:, 0:512] for x in cx.p]
                wdt = 2048 // self.H
                self.KNv = [k.rearrange("p s (g c) -> p (s g) c", c=wdt) for k in self.KN]
                self.QNv = self.QN.rearrange("p i s (g c) -> p i (s g) c", c=wdt)

        def self_pe(w, sx):
            def scores(u):
                for i in range(2):
                    ins = nc.tensor.matmul(bank((0, 1, 4)[u % 3])[:, i * 256:(i + 1) * 256], sx.QT[:, u, i * P:(i + 1) * P],
                                           sx.kT[:, u * 16 // sx.H, :], start=True, stop=True)
                ins.then_inc(s_full, 1)

            def probs(u):
                nc.tensor.wait_ge(sp_ready, w.up(sp_ready))
                for k in range(2):
                    for i in range(2):
                        ins = nc.tensor.transpose(bank(2 + u % 2)[:, k * 256 + i * P:k * 256 + (i + 1) * P],
                                                  sx.p[u % 2][:, i * 256 + k * P:i * 256 + (k + 1) * P], ident)
                ins.then_inc(pt_full, 1)

            def values(u):
                nc.tensor.wait_ge(pt_ready, w.up(pt_ready))
                h, g = u % 4, u // 4
                for k in range(2):
                    ins = nc.tensor.matmul(bank(6)[32 * h:32 * h + sx.e + 1, (g % 2) * 256:(g % 2) * 256 + 256],
                                           sx.V[:, k, u, :], sx.pT[u % 2][:, k, :], start=(k == 0), stop=(k == 1),
                                           tile_position=(0, 32 * h))
                ins.then_inc(spv_done, 1)

            def out_transposes(g):
                nc.tensor.wait_ge(tr_free, w.up(tr_free))
                for i in range(2):
                    ins = nc.tensor.transpose(bank(7)[:, i * P:(i + 1) * P],
                                              sx.pvs[:, (g % 2) * 256 + i * P:(g % 2) * 256 + (i + 1) * P], ident)
                ins.then_inc(tr_full, 1)

            nc.tensor.wait_ge(qt_ready, w.up(qt_ready, 4))
            for half in range(2):
                nc.tensor.wait_ge(kt_free[half], w.same(kt_free[half], 1))
            for u in range(sx.H + 4):
                if u < sx.H:
                    scores(u)
                if 2 <= u <= sx.H + 1:
                    probs(u - 2)
                if u % 4 == 3 and u >= 7:
                    nc.tensor.wait_ge(pvs_ready, w.up(pvs_ready))
                if 3 <= u <= sx.H + 2:
                    values(u - 3)
                if u % 4 == 3 and u >= 7:
                    out_transposes((u - 7) // 4)

        def self_act(w, sx):
            def copy(u):
                nc.scalar.wait_ge(pt_full, w.up(pt_full))
                nc.scalar.wait_ge(spv_done, w.up(spv_done))
                nc.scalar.activation(sx.pT[u % 2], bank(2 + u % 2).rearrange("p (k t) -> p k t", k=2),
                                     ACT.Copy).then_inc(pt_ready, 1)

            for u in range(sx.H + 1):
                if u < sx.H:
                    nc.scalar.wait_ge(s_masked, w.up(s_masked))
                    for i in range(2):
                        ins = nc.scalar.activation(sx.p[u % 2][:, i * 256:(i + 1) * 256], sx.s[u % 3][:, i, :], ACT.Exp,
                                                   bias=sx.nm[:, u % 3, i:i + 1])
                    ins.then_inc(sp_ready, 1)
                if u:
                    copy(u - 1)
            w.skip(tr_full, sx.quads)

        def self_dve(w, sx, mask, finish):
            def masked(u):
                nc.vector.wait_ge(s_full, w.up(s_full))
                if u >= 3:
                    nc.vector.wait_ge(sp_ready, w.up(sp_ready))
                for i in range(2):
                    w.settle(settled)
                    link(w, nc.vector.tensor_tensor_reduce(
                        out=sx.s[u % 3][:, i, :], in0=bank((0, 1, 4)[u % 3])[:, i * 256:(i + 1) * 256], in1=mask[:, i, :],
                        scale=1.0, scalar=LOWEST, op0=ALU.add, op1=ALU.max, accum_out=sx.sm[:, u % 3, i:i + 1]))
                nc.vector.tensor_scalar(sx.nm[:, u % 3, :], sx.sm[:, u % 3, :], -1.0, None, ALU.mult).then_inc(s_masked, 1)

            for u in range(sx.H + 4):
                if u < sx.H:
                    masked(u)
                if u >= 6 and u % 4 == 2:
                    g = (u - 6) // 4
                    nc.vector.wait_ge(spv_done, w.up(spv_done, 4))
                    nc.vector.tensor_copy(sx.pvs[:, (g % 2) * 256:(g % 2) * 256 + 256],
                                          bank(6)[:, (g % 2) * 256:(g % 2) * 256 + 256]).then_inc(pvs_ready, 1)
                if u >= 7 and u % 4 == 3:
                    g = (u - 7) // 4
                    nc.vector.wait_ge(tr_full, w.up(tr_full))
                    v = bank(7)[:, 0:256].rearrange("p (u h e) -> p u h e", u=2, h=4)
                    link(w, nc.vector.reciprocal(sx.rec[:, 0:2, :], v[:, :, :, sx.e]))
                    finish(w, sx, g, v)
                    nc.vector.sem_inc(tr_free, 1)
            w.skip(sp_ready, 3)

        def vec(a, n):
            return a.cut([n, D])

        a = Arena()
        x0 = Ctx(a, 16, L0_TILES, L0_SPANS)
        x0_ctxT = a.cut([2, CTX])
        x0_w = a.cut([2, 6 * 256])
        x0_v = vec(a, 9)
        x0_kraw = a.cut([14, D])
        x0_ss, x0_std, x0_rk = a.cut([16]), a.cut([16]), a.cut([16])
        x0_tail = a.cut([14, 7])
        x0_len = a.cut([1])
        x0_flag = a.cut([2])
        x0_junk = x0_kraw[:, 0, :]
        x0_sq = a.cut([D])
        x0_wts = a.cut([CTX])
        x0_junk2 = x0.kT.rearrange("p s t -> p (s t)")[:, 0:2 * CTX].bitcast(F32)
        x0_dec = a.cut([2])
        x0_q = a.cut([NB, 2, D])
        x0_kTf = x0.kT.rearrange("p s t -> p (s t)").bitcast(F32)
        x0_Z = x0_kTf[:, CTX:CTX + T8 * D].rearrange("p (t d) -> p t d", t=T8)
        x0_ZT = x0_kTf[:, CTX + T8 * D:CTX + 2 * T8 * D].rearrange("p (c b t) -> p c b t", c=2, b=NB)
        X0_QBANKS = (3, 4, 5, 7)

        def x0_wkv(t):
            return x0_w[:, :, 256:768] if t >= 3 else x0_w[:, :, 768:1280]

        def x0_sp(sp, w):
            sp.dma_start(x0_dec[:, 0:1], d["decay"].partition_broadcast(P)).then_inc(dec_in, 16)
            sp.dma_start(x0_len.bitcast(I32), d["lens"].partition_broadcast(P)).then_inc(w_in, 16)
            sp.dma_start(x0_w[:, :, :], d["w_x0"]).then_inc(w_in, 16)
            sp.dma_start(x0_v.rearrange("p n d -> p (n d)"), d["v_x0"].partition_broadcast(P)).then_inc(w_in, 16)
            for b in w.loop(NB, "x0"):
                sp.wait_ge(ctx_used, w.up(ctx_used))
                sp.dma_start(x0_ctxT[:, :, :], d["ctxT"][b]).then_inc(ctx_in, 16)

        def x0_pe(w):
            norm_pe(w, x0_Z)
            nc.tensor.wait_ge(t2_out, w.up(t2_out, NB))
            nc.tensor.wait_ge(w_in, w.up(w_in, 48))
            for b in range(NB):
                proj_nat(x0_ZT[:, :, b, :], x0_w[:, :, 0:256], bank(X0_QBANKS[b])).then_inc(q_ps, 1)
            for b in w.loop(NB, "x0"):
                keys_pe(w, x0, x0_ctxT, x0_wkv)
                nc.tensor.wait_ge(qn_ready, w.up(qn_ready))
                q_stacks_pe(w, x0.QN)
                key_stacks_pe(w, x0)
                att_pe(w, x0)
                t2_pe(w, onat)
                nc.tensor.wait_ge(t2_out, w.up(t2_out))
                proj_nat(oT, x0_w[:, :, 1280:1536], bank(3)).then_inc(proj_ps, 1)

        def x0_act(w):
            nc.scalar.wait_ge(dec_in, w.up(dec_in, 16))
            nc.scalar.activation(x0_dec[:, 1:2], x0_dec[:, 0:1], ACT.Exp, scale=-1.0).then_inc(fm_exp, 1)
            norm_act(w, x0_ZT)
            for b in w.loop(NB, "x0"):
                nc.scalar.wait_ge(q_sb, w.up(q_sb))
                for i in range(2):
                    link(w, nc.scalar.activation(x0_sq[:, :], x0.q[:, i, :], ACT.Square, accum_out=x0_ss[:, 14 + i:15 + i]))
                for t, (k0, n) in enumerate(x0.tiles):
                    nc.scalar.wait_ge(kraw_ready, w.up(kraw_ready))
                    link(w, nc.scalar.activation(x0_sq[:n, :], x0_kraw[:n, t, :], ACT.Square, accum_out=x0_ss[:n, t:t + 1]))
                nc.scalar.activation(x0_std[:, :], x0_ss[:, :], ACT.Sqrt, bias=eps6, scale=1.0 / D).then_inc(k_std, 1)
                q_stacks_act(w, x0.QT, x0.slots)
                keys_act(w, x0, lambda t: x0.kn[t % 2])
                att_act(w, x0)
                t2_act(w, oT)

        def x0_start(w):
            nc.vector.wait_ge(w_in, w.up(w_in, 48))
            for buf in x0.KN:
                nc.vector.memset(buf[:, :, :], 0.0)
            nc.vector.memset(x0.QN[:, :, :, :], 0.0)
            nc.vector.memset(x0_ss[:, :], 1.0)
            nc.vector.memset(x0.V[:, :, :, 16:17], 1.0)
            link(w, nc.vector.memset(bank(6), 0.0))
            nc.vector.memset(x0.QN[:, :, :, 102:103], 1.0)
            link(w, nc.vector.tensor_copy(x0_flag[:, 0:1], x0_len.bitcast(I32)))
            link(w, nc.vector.tensor_scalar(x0_flag[:, 1:2], x0_flag[:, 0:1], 0.0, None, ALU.is_gt))
            link(w, nc.vector.tensor_copy(x0_tail[:, :, :], cst[:, C_TAIL:C_TAIL + 98].rearrange("p (t j) -> p t j", t=14)))
            link(w, nc.vector.tensor_scalar(x0_tail[:, 3:14, 6], cst[:, C_KEY:C_KEY + 11], x0_flag[:, 0:1], -BIG,
                                            ALU.is_ge, ALU.mult))
            link(w, nc.vector.tensor_scalar(x0_tail[:, 3:14, 6], x0_tail[:, 3:14, 6], x0_flag[:, 1:2], None, ALU.mult))
            nc.vector.tensor_scalar(x0_v[:, 3, :], x0_v[:, 3, :], x0_flag[:, 1:2], None, ALU.mult)
            nc.vector.tensor_scalar(x0_v[:, 1, :], x0_v[:, 1, :], 0.25, None, ALU.mult)
            nc.vector.wait_ge(fm_exp, w.up(fm_exp))
            link(w, nc.vector.tensor_scalar(x0_dec[:, 0:1], x0_dec[:, 1:2], 1.0, None, ALU.add))
            link(w, nc.vector.reciprocal(x0_dec[:, 1:2], x0_dec[:, 0:1]))
            decay_row = x0_junk2[:, 0:CTX]
            ones_row = x0_kraw.rearrange("p t d -> p (t d)")[:, 0:CTX]
            nc.vector.memset(ones_row, 1.0)
            link(w, nc.vector.memset(decay_row, 0.0))
            link(w, nc.vector.tensor_scalar(decay_row, decay_row, x0_dec[:, 1:2], None, ALU.add))
            link(w, nc.vector.tensor_tensor_scan(x0_wts[:, ::-1], decay_row, ones_row, 0.0, ALU.mult, ALU.add))
            link(w, nc.vector.tensor_reduce(csum[:, :], x0_wts[:, :], AX.X, ALU.add))

        def x0_finish(w, cx, g, u):
            link(w, nc.vector.tensor_tensor(cx.tmp[:, :, :, :], u[:, :, :, 0:16], spread(cx.rec[:, :, :], 3, 16), ALU.mult))
            t = cx.tmp.rearrange("p u h e -> p u (h e)")
            link(w, nc.vector.tensor_tensor(onat[:, :, g * 64:(g + 1) * 64], t[:, 0:2, :], t[:, 2:4, :], ALU.add))

        def x0_dve(w):
            norm_dve(w, x0_Z)
            x0_start(w)
            for b in range(NB):
                nc.vector.wait_ge(q_ps, w.up(q_ps))
                link(w, nc.vector.tensor_tensor(x0_q[:, b, :, :], bank(X0_QBANKS[b]).rearrange("p (i d) -> p i d", i=2),
                                                spread(x0_v[:, 0, :], 1, 2), ALU.add))
            for b in w.loop(NB, "x0"):
                w.settle(settled)
                nc.vector.tensor_copy(x0.q, x0_q[:, b, :, :]).then_inc(q_sb, 1)
                for t, (k0, n) in enumerate(x0.tiles):
                    bk, bv = (2, 4) if t >= 3 else (5, 7)
                    nc.vector.wait_ge(kv_ps, w.up(kv_ps))
                    nc.vector.tensor_tensor(x0_kraw[:n, t, :], bank(t % 3)[:n, 0:256], x0_v[:n, bk, :], ALU.add).then_inc(kraw_ready, 1)
                    nc.vector.tensor_tensor(x0.V[:n, t, :, 0:16], bank(t % 3)[:n, 256:512].rearrange("p (h e) -> p h e", h=16),
                                            x0_v[:n, bv, :].rearrange("p (h e) -> p h e", h=16), ALU.add).then_inc(kv_free, 1)
                nc.vector.wait_ge(k_std, w.up(k_std))
                link(w, nc.vector.reciprocal(x0_rk[:, :], x0_std[:, :]))
                for i in range(2):
                    ins = nc.vector.scalar_tensor_tensor(out=x0.q[:, i, :], in0=x0.q[:, i, :], scalar=x0_rk[:, 14 + i:15 + i],
                                                         in1=x0_v[:, 1, :], op0=ALU.mult, op1=ALU.mult)
                link(w, ins)
                link(w, nc.vector.memset(x0.QN[:, :, :, 96:102], 0.0))
                split_q(w, x0.q, x0.qr, x0.QNv, 16, 16)
                nc.vector.sem_inc(qn_ready, 1)
                w.skip(tr_full, 4)

                def make(t):
                    k0, n = x0.tiles[t]
                    nc.vector.scalar_tensor_tensor(out=x0.kn[t % 2][:n, :], in0=x0_kraw[:n, t, :], scalar=x0_rk[:n, t:t + 1],
                                                   in1=x0_v[:n, 3 if t >= 3 else 6, :], op0=ALU.mult, op1=ALU.mult).then_inc(kn_ready, 1)

                def tail(t):
                    n = x0.tiles[t][1]
                    nc.vector.tensor_copy(x0.KN[t % 2][:n, :, 96:103], spread(x0_tail[:n, t, :], 1, 16))

                keys_dve(w, x0, make, lambda t: x0.kn[t % 2], tail)
                for c in range(2):
                    link(w, nc.vector.tensor_tensor_reduce(out=x0_kraw.rearrange("p t d -> p (t d)")[:, 0:CTX], in0=x0_ctxT[:, c, :], in1=x0_wts[:, :],
                                                           scale=1.0, scalar=0.0, op0=ALU.mult, op1=ALU.add,
                                                           accum_out=cwb[:, c:c + 1]))
                nc.vector.tensor_copy(cw[:, b, :], cwb[:, :])
                nc.vector.sem_inc(ctx_used, 1)
                att_dve(w, x0, x0_finish)
                nc.vector.sem_inc(t2_in, 1)
                w.skip(tr_full)
                nc.vector.wait_ge(proj_ps, w.up(proj_ps))
                link(w, nc.vector.tensor_tensor(X[:, b, :, :], X[:, b, :, :], bank(3).rearrange("p (i d) -> p i d", i=2), ALU.add))
                link(w, nc.vector.tensor_tensor(X[:, b, :, :], X[:, b, :, :], spread(x0_v[:, 8, :], 1, 2), ALU.add))
                nc.vector.sem_inc(phase_end, 1)

        a = Arena()
        f0 = Self(a, 16)
        f0_w = a.cut([2, 4 * 256])
        f0_mlp = a.cut([2, 2, 1024])
        f0_down = a.cut([8, D])
        f0_A = a.cut([2, 16])
        f0_B = a.cut([1024])
        f0_v = a.cut([2, D])
        f0_Z, f0_x1, f0_h = (a.cut([T8, D]) for _ in range(3))
        f0_xT, f0_HT = a.cut([2, NB, S]), a.cut([2, NB, S])
        f0_q, f0_k, f0_vv = (a.cut([NB, 2, D]) for _ in range(3))
        f0_hT, f0_aT = a.cut([2, S]), a.cut([2, S])
        f0_kraw = a.cut([2, D])
        f0_sq = a.cut([D])
        f0_ss, f0_std, f0_rr = a.cut([T8]), a.cut([T8]), a.cut([T8])
        f0_th, f0_mT = a.cut([S]), a.cut([S])
        f0_sg = [a.cut([S]) for _ in range(2)]
        f0_inter = a.cut([8, S])

        def f0_sp(sp, w):
            sp.wait_ge(phase_end, w.up(phase_end, 4))
            for dst, name in ((f0_w, "w_f0"), (f0_mlp, "mlp_f0"), (f0_down, "down_f0"), (f0_A, "A_f0")):
                sp.dma_start(dst, d[name]).then_inc(w_in, 16)
            sp.dma_start(f0_B[0:16, :], d["B_f0"]).then_inc(w_in, 16)
            sp.dma_start(f0_v.rearrange("p n d -> p (n d)"), d["v_f0"].partition_broadcast(P)).then_inc(w_in, 16)

        def f0_pe(w):
            nc.tensor.wait_ge(phase_end, w.up(phase_end, 4))
            norm_pe(w, f0_x1)
            nc.tensor.wait_ge(t2_out, w.up(t2_out, NB))
            norm_pe(w, f0_h)
            nc.tensor.wait_ge(t2_out, w.up(t2_out, NB))
            nc.tensor.wait_ge(w_in, w.up(w_in, 96))
            for k in range(3 * NB):
                if k >= 6:
                    nc.tensor.wait_ge(qkv_out, w.up(qkv_out))
                proj_nat(f0_xT[:, :, k // 3, :], f0_w[:, :, k % 3 * 256:(k % 3 + 1) * 256], bank(k % 6)).then_inc(q_ps, 1)
            w.skip(qkv_out, 6)
            for b in w.loop(NB, "f0"):
                key_stacks_pe(w, f0)
                nc.tensor.wait_ge(qn_ready, w.up(qn_ready))
                q_stacks_pe(w, f0.QN)
                self_pe(w, f0)
                t2_pe(w, onat)
                nc.tensor.wait_ge(t2_out, w.up(t2_out))
                for o in range(2):
                    for c in range(2):
                        ins = nc.tensor.matmul(bank(0)[:, o * 256:(o + 1) * 256], f0_w[:, c, 768 + o * P:768 + (o + 1) * P],
                                               oT[:, c, :], start=(c == 0), stop=(c == 1))
                ins.then_inc(attn_ps, 1)
                nc.tensor.wait_ge(mod_sb, w.up(mod_sb))
                for j, src in enumerate((f0_aT, f0_hT)):
                    for c in range(2):
                        ins = nc.tensor.matmul(bank(1)[0:16, j * 256:(j + 1) * 256], f0_A[:, c, :], src[:, c, :],
                                               start=(c == 0), stop=(c == 1))
                ins.then_inc(mod_ps, 1)
                nc.tensor.wait_ge(mod_sb, w.up(mod_sb))
                for f in range(8):
                    if f >= 2:
                        nc.tensor.wait_ge(inter_ready, w.up(inter_ready))
                    gate, up = bank(2 + f % 2)[:, 0:256], bank(2 + f % 2)[:, 256:512]
                    for c in range(2):
                        nc.tensor.matmul(gate, f0_mlp[:, c, 0, f * P:(f + 1) * P], f0_hT[:, c, :], start=(c == 0), stop=False)
                    nc.tensor.matmul(gate, f0_B[0:16, f * P:(f + 1) * P], f0_mT[0:16, :], start=False, stop=True)
                    for c in range(2):
                        ins = nc.tensor.matmul(up, f0_mlp[:, c, 1, f * P:(f + 1) * P], f0_hT[:, c, :], start=(c == 0), stop=(c == 1))
                    ins.then_inc(gu_ps, 1)
                nc.tensor.wait_ge(inter_ready, w.up(inter_ready, 2))
                for i in range(2):
                    for f in range(8):
                        ins = nc.tensor.matmul(bank(0)[:, i * 256:(i + 1) * 256], f0_inter[:, f, i * P:(i + 1) * P], f0_down[:, f, :],
                                               start=(f == 0), stop=(f == 7))
                ins.then_inc(mlp_ps, 1)

        def f0_act(w):
            nc.scalar.wait_ge(phase_end, w.up(phase_end, 4))
            nc.scalar.wait_ge(ln_var, w.up(ln_var))
            nc.scalar.activation(all_std, all_mv[:, :, 1], ACT.Sqrt, bias=eps5).then_inc(ln_std, 1)
            nc.scalar.wait_ge(ln_var, w.up(ln_var))
            nc.scalar.activation(f0_std, f0_ss, ACT.Sqrt, bias=eps6, scale=1.0 / D).then_inc(ln_std, 1)
            norm_out_act(w, f0_xT)
            norm_out_act(w, f0_HT)
            for b in w.loop(NB, "f0"):
                self_keys_act(w, f0, lambda t: f0_kraw[:, t, :])
                q_stacks_act(w, f0.QT, f0.slots)
                self_act(w, f0)
                t2_act(w, oT)
                nc.scalar.wait_ge(attn_ps, w.up(attn_ps))
                nc.scalar.activation(f0_aT, bank(0).rearrange("p (c t) -> p c t", c=2), ACT.Copy).then_inc(mod_sb, 1)
                nc.scalar.wait_ge(mod_ps, w.up(mod_ps))
                nc.scalar.activation(f0_th[0:16, :], bank(1)[0:16, 0:256], ACT.Tanh).then_inc(silu_ready, 1)
                for f in range(8):
                    nc.scalar.wait_ge(gu_ps, w.up(gu_ps))
                    if f >= 2:
                        nc.scalar.wait_ge(inter_ready, w.up(inter_ready))
                    nc.scalar.activation(f0_sg[f % 2], bank(2 + f % 2)[:, 0:256], ACT.Silu).then_inc(silu_ready, 1)
                w.skip(inter_ready, 2)

        def f0_dve(w):
            for t in range(T8):
                ins = nc.vector.bn_stats(all6[:, t, :], X[:, t // 2, t % 2, :])
            link(w, ins)
            for t in range(T8):
                ins = nc.vector.bn_aggr(all_mv[:, t, :], all6[:, t, :])
            ins.then_inc(ln_var, 1)
            for buf in f0.KN:
                nc.vector.memset(buf, 0.0)
            nc.vector.memset(f0.QN, 0.0)
            nc.vector.memset(f0.V[:, :, :, 16:17], 1.0)
            link(w, nc.vector.memset(bank(6), 0.0))
            nc.vector.wait_ge(ln_std, w.up(ln_std))
            link(w, nc.vector.reciprocal(all_rstd, all_std))
            for t in range(T8):
                ins = nc.vector.tensor_scalar(f0_Z[:, t, :], X[:, t // 2, t % 2, :], all_mv[:, t, 0:1], all_rstd[:, t:t + 1],
                                              ALU.subtract, ALU.mult)
            link(w, ins)
            for t in range(T8):
                link(w, nc.vector.tensor_tensor_reduce(out=f0_sq, in0=f0_Z[:, t, :], in1=f0_Z[:, t, :], scale=1.0, scalar=0.0,
                                                       op0=ALU.mult, op1=ALU.add, accum_out=f0_ss[:, t:t + 1]))
            nc.vector.sem_inc(ln_var, 1)
            nc.vector.wait_ge(ln_std, w.up(ln_std))
            link(w, nc.vector.reciprocal(f0_rr, f0_std))
            nc.vector.wait_ge(w_in, w.up(w_in, 96))
            for k, dst in enumerate((f0_x1, f0_h)):
                for t in range(T8):
                    ins = nc.vector.scalar_tensor_tensor(out=dst[:, t, :], in0=f0_Z[:, t, :], scalar=f0_rr[:, t:t + 1],
                                                         in1=f0_v[:, k, :], op0=ALU.mult, op1=ALU.mult)
                    if t % 2:
                        ins.then_inc(t2_in, 1)
            w.skip(tr_full, 2 * NB)
            for b in range(NB):
                for j, dst in enumerate((f0_q, f0_k, f0_vv)):
                    nc.vector.wait_ge(q_ps, w.up(q_ps))
                    nc.vector.tensor_scalar(dst[:, b, :, :], bank((3 * b + j) % 6).rearrange("p (i d) -> p i d", i=2),
                                            (0.25, 1.0, 1.0)[j], None, ALU.mult).then_inc(qkv_out, 1)
            w.skip(qkv_out, 3 * NB)
            nc.vector.wait_ge(qkv_out, w.same(qkv_out))
            causal = cst[:, C_CAUSAL:C_CAUSAL + 512].rearrange("p (i k) -> p i k", i=2)
            for b in w.loop(NB, "f0"):
                w.settle(settled)
                nc.vector.tensor_copy(f0_kraw, f0_k[:, b, :, :])
                nc.vector.tensor_copy(f0.q, f0_q[:, b, :, :])
                nc.vector.tensor_copy(f0_hT, f0_HT[:, :, b, :])
                link(w, nc.vector.tensor_copy(f0.V[:, :, :, 0:16], f0_vv[:, b, :, :].rearrange("p i (h e) -> p i h e", h=16)))
                nc.vector.sem_inc(kn_ready, 2)
                self_keys_dve(w, f0, lambda t: f0_kraw[:, t, :], lambda: split_q(w, f0.q, f0.qr, f0.QNv, 16, 16))
                self_dve(w, f0, causal, lambda w, sx, g, v: link(w, nc.vector.tensor_tensor(
                    onat[:, :, g * 64:(g + 1) * 64].rearrange("p i (h e) -> p i h e", h=4), v[:, :, :, 0:16],
                    spread(sx.rec, 3, 16), ALU.mult)))
                nc.vector.sem_inc(t2_in, 1)
                w.skip(tr_full)
                nc.vector.wait_ge(mod_ps, w.up(mod_ps))
                nc.vector.wait_ge(silu_ready, w.up(silu_ready))
                nc.vector.scalar_tensor_tensor(out=f0_mT[0:16, :], in0=bank(1)[0:16, 256:512], scalar=0.1, in1=f0_th[0:16, :],
                                               op0=ALU.mult, op1=ALU.mult).then_inc(mod_sb, 1)
                link(w, nc.vector.tensor_tensor(X[:, b, :, :], X[:, b, :, :], f0_Z.rearrange("p (b i) d -> p b i d", i=2)[:, b, :, :], ALU.add))
                for f in range(8):
                    nc.vector.wait_ge(silu_ready, w.up(silu_ready))
                    nc.vector.tensor_tensor(f0_inter[:, f, :], f0_sg[f % 2], bank(2 + f % 2)[:, 256:512], ALU.mult).then_inc(inter_ready, 1)
                nc.vector.wait_ge(mlp_ps, w.up(mlp_ps))
                link(w, nc.vector.tensor_tensor(X[:, b, :, :], X[:, b, :, :], bank(0).rearrange("p (i d) -> p i d", i=2), ALU.add))
                nc.vector.sem_inc(phase_end, 1)

        a = Arena()
        x1_w = a.cut([2, 2 * D])
        x1_v = a.cut([3, D])
        x1_bin = a.cut([2])
        x1_scs = a.cut([2])
        x1_s = a.cut([2, NB])
        x1_sB = a.cut([2, NB, P])
        x1_y = a.cut([2, D])

        def x1_sp(sp, w):
            sp.wait_ge(phase_end, w.up(phase_end, 4))
            sp.dma_start(x1_w, d["w_x1"]).then_inc(w_in, 16)
            sp.dma_start(x1_v.rearrange("p n d -> p (n d)"), d["v_x1"].partition_broadcast(P)).then_inc(w_in, 16)
            sp.dma_start(x1_bin, d["bin_x1"]).then_inc(w_in, 16)

        def x1_pe(w):
            nc.tensor.wait_ge(phase_end, w.up(phase_end, 4))
            nc.tensor.wait_ge(w_in, w.up(w_in, 48))
            for o in range(2):
                for c in range(2):
                    ins = nc.tensor.matmul(bank(0)[:, o * NB:(o + 1) * NB], x1_w[:, c, o * P:(o + 1) * P], cw[:, :, c],
                                           start=(c == 0), stop=(c == 1))
            ins.then_inc(sum_ps, 1)
            nc.tensor.wait_ge(sum_sb, w.up(sum_sb))
            for b in range(NB):
                for c in range(2):
                    ins = nc.tensor.matmul(bank(1 + b // 2)[:, b % 2 * 256:b % 2 * 256 + 256], x1_sB[:, c, b, :], x1_w[:, c, D:2 * D],
                                           start=(c == 0), stop=(c == 1))
            ins.then_inc(sum_ps, 1)

        def x1_act(w):
            nc.scalar.wait_ge(phase_end, w.up(phase_end, 4))
            for b in w.loop(NB, "x1"):
                ln_act(w)
                ln_act(w)

        def x1_dve(w):
            nc.vector.wait_ge(w_in, w.up(w_in, 48))
            nc.vector.wait_ge(sum_ps, w.up(sum_ps))
            link(w, nc.vector.tensor_scalar(x1_scs, x1_bin, csum[:, 0:1], None, ALU.mult))
            for o in range(2):
                link(w, nc.vector.tensor_scalar(x1_s[:, o, :], bank(0)[:, o * NB:(o + 1) * NB], x1_scs[:, o:o + 1], 1.0 / CTX,
                                                ALU.add, ALU.mult))
            nc.vector.tensor_copy(x1_sB, spread(x1_s, 3, P)).then_inc(sum_sb, 1)
            nc.vector.wait_ge(sum_ps, w.up(sum_ps))
            for b in w.loop(NB, "x1"):
                ln_dve(w, b)
                link(w, nc.vector.tensor_tensor(x1_y, z, spread(PS[:, 1:3, :].rearrange("p a (b d) -> p (a b) d", b=2)[:, b, :], 1, 2), ALU.add))
                link(w, nc.vector.tensor_tensor(x1_y, x1_y, spread(x1_v[:, 0, :], 1, 2), ALU.add))
                ln_dve(w, b, dst=z, src=x1_y)
                link(w, nc.vector.tensor_tensor(z, z, spread(x1_v[:, 1, :], 1, 2), ALU.mult))
                link(w, nc.vector.tensor_tensor(z, z, spread(x1_v[:, 2, :], 1, 2), ALU.add))
                link(w, nc.vector.tensor_tensor(X[:, b, :, :], X[:, b, :, :], z, ALU.add))
                nc.vector.sem_inc(phase_end, 1)

        class Experts:

            def __init__(self, name):
                self.name = name
                self.up, self.chunks, self.E = FFNS[name]
                a = Arena()
                self.hT = a.cut([2, NB, S])
                self.slot = [a.cut([7, P]) for _ in range(2)]
                self.router = a.cut([2, self.E])
                self.stacks = 2 if name == "f1" else 1
                self.WN = a.cut([T8, 2, P], BF16)
                self.WT = a.cut([self.stacks, T8 * P], BF16)
                self.W = a.cut([T8, self.E])
                self.Wr = a.cut([T8, self.E])
                self.bias = a.cut([16])
                n = 64 if name == "f1" else 18
                self.lg, self.ex, self.mr, self.sel = (a.cut([T8, n]) for _ in range(4))
                self.m8 = a.cut([T8, 8])
                self.shared, self.ws, self.rs = a.cut([T8]), a.cut([T8]), a.cut([T8])
                self.gp, self.gr, self.g8 = a.cut([T8, 10]), a.cut([T8, 10]), a.cut([T8, 8])
                self.pr = a.cut([T8, 8, 2])
                self.Z = a.cut([T8, D])
                self.sg = [a.cut([512]) for _ in range(2)]
                self.su = a.cut([512])
                self.inter = [a.cut([512]) for _ in range(2)]
                self.zeros = a.cut([512], BF16)

        def ffn_sp(sp, w, f):
            sp.wait_ge(phase_end, w.up(phase_end, 4))
            sp.dma_start(f.router, d["router_" + f.name]).then_inc(w_in, 16)
            if f.name == "f3":
                sp.dma_start(f.bias, d["bias_f3"].partition_broadcast(P)).then_inc(w_in, 16)
            src = d["chunks_" + f.name]
            for c in range(2):
                sp.dma_start(f.slot[c], src[c]).then_inc(wc_in[c], 16)
            sp.wait_ge(down_ps, w.up(down_ps, 2))
            sp.dma_start(f.slot[0], src[2]).then_inc(wc_in[0], 16)
            for j in w.loop((f.chunks - 3) // 2, f.name + "w"):
                for k in range(2):
                    sp.wait_ge(down_ps, w.up(down_ps, 2))
                    sp.dma_start(f.slot[1 - k], src[2 * j + 3 + k]).then_inc(wc_in[1 - k], 16)
            w.skip(down_ps, 4)

        def ffn_pe(w, f):
            nc.tensor.wait_ge(phase_end, w.up(phase_end, 4))
            nc.tensor.wait_ge(w_in, w.up(w_in, 32 if f.name == "f3" else 16))
            norm_pe(w, f.Z)
            for b in range(NB):
                nc.tensor.wait_ge(t2_out, w.up(t2_out))
                for i in range(2):
                    t = 2 * b + i
                    for c in range(2):
                        ins = nc.tensor.matmul(bank(t // 4)[:, t % 4 * P:t % 4 * P + f.E], f.hT[:, c, b, i * P:(i + 1) * P], f.router[:, c, :],
                                               start=(c == 0), stop=(c == 1))
            ins.then_inc(logits_ps, 1)
            nc.tensor.wait_ge(wt_ready, w.up(wt_ready))
            for k in range(f.stacks):
                for t in range(T8):
                    ins = nc.tensor.transpose(bank16(5 + k)[:, t * P:(t + 1) * P], f.WN[:, t, k, :], identb)
            ins.then_inc(tr_full, 1)
            nc.tensor.wait_ge(t2_out, w.up(t2_out))

            def unit(s, hf, lag):
                rhs = [f.hT[:, c, 2 * hf:2 * hf + 2, :] for c in range(2)]
                for c in range(2):
                    ins = nc.tensor.matmul(bank(hf), f.slot[s][:, c, :], rhs[c], start=(c == 0), stop=(c == 1))
                ins.then_inc(gu_ps, 1)
                if lag:
                    nc.tensor.wait_ge(inter_ready, w.up(inter_ready))
                if f.up:
                    for c in range(2):
                        nc.tensor.matmul(bank(2), f.slot[s][:, 2 + c, :], rhs[c], start=(c == 0), stop=(c == 1))
                pick = f.slot[s][:, 6, :].bitcast(BF16)
                for k in range(f.stacks):
                    ins = nc.tensor.matmul(bank(3), pick[:, k * P:(k + 1) * P], f.WT[:, k, hf * 512:(hf + 1) * 512],
                                           start=(k == 0), stop=(k == f.stacks - 1))
                ins.then_inc(route_ps, 1)
                if lag:
                    lag()

            def down(s, hf):
                for j in range(4):
                    t = 4 * hf + j
                    ins = nc.tensor.matmul(bank(4 + t // 2)[:, t % 2 * 256:t % 2 * 256 + 256], f.inter[hf][:, j * P:(j + 1) * P],
                                           f.slot[s][:, 4:6, :], start=False, stop=False, skip_group_check=True)
                ins.then_inc(down_ps, 1)

            for k in range(4):
                nc.tensor.matmul(bank(4 + k), f.zeros[:, 0:P], f.zeros, start=True, stop=False, skip_group_check=True)
            nc.tensor.wait_ge(wc_in[0], w.up(wc_in[0], 16))
            unit(0, 0, None)
            unit(0, 1, lambda: down(0, 0))
            for j in w.loop((f.chunks - 1) // 2, f.name + "c"):
                nc.tensor.wait_ge(wc_in[1], w.up(wc_in[1], 16))
                unit(1, 0, lambda: down(0, 1))
                unit(1, 1, lambda: down(1, 0))
                nc.tensor.wait_ge(wc_in[0], w.up(wc_in[0], 16))
                unit(0, 0, lambda: down(1, 1))
                unit(0, 1, lambda: down(0, 0))
            nc.tensor.wait_ge(inter_ready, w.up(inter_ready))
            down(0, 1)

        def ffn_act(w, f):
            nc.scalar.wait_ge(phase_end, w.up(phase_end, 4))
            norm_act(w, f.hT)
            if f.name == "f3":
                nc.scalar.wait_ge(logits_ps, w.up(logits_ps))
                nc.scalar.activation(f.ex[:, :, 0:16], logits_of(16), ACT.Exp, scale=-1.0).then_inc(route_exp, 1)
            else:
                n = f.E - 1
                nc.scalar.wait_ge(route_in, w.up(route_in))
                if f.name == "f1":
                    nc.scalar.activation(f.ws, f.shared, ACT.Exp, scale=-1.0)
                nc.scalar.activation(f.ex[:, :, 0:n], f.ex[:, :, 0:n], ACT.Exp).then_inc(route_exp, 1)
                w.skip(logits_ps)
            nc.scalar.wait_ge(tr_full, w.up(tr_full))
            src = PS[:, 5:5 + f.stacks, :].rearrange("p k t -> p (k t)").bitcast(BF16)
            nc.scalar.activation(f.WT.rearrange("p k t -> p (k t)"), src, ACT.Copy).then_inc(t2_out, 1)
            w.skip(t2_out)

            def silu(hf, wait=True):
                nc.scalar.wait_ge(gu_ps, w.up(gu_ps))
                if wait:
                    nc.scalar.wait_ge(inter_ready, w.up(inter_ready))
                nc.scalar.activation(f.sg[hf], bank(hf), ACT.Silu).then_inc(silu_ready, 1)

            silu(0, False)
            silu(1, False)
            for j in w.loop((f.chunks - 1) // 2, f.name + "c"):
                for hf in (0, 1, 0, 1):
                    silu(hf)
            w.skip(inter_ready, 2)

        def logits_of(n):
            return PS[:, 0:2, :].rearrange("p a (t e) -> p (a t) e", t=4)[:, :, 0:n]

        def ffn_route(w, f):
            n, top = {"f1": (64, 8), "f2": (8, 2), "f3": (16, 6)}[f.name]
            if f.name == "f3":
                nc.vector.wait_ge(route_exp, w.up(route_exp))
                link(w, nc.vector.tensor_scalar(f.sel[:, :, 0:16], f.ex[:, :, 0:16], 1.0, None, ALU.add))
                link(w, nc.vector.reciprocal(f.ex[:, :, 0:16], f.sel[:, :, 0:16]))
                link(w, nc.vector.tensor_tensor(f.lg[:, :, 0:16], f.ex[:, :, 0:16], spread(f.bias, 1, T8), ALU.add))
                q = f.lg[:, :, 0:16].rearrange("p i (a b) -> p i a b", b=2)
                link(w, nc.vector.tensor_tensor(f.pr[:, :, :, 0], q[:, :, :, 0], q[:, :, :, 1], ALU.max))
                link(w, nc.vector.tensor_tensor(f.pr[:, :, :, 1], q[:, :, :, 0], q[:, :, :, 1], ALU.min))
                hi = f.pr[:, :, :, 0].rearrange("p i (g b) -> p i g b", b=2)
                lo = f.pr[:, :, :, 1].rearrange("p i (g b) -> p i g b", b=2)
                link(w, nc.vector.tensor_tensor(f.mr[:, :, 0:4], hi[:, :, :, 0], hi[:, :, :, 1], ALU.max))
                link(w, nc.vector.tensor_tensor(f.mr[:, :, 4:8], hi[:, :, :, 0], hi[:, :, :, 1], ALU.min))
                link(w, nc.vector.tensor_tensor(f.mr[:, :, 8:12], lo[:, :, :, 0], lo[:, :, :, 1], ALU.max))
                link(w, nc.vector.tensor_tensor(f.mr[:, :, 4:8], f.mr[:, :, 4:8], f.mr[:, :, 8:12], ALU.max))
                link(w, nc.vector.tensor_tensor(f.gp[:, :, 0:4], f.mr[:, :, 0:4], f.mr[:, :, 4:8], ALU.add))
                for t in range(T8):
                    ins = nc.vector.max(f.g8[:, t, :], f.gp[:, t, :])
                link(w, ins)
                link(w, nc.vector.memset(f.g8[:, :, 2:8], -1e30))
                for t in range(T8):
                    ins = nc.vector.match_replace(f.gr[:, t, :], f.g8[:, t, :], f.gp[:, t, :], -3e38)
                link(w, ins)
                link(w, nc.vector.tensor_tensor(f.gr[:, :, 0:4], f.gr[:, :, 0:4], f.gp[:, :, 0:4], ALU.is_lt))
                lg4 = f.lg[:, :, 0:16].rearrange("p i (g b) -> p i g b", b=4)
                link(w, nc.vector.tensor_tensor(lg4, lg4, spread(f.gr[:, :, 0:4], 3, 4), ALU.mult))
                link(w, nc.vector.tensor_scalar(f.lg[:, :, 0:16], f.lg[:, :, 0:16], 0.0, None, ALU.add))
            else:
                link(w, nc.vector.tensor_copy(f.lg[:, :, 0:n], logits_of(n)))
                if f.name == "f1":
                    nc.vector.tensor_copy(f.shared, logits_of(f.E)[:, :, n])
            for t in range(T8):
                ins = nc.vector.max(f.m8[:, t, :], f.lg[:, t, 0:n])
            link(w, ins)
            if f.name != "f3":
                nc.vector.tensor_tensor(f.ex[:, :, 0:n], f.lg[:, :, 0:n], spread(f.m8[:, :, 0], 2, n), ALU.subtract).then_inc(route_in, 1)
            if top < 8:
                link(w, nc.vector.memset(f.m8[:, :, top:8], -1e30))
            for t in range(T8):
                ins = nc.vector.match_replace(f.mr[:, t, :], f.m8[:, t, :], f.lg[:, t, :], -3e38)
            link(w, ins)
            link(w, nc.vector.tensor_tensor(f.sel[:, :, 0:n], f.mr[:, :, 0:n], f.lg[:, :, 0:n], ALU.is_lt))
            if f.name != "f3":
                nc.vector.wait_ge(route_exp, w.up(route_exp))
            if f.name == "f1":
                link(w, nc.vector.tensor_scalar(f.rs, f.ws, 1.0, None, ALU.add))
                link(w, nc.vector.reciprocal(f.W[:, :, n], f.rs))
            link(w, nc.vector.tensor_tensor(f.mr[:, :, 0:n], f.ex[:, :, 0:n], f.sel[:, :, 0:n], ALU.mult))
            link(w, nc.vector.tensor_reduce(f.ws, f.mr[:, :, 0:n], AX.X, ALU.add))
            if f.name == "f3":
                link(w, nc.vector.tensor_scalar(f.ws, f.ws, 1e-20, None, ALU.add))
            link(w, nc.vector.reciprocal(f.rs, f.ws))
            if f.name == "f3":
                link(w, nc.vector.tensor_scalar(f.rs, f.rs, 2.5, None, ALU.mult))
            link(w, nc.vector.tensor_tensor(f.W[:, :, 0:n], f.mr[:, :, 0:n], spread(f.rs, 2, n), ALU.mult))
            E = f.E
            if f.name == "f1":
                parts = [[(f.WN[:, :, 0, 0:n], 0, n), (f.WN[:, :, 1, n:n + 1], n, E)],
                         [(f.WN[:, :, 0, n:2 * n], 0, n), (f.WN[:, :, 1, n + 1:n + 2], n, E)],
                         [(f.WN[:, :, 1, 0:n], 0, n), (f.WN[:, :, 1, n + 2:n + 3], n, E)]]
            else:
                parts = [[(f.WN[:, :, 0, j * E:(j + 1) * E], 0, E)] for j in range(3)]
            for j, part in enumerate(parts):
                src = f.Wr if j else f.W
                for dst, lo, hi in part:
                    ins = nc.vector.tensor_copy(dst, src[:, :, lo:hi])
                link(w, ins)
                if j < 2:
                    for dst, lo, hi in part:
                        ins = nc.vector.tensor_tensor(f.Wr[:, :, lo:hi], src[:, :, lo:hi], dst, ALU.subtract)
                    link(w, ins)
            nc.vector.sem_inc(wt_ready, 1)

        def ffn_dve(w, f):
            nc.vector.memset(f.lg, -1e30)
            nc.vector.memset(f.gp, -1e30)
            nc.vector.memset(f.W, 1.0)
            nc.vector.memset(f.WN, 0.0)
            link(w, nc.vector.memset(f.zeros, 0.0))
            nc.vector.wait_ge(w_in, w.up(w_in, 32 if f.name == "f3" else 16))
            norm_dve(w, f.Z)
            w.skip(tr_full)
            nc.vector.wait_ge(logits_ps, w.up(logits_ps))
            ffn_route(w, f)

            def gated(hf):
                nc.vector.wait_ge(silu_ready, w.up(silu_ready))
                nc.vector.wait_ge(route_ps, w.up(route_ps))
                src = f.sg[hf]
                if f.up:
                    link(w, nc.vector.tensor_tensor(f.su, f.sg[hf], bank(2), ALU.mult))
                    src = f.su
                nc.vector.tensor_tensor(f.inter[hf], src, bank(3), ALU.mult).then_inc(inter_ready, 1)

            gated(0)
            gated(1)
            for j in w.loop((f.chunks - 1) // 2, f.name + "c"):
                for hf in (0, 1, 0, 1):
                    nc.vector.wait_ge(down_ps, w.up(down_ps))
                    gated(hf)
            nc.vector.wait_ge(down_ps, w.up(down_ps, 2))
            for b in range(NB):
                link(w, nc.vector.tensor_tensor(X[:, b, :, :], X[:, b, :, :], bank(4 + b).rearrange("p (i d) -> p i d", i=2), ALU.add))
                nc.vector.sem_inc(phase_end, 1)

        ffns = {name: Experts(name) for name in FFNS}

        a = Arena()
        x2 = Ctx(a, 8, CTX_TILES, L2_SPANS)
        x2s = Self(a, 8, x2)
        x2_ctxT = a.cut([2, CTX])
        x2_w = a.cut([2, 4 * 256])
        x2_mask = a.cut([2, S])
        x2_q, x2_k, x2_v = (a.cut([NB, 2, D]) for _ in range(3))
        x2_Z = x2.kT.rearrange("p s t -> p (s t)").bitcast(F32)
        x2_ZT = x2_Z[:, T8 * D:2 * T8 * D].rearrange("p (c b t) -> p c b t", c=2, b=NB)
        x2_Z = x2_Z[:, 0:T8 * D].rearrange("p (t d) -> p t d", t=T8)
        x2_gate, x2_tg = a.cut([32]), a.cut([32])
        cos = cst[:, C_COS:C_COS + 16].rearrange("p (i e) -> p i e", i=2)
        sin = cst[:, C_SIN:C_SIN + 16].rearrange("p (i e) -> p i e", i=2)

        def x2_sp(sp, w):
            sp.wait_ge(phase_end, w.up(phase_end, 4))
            sp.dma_start(x2_w, d["w_x2"]).then_inc(w_in, 16)
            sp.dma_start(x2_gate, d["gate_x2"].partition_broadcast(P)).then_inc(gate_w, 16)
            for b in w.loop(NB, "x2"):
                sp.wait_ge(mask_used, w.up(mask_used))
                sp.dma_start(x2_mask, d["mask"][b]).then_inc(mask_in, 16)
                sp.wait_ge(ctx_used, w.up(ctx_used))
                sp.dma_start(x2_ctxT, d["ctxT"][b]).then_inc(ctx_in, 16)

        def x2_pe(w):
            nc.tensor.wait_ge(phase_end, w.up(phase_end, 4))
            norm_pe(w, x2_Z)
            nc.tensor.wait_ge(w_in, w.up(w_in, 16))
            nc.tensor.wait_ge(t2_out, w.up(t2_out, NB))
            for k in range(3 * NB):
                if k >= 6:
                    nc.tensor.wait_ge(qkv_out, w.up(qkv_out))
                proj_nat(x2_ZT[:, :, k // 3, :], x2_w[:, :, k % 3 * 256:(k % 3 + 1) * 256], bank(k % 6)).then_inc(q_ps, 1)
            w.skip(qkv_out, 6)
            for b in w.loop(NB, "x2"):
                key_stacks_pe(w, x2s)
                nc.tensor.wait_ge(qn_ready, w.up(qn_ready))
                q_stacks_pe(w, x2.QN)
                self_pe(w, x2s)
                keys_pe(w, x2, x2_ctxT, lambda t: x2_w[:, :, 256:768], stacks=True)
                att_pe(w, x2, first=False)
                t2_pe(w, onat)
                nc.tensor.wait_ge(t2_out, w.up(t2_out))
                proj_nat(oT, x2_w[:, :, 768:1024], bank(0)).then_inc(proj_ps, 1)

        def x2_act(w):
            nc.scalar.wait_ge(phase_end, w.up(phase_end, 4))
            nc.scalar.wait_ge(gate_w, w.up(gate_w, 16))
            nc.scalar.activation(x2_tg, x2_gate, ACT.Tanh).then_inc(gate_ready, 1)
            norm_act(w, x2_ZT)
            for b in w.loop(NB, "x2"):
                self_keys_act(w, x2s, lambda t: x2.kn[t])
                q_stacks_act(w, x2.QT, x2.slots)
                self_act(w, x2s)
                keys_act(w, x2, lambda t: x2.kn[t % 2])
                att_act(w, x2)
                t2_act(w, oT)

        def x2_finish_self(w, sx, g, v):
            link(w, nc.vector.tensor_tensor(onat[:, :, g * 32:(g + 1) * 32].rearrange("p i (h e) -> p i h e", h=4),
                                            v[:, :, :, 0:8], spread(sx.rec, 3, 8), ALU.mult))

        def x2_finish(w, cx, g, u):
            link(w, nc.vector.tensor_tensor(cx.rec, cx.rec, spread(x2_tg[:, 4 * g:4 * g + 4], 1, 2), ALU.mult))
            link(w, nc.vector.tensor_tensor(cx.tmp, u[:, :, :, 0:8], spread(cx.rec, 3, 8), ALU.mult))
            o = onat[:, :, g * 32:(g + 1) * 32]
            link(w, nc.vector.tensor_tensor(o, o, cx.tmp.rearrange("p i h e -> p i (h e)"), ALU.add))

        def rope(w, dst, ps):
            v = ps.rearrange("p (i h e) -> p i h e", i=2, h=32)
            o = dst.rearrange("p i (h e) -> p i h e", h=32)
            r = x2.qr.rearrange("p i (h e) -> p i h e", h=32)
            link(w, nc.vector.tensor_tensor(o, v, spread(cos, 2, 32), ALU.mult))
            link(w, nc.vector.tensor_tensor(r[:, :, :, 0:4], v[:, :, :, 4:8], spread(sin[:, :, 0:4], 2, 32), ALU.mult))
            link(w, nc.vector.tensor_tensor(r[:, :, :, 4:8], v[:, :, :, 0:4], spread(sin[:, :, 4:8], 2, 32), ALU.mult))
            link(w, nc.vector.tensor_tensor(dst, dst, x2.qr, ALU.add))

        def x2_dve(w):
            norm_dve(w, x2_Z)
            for buf in x2.KN + [x2.QN, x2.QT] + x2.QTm:
                link(w, nc.vector.memset(buf, 0.0))
            for kv in x2.KNv:
                link(w, nc.vector.memset(kv[:, :, 48:51], 1.0))
            nc.vector.memset(x2.V[:, :, :, 8:9], 1.0)
            nc.vector.memset(x2s.V[:, :, :, 8:9], 1.0)
            nc.vector.wait_ge(gate_ready, w.up(gate_ready))
            nc.vector.wait_ge(w_in, w.up(w_in, 16))
            for b in range(NB):
                for j, dst in enumerate((x2_q, x2_k, x2_v)):
                    nc.vector.wait_ge(q_ps, w.up(q_ps))
                    ps = bank((3 * b + j) % 6)
                    if j < 2:
                        rope(w, dst[:, b, :, :], ps)
                    else:
                        link(w, nc.vector.tensor_copy(dst[:, b, :, :], ps.rearrange("p (i d) -> p i d", i=2)))
                    nc.vector.sem_inc(qkv_out, 1)
            link(w, nc.vector.tensor_scalar(x2_q, x2_q, 8.0 ** -0.5, None, ALU.mult))
            link(w, nc.vector.memset(bank(6), 0.0))
            for b in w.loop(NB, "x2"):
                w.settle(settled)
                for t in range(2):
                    nc.vector.tensor_copy(x2.kn[t], x2_k[:, b, t, :])
                nc.vector.tensor_copy(x2.q, x2_q[:, b, :, :])
                link(w, nc.vector.tensor_copy(x2s.V[:, :, :, 0:8], x2_v[:, b, :, :].rearrange("p i (h e) -> p i h e", h=32)))
                nc.vector.sem_inc(kn_ready, 2)
                nc.vector.wait_ge(mask_in, w.up(mask_in, 16))
                link(w, nc.vector.tensor_scalar(x2_mask, x2_mask, LOWEST, None, ALU.max))

                def q_part():
                    link(w, nc.vector.memset(x2.QNv[:, :, :, 48:51], 0.0))
                    split_q(w, x2.q, x2.qr, x2.QNv, 32, 8)

                self_keys_dve(w, x2s, lambda t: x2.kn[t], q_part)
                self_dve(w, x2s, x2_mask, x2_finish_self)
                nc.vector.sem_inc(mask_used, 1)

                def make(t):
                    k0, n = x2.tiles[t]
                    nc.vector.wait_ge(kv_ps, w.up(kv_ps))
                    nc.vector.tensor_copy(x2.kn[t % 2][:n, :], bank(t % 3)[:n, 0:256]).then_inc(kn_ready, 1)
                    nc.vector.tensor_copy(x2.V[:n, t, :, 0:8], bank(t % 3)[:n, 256:512].rearrange("p (h e) -> p h e", h=32)).then_inc(kv_free, 1)

                keys_dve(w, x2, make, lambda t: x2.kn[t % 2])
                nc.vector.sem_inc(ctx_used, 1)
                att_dve(w, x2, x2_finish)
                nc.vector.sem_inc(t2_in, 1)
                w.skip(tr_full)
                nc.vector.wait_ge(proj_ps, w.up(proj_ps))
                link(w, nc.vector.tensor_tensor(X[:, b, :, :], X[:, b, :, :], bank(0).rearrange("p (i d) -> p i d", i=2), ALU.add))
                nc.vector.sem_inc(phase_end, 1)

        a = Arena()
        x3_ctxT = a.cut([2, CTX])
        x3_w = a.cut([2, 5 * 256])
        x3_bg = a.cut([D])
        x3_qT, x3_qe, x3_qm = a.cut([2, S]), a.cut([2, S]), a.cut([2, S])
        x3_g, x3_ge = a.cut([2, D]), a.cut([2, D])
        x3_ke = [a.cut([D]) for _ in range(2)]
        x3_kmin = [a.cut([D]) for _ in range(2)]
        x3_km = [a.cut([D]) for _ in range(2)]
        x3_vm = [a.cut([2, P + 1]) for _ in range(2)]
        x3_S = a.cut([2, P + 8])
        x3_rec = a.cut([2, 16])
        x3_Z, x3_ZT = a.cut([T8, D]), a.cut([2, NB, S])

        def x3_sp(sp, w):
            sp.wait_ge(phase_end, w.up(phase_end, 4))
            sp.dma_start(x3_w, d["w_x3"]).then_inc(w_in, 16)
            sp.dma_start(x3_bg, d["bg_x3"].partition_broadcast(P)).then_inc(w_in, 16)
            for b in w.loop(NB, "x3"):
                sp.wait_ge(ctx_used, w.up(ctx_used))
                sp.dma_start(x3_ctxT, d["ctxT"][b]).then_inc(ctx_in, 16)

        def x3_pe(w):
            nc.tensor.wait_ge(phase_end, w.up(phase_end, 4))
            norm_pe(w, x3_Z)
            w.skip(t2_out, NB)
            nc.tensor.wait_ge(w_in, w.up(w_in, 32))
            for b in w.loop(NB, "x3"):
                nc.tensor.wait_ge(t2_in, w.up(t2_in))
                for o in range(2):
                    for c in range(2):
                        ins = nc.tensor.matmul(bank(0)[:, o * 256:(o + 1) * 256], x3_w[:, c, o * P:(o + 1) * P], zT[:, c, :],
                                               start=(c == 0), stop=(c == 1))
                ins.then_inc(q_ps, 1)
                proj_nat(zT, x3_w[:, :, 256:512], bank(1)).then_inc(q_ps, 1)
                nc.tensor.wait_ge(ctx_in, w.up(ctx_in, 16))

                def summary(t):
                    n = CTX_TILES[t][1]
                    nc.tensor.wait_ge(km_ready, w.up(km_ready))
                    if n < P:
                        w.settle(settled)
                    for c in range(2):
                        ins = nc.tensor.matmul(bank(4 + c)[:, 0:P + 1], x3_km[t % 2][:n, c * P:(c + 1) * P], x3_vm[t % 2][:n, c, :],
                                               start=(t == 0), stop=(t == len(CTX_TILES) - 1))
                    ins.then_inc(ks_ps, 1)

                nc.tensor.wait_ge(gate_in, w.up(gate_in))
                for t, (k0, n) in enumerate(CTX_TILES):
                    for j, to in enumerate((2 + t % 2, (0, 6)[t % 2])):
                        for c in range(2):
                            ins = nc.tensor.matmul(bank(to)[:n, 0:256], x3_ctxT[:, c, k0:k0 + n], x3_w[:, c, 512 + 256 * j:768 + 256 * j],
                                                   start=(c == 0), stop=(c == 1))
                        ins.then_inc((kv_ps, v_ps)[j], 1)
                    if t:
                        summary(t - 1)
                summary(len(CTX_TILES) - 1)
                nc.tensor.wait_ge(sum_sb, w.up(sum_sb))
                for i in range(2):
                    for c in range(2):
                        ins = nc.tensor.matmul(bank((6, 0)[i])[:, c * 136:(c + 1) * 136], x3_qT[:, c, i * P:(i + 1) * P], x3_S[:, c, :],
                                               start=True, stop=True)
                ins.then_inc(sum_ps, 1)
                t2_pe(w, onat)
                nc.tensor.wait_ge(t2_out, w.up(t2_out))
                proj_nat(oT, x3_w[:, :, 1024:1280], bank(1)).then_inc(proj_ps, 1)

        def x3_act(w):
            nc.scalar.wait_ge(phase_end, w.up(phase_end, 4))
            norm_act(w, x3_ZT)
            nc.scalar.wait_ge(t2_out, w.same(t2_out))
            nc.scalar.sem_inc(norm_out, 1)
            for b in w.loop(NB, "x3"):
                nc.scalar.wait_ge(fm_in, w.up(fm_in))
                nc.scalar.activation(x3_qe, x3_qm, ACT.Exp).then_inc(fm_exp, 1)
                nc.scalar.wait_ge(gate_in, w.up(gate_in))
                nc.scalar.activation(x3_ge, x3_g, ACT.Exp, scale=-1.0).then_inc(gate_ready, 1)
                for t, (k0, n) in enumerate(CTX_TILES):
                    nc.scalar.wait_ge(v_ps, w.up(v_ps))
                    nc.scalar.wait_ge(ks_ps, w.up(ks_ps))
                    link(w, nc.scalar.activation(x3_vm[t % 2][:n, :, 0:P], bank((0, 6)[t % 2])[:n, 0:256].rearrange("p (c e) -> p c e", c=2), ACT.Copy))
                    nc.scalar.wait_ge(fm_in, w.up(fm_in))
                    nc.scalar.activation(x3_ke[t % 2][:n, :], x3_kmin[t % 2][:n, :], ACT.Exp).then_inc(fm_exp, 1)
                t2_act(w, oT)

        def x3_dve(w):
            norm_dve(w, x3_Z)
            for v in x3_vm:
                link(w, nc.vector.memset(v, 1.0))
            nc.vector.wait_ge(w_in, w.up(w_in, 32))
            blk = cst[:, C_BLK:C_BLK + 8]
            nc.vector.wait_ge(norm_out, w.up(norm_out))
            for b in w.loop(NB, "x3"):
                w.settle(settled)
                nc.vector.tensor_copy(zT, x3_ZT[:, :, b, :]).then_inc(t2_in, 1)
                nc.vector.wait_ge(q_ps, w.up(q_ps))
                qps = bank(0).rearrange("p (c t) -> p c t", c=2)
                nc.vector.tensor_scalar(x3_qm, qps, 0.0, None, ALU.min).then_inc(fm_in, 1)
                nc.vector.wait_ge(fm_exp, w.up(fm_exp))
                link(w, nc.vector.scalar_tensor_tensor(out=x3_qT, in0=qps, scalar=1.0, in1=x3_qe, op0=ALU.add, op1=ALU.max))
                nc.vector.wait_ge(q_ps, w.up(q_ps))
                nc.vector.tensor_tensor(x3_g, bank(1).rearrange("p (i d) -> p i d", i=2), spread(x3_bg, 1, 2), ALU.add).then_inc(gate_in, 1)
                nc.vector.wait_ge(gate_ready, w.up(gate_ready))
                link(w, nc.vector.tensor_scalar(x3_g, x3_ge, 1.0, None, ALU.add))
                link(w, nc.vector.reciprocal(x3_g, x3_g))

                def feature(t):
                    n = CTX_TILES[t][1]
                    nc.vector.wait_ge(fm_exp, w.up(fm_exp))
                    nc.vector.wait_ge(ks_ps, w.up(ks_ps))
                    nc.vector.scalar_tensor_tensor(out=x3_km[t % 2][:n, :], in0=bank(2 + t % 2)[:n, 0:256], scalar=1.0,
                                                   in1=x3_ke[t % 2][:n, :], op0=ALU.add, op1=ALU.max).then_inc(km_ready, 1)

                for t, (k0, n) in enumerate(CTX_TILES):
                    nc.vector.wait_ge(kv_ps, w.up(kv_ps))
                    nc.vector.tensor_scalar(x3_kmin[t % 2][:n, :], bank(2 + t % 2)[:n, 0:256], 0.0, None, ALU.min).then_inc(fm_in, 1)
                    feature(t)
                nc.vector.sem_inc(ctx_used, 1)
                nc.vector.wait_ge(ks_ps, w.same(ks_ps, 2))
                for c in range(2):
                    link(w, nc.vector.tensor_tensor(x3_S[:, c, 0:P], bank(4 + c)[:, 0:P], cst[:, C_BMASK:C_BMASK + P], ALU.mult))
                    link(w, nc.vector.tensor_scalar(x3_S[:, c, P:P + 8], blk, bank(4 + c)[:, P:P + 1], None, ALU.mult))
                nc.vector.sem_inc(sum_sb, 1)
                nc.vector.wait_ge(sum_ps, w.up(sum_ps))
                for i in range(2):
                    v = bank((6, 0)[i])[:, 0:272].rearrange("p (c e) -> p c e", c=2)
                    rec = x3_rec[:, i, :]
                    rc = rec.rearrange("p (c h) -> p c h", c=2)
                    link(w, nc.vector.tensor_scalar(rc, v[:, :, P:P + 8], 1e-6, None, ALU.add))
                    link(w, nc.vector.reciprocal(rec, rec))
                    link(w, nc.vector.tensor_tensor(onat[:, i, :].rearrange("p (c h e) -> p c h e", c=2, h=8),
                                                    v[:, :, 0:P].rearrange("p c (h e) -> p c h e", h=8),
                                                    spread(rc, 3, 16), ALU.mult))
                link(w, nc.vector.tensor_tensor(onat, onat, x3_g, ALU.mult))
                nc.vector.sem_inc(t2_in, 1)
                w.skip(tr_full)
                nc.vector.wait_ge(proj_ps, w.up(proj_ps))
                link(w, nc.vector.tensor_tensor(X[:, b, :, :], X[:, b, :, :], bank(1).rearrange("p (i d) -> p i d", i=2), ALU.add))
                nc.vector.sem_inc(phase_end, 1)

        with nc.Block() as block:
            @block.sync
            def _(sp):
                w = Counts(sp, "sp", steps)
                sp.dma_start(cst, d["consts"]).then_inc(consts_in, 16)
                for b in range(NB):
                    sp.dma_start(X[:, b, :, :], d["x"][b].rearrange("(i p) d -> p i d", p=P)).then_inc(consts_in, 16)
                x0_sp(sp, w)
                f0_sp(sp, w)
                x1_sp(sp, w)
                ffn_sp(sp, w, ffns['f1'])
                x2_sp(sp, w)
                ffn_sp(sp, w, ffns['f2'])
                x3_sp(sp, w)
                ffn_sp(sp, w, ffns['f3'])
                sp.wait_ge(phase_end, w.up(phase_end, 4))
                for b in range(NB):
                    sp.dma_start(out[b].rearrange("(i p) d -> p i d", p=P), X[:, b, :, :]).then_inc(out_done, 16)
                sp.wait_ge(out_done, 16 * NB)

            @block.gpsimd
            def _(pool):
                pool.sem_inc(ctx_used, 1)
                pool.sem_inc(tr_free, 1)
                pool.sem_inc(kv_free, 3)
                pool.sem_inc(kt_free[0], 1)
                pool.sem_inc(kt_free[1], 1)
                pool.sem_inc(mx_free, 2)
                pool.sem_inc(pv_done, 2)
                pool.sem_inc(spv_done, 2)
                pool.sem_inc(mask_used, 1)
                pool.sem_inc(ks_ps, 2)

            @block.scalar
            def _(act):
                w = Counts(act, "act", steps)
                act.wait_ge(consts_in, w.up(consts_in, 80))
                x0_act(w)
                f0_act(w)
                x1_act(w)
                ffn_act(w, ffns['f1'])
                x2_act(w)
                ffn_act(w, ffns['f2'])
                x3_act(w)
                ffn_act(w, ffns['f3'])

            @block.vector
            def _(dve):
                w = Counts(dve, "dve", steps)
                w.skip(mx_free, 2)
                w.skip(pv_done, 2)
                w.skip(spv_done, 2)
                dve.wait_ge(consts_in, w.up(consts_in, 80))
                nc.vector.tensor_copy(identb, ident).then_inc(consts_ready, 1)
                x0_dve(w)
                f0_dve(w)
                x1_dve(w)
                ffn_dve(w, ffns['f1'])
                x2_dve(w)
                ffn_dve(w, ffns['f2'])
                x3_dve(w)
                ffn_dve(w, ffns['f3'])

            @block.tensor
            def _(pe):
                w = Counts(pe, "pe", steps)
                pe.wait_ge(consts_ready, w.up(consts_ready))
                x0_pe(w)
                f0_pe(w)
                x1_pe(w)
                ffn_pe(w, ffns['f1'])
                x2_pe(w)
                ffn_pe(w, ffns['f2'])
                x3_pe(w)
                ffn_pe(w, ffns['f3'])


def host_consts():
    c = np.zeros((P, NCST), np.float32)
    p = np.arange(P)
    c[:, C_EPS5], c[:, C_EPS6], c[:, C_ONE] = 1e-5, 1e-6, 1.0
    for t in range(11):
        c[:, C_KEY + t] = P * t + p
    tail = np.zeros((14, 7), np.float32)
    tail[:3, 0:3] = 1.0
    tail[3:, 3:6] = 1.0
    c[:, C_TAIL:C_TAIL + 98] = tail.reshape(1, -1)
    inv = 1.0 / 10000.0 ** (np.arange(0, 8, 2, dtype=np.float32) / 8)
    emb = np.outer(np.arange(S, dtype=np.float32), inv)
    emb = np.concatenate([emb, emb], -1)
    cos, sin = np.cos(emb), np.sin(emb)
    sin = np.concatenate([-sin[:, :4], sin[:, 4:]], -1)
    c[:, C_COS:C_COS + 16] = cos.reshape(2, P, 8).transpose(1, 0, 2).reshape(P, 16)
    c[:, C_SIN:C_SIN + 16] = sin.reshape(2, P, 8).transpose(1, 0, 2).reshape(P, 16)
    c[:, C_BLK:C_BLK + 8] = (p[:, None] // 16 == np.arange(8)[None, :])
    c[:, C_BMASK:C_BMASK + P] = (p[:, None] // 16 == p[None, :] // 16)
    c[:, C_IDENT:C_IDENT + P] = np.eye(P)
    q = p[:, None, None] + P * np.arange(2)[None, :, None]
    k = np.arange(S)[None, None, :]
    c[:, C_CAUSAL:C_CAUSAL + 512] = np.where(k > q, -BIG, 0.0).reshape(P, 512)
    return c


def pick_rows(E):
    r = np.full((P, 2), -2)
    if E > P // 3:
        r[:, 0] = np.arange(P) % (E - 1)
        r[:E - 1, 1] = np.arange(E - 1)
        r[E - 1:E + 2, 1] = E - 1
    else:
        r[:3 * E, 0] = np.arange(3 * E) % E
    return r


def rows(w, n=None):
    return np.ascontiguousarray(w.reshape(2, P, -1).transpose(1, 0, 2))


def kernel(**inputs):
    import concourse.bacc as bacc
    from concourse.bass_utils import run_bass_kernel_spmd

    v = {k: np.asarray(a) for k, a in inputs.items()}
    cat = np.concatenate
    arrays = {
        "consts": host_consts(),
        "x": v["x"],
        "ctxT": v["ctx_2048"].transpose(0, 2, 1).reshape(NB, 2, P, CTX).transpose(0, 2, 1, 3),
        "decay": v["L1_xattn_decay"].reshape(1),
        "lens": v["L0_xattn_context_lens"].reshape(1),
        "w_x0": rows(cat([v["L0_xattn_" + n] for n in ("Wq", "Wk", "Wv", "Wk_img", "Wv_img", "Wo")], 1)),
        "v_x0": cat([v["L0_xattn_" + n] for n in ("bq", "gq", "bk", "gk", "bv", "bk_img", "gk_img", "bv_img", "bo")]),
    }
    T = np.transpose

    def chunks(gate, up, down, name):
        n, E, R = FFNS[name][1], FFNS[name][2], FFNS[name][1] * P

        def padded(w):
            return cat([w, np.zeros((R - w.shape[0],) + w.shape[1:], w.dtype)])

        def turned(w):
            return T(padded(w).reshape(n, P, 2, P), (0, 3, 2, 1))

        sizes = {"f1": [64] * 65, "f2": [176] * 9, "f3": [176] * 16 + [352]}[name]
        owner = np.full(R, -1)
        owner[:sum(sizes)] = np.repeat(np.arange(E), sizes)
        pick = np.where(pick_rows(E)[None, :, :, None] == owner.reshape(n, 1, 1, P), 0x3F80, 0).astype(np.uint16)
        pick = np.ascontiguousarray(pick.reshape(n, P, 2 * P)).view(np.float32).reshape(n, P, 1, P)
        g = turned(gate)
        u = turned(up) if up is not None else np.zeros_like(g)
        return cat([g, u, padded(down).reshape(n, P, 2, P), pick], 2)

    gu = v["L1_ffn_gu_w"]
    arrays.update({
        "w_f0": rows(cat([v["L0_ffn_" + n].T for n in ("Wq", "Wk", "Wv", "Wo")], 1)),
        "mlp_f0": T(np.stack([rows(v["L0_ffn_W_in_base"].T), rows(v["L0_ffn_W_up_base"].T)]), (1, 2, 0, 3)),
        "down_f0": T(v["L0_ffn_W_down"].T.reshape(8, P, D), (1, 0, 2)),
        "A_f0": rows(v["L0_ffn_A"]),
        "B_f0": v["L0_ffn_B"],
        "v_f0": cat([v["L0_ffn_ln1_w"], v["L0_ffn_ln2_w"]]),
        "w_x1": rows(cat([v["L1_xattn_W_in"].T, v["L1_xattn_W_out"].T], 1)),
        "v_x1": cat([v["L1_xattn_" + n] for n in ("b_out", "gamma", "beta")]),
        "bin_x1": v["L1_xattn_b_in"].reshape(2, P).T,
        "router_f1": rows(cat([v["L1_ffn_gate_w"], v["L1_ffn_sh_gate1_w"]]).T),
        "chunks_f1": chunks(cat([gu[:, :64].reshape(-1, D), v["L1_ffn_sh_gate_w"]]), cat([gu[:, 64:].reshape(-1, D), v["L1_ffn_sh_up_w"]]),
                            cat([T(v["L1_ffn_dp_w"], (0, 2, 1)).reshape(-1, D), v["L1_ffn_sh_down_w"].T]), "f1"),
        "w_x2": rows(cat([v["L2_xattn_" + n] for n in ("Wq", "Wk", "Wv", "Wo")], 1)),
        "gate_x2": v["L2_xattn_gate"].reshape(-1),
        "mask": v["mask_Bx1xSxS_fk0"].reshape(NB, 2, P, S).transpose(0, 2, 1, 3),
        "router_f2": rows(cat([v["L2_ffn_w_router"], np.zeros((D, 1), np.float32)], 1)),
        "chunks_f2": chunks(cat([T(v["L2_ffn_w1"], (0, 2, 1)).reshape(-1, D), v["L2_ffn_w_shared1"].T]), None,
                            cat([v["L2_ffn_w2"].reshape(-1, D), v["L2_ffn_w_shared2"]]), "f2"),
        "w_x3": rows(cat([v["L3_xattn_" + n].T for n in ("Wq", "Wg", "Wkv", "Wo")], 1)),
        "bg_x3": v["L3_xattn_bg"],
        "router_f3": rows(cat([v["L3_ffn_gate_weight"], np.zeros((1, D), np.float32)]).T),
        "bias_f3": v["L3_ffn_e_score_correction_bias"],
        "chunks_f3": chunks(cat([v["L3_ffn_gate_proj"].reshape(-1, D), v["L3_ffn_shared_gate_w"]]),
                            cat([v["L3_ffn_up_proj"].reshape(-1, D), v["L3_ffn_shared_up_w"]]),
                            cat([T(v["L3_ffn_down_proj"], (0, 2, 1)).reshape(-1, D), v["L3_ffn_shared_down_w"].T]), "f3"),
    })
    arrays = {k: np.ascontiguousarray(a) for k, a in arrays.items()}

    def program(steps):
        nc = bacc.Bacc("TRN2", target_bir_lowering=False, num_devices=1)
        d = {k: nc.dram_tensor(f"in_{k}", a.shape, mybir.dt.from_np(a.dtype), kind="ExternalInput").ap() for k, a in arrays.items()}
        out = nc.dram_tensor("out_x", (NB, S, D), F32, kind="ExternalOutput").ap()
        build(nc, d, out, steps)
        return nc

    steps = {}
    program(steps)
    r = run_bass_kernel_spmd(program(steps), [{f"in_{k}": a for k, a in arrays.items()}], core_ids=[0])
    return r.results[0]["out_x"]
```
